# Optimizing a Trainium2 kernel written in Bass

```python
import numpy as np
import jax
import jax.numpy as jnp

def _softmax(x, axis=-1):
    return jax.nn.softmax(x, axis=axis)

def _gelu(x):
    return jax.nn.gelu(x, approximate=True)

def _silu(x):
    return jax.nn.silu(x)

def _sigmoid(x):
    return jax.nn.sigmoid(x)

def _layernorm(x, axis=-1, eps=1e-05):
    m = jnp.mean(x, axis=axis, keepdims=True)
    v = jnp.var(x, axis=axis, keepdims=True)
    return (x - m) / jnp.sqrt(v + eps)

def _scatter_add(tgt, idx, src, axis=0):
    return tgt.at[idx].add(src)

def _segment_sum(src, seg, n):
    return jax.ops.segment_sum(src, seg, n)
kernel_name = 'mk_adaln_attn_ffn_d1_seqx_r8_3db5d1'

def setup_inputs(seed: int=0):
    np.random.seed(seed)
    _w = jnp.asarray

    def _rec_inputs():
        import jax
        import jax.numpy as jnp
        _rk = jax.random.key(seed)
        x = -7.109e-05 + 0.9999 * jax.random.normal(jax.random.fold_in(_rk, 1), (128, 32, 512), jnp.float32)
        _lenS = 32 - jax.random.randint(jax.random.fold_in(_rk, 7), (128,), 0, max(1, 32 // 4) + 1, jnp.int32)
        _lenS2 = 32 - jax.random.randint(jax.random.fold_in(_rk, 8), (128,), 0, max(1, 32 // 4) + 1, jnp.int32)
        itok_B_0_15 = jax.random.randint(jax.random.fold_in(_rk, 11), (128,), 0, 16, jnp.int32)
        itok_B_78_3631 = jax.random.randint(jax.random.fold_in(_rk, 12), (128,), 78, 454, jnp.int32)
        return (x, itok_B_0_15, itok_B_78_3631)
    x, itok_B_0_15, itok_B_78_3631 = _rec_inputs()

    def _L0_cond_setup():
        import jax, jax.numpy as jnp
        import numpy as np
        B, C, T = (64, 32, 512)
        S, D = (16, 32)
        key = jax.random.key(seed)
        k1, k2, k3 = jax.random.split(key, 3)
        x = jax.random.normal(k1, (B, C, T), dtype=jnp.float32)
        condition = jax.random.randint(k2, (B,), 0, S, dtype=jnp.int64)
        bound = float(np.sqrt(6.0 / C))
        weights = jax.random.uniform(k3, (S, C, D), dtype=jnp.float32, minval=-bound, maxval=bound)
        return {'x': x, 'condition': condition, 'weights': weights}
    _L0_cond_all = _L0_cond_setup()
    _L0_cond_in = {k: v for k, v in _L0_cond_all.items() if k in ('weights',)}
    del _L0_cond_all

    def _L0_attn_setup():
        import jax, jax.numpy as jnp
        import numpy as np
        HIDDEN = 512
        N_HEADS = 32
        KV_HEADS = 8
        HEAD_DIM = 128
        LOW_RANK = 64
        TOP_K_ROPE = 32
        ROPE_THETA = 10000.0
        B, S = (2, 256)
        GROUPS = N_HEADS // KV_HEADS
        _half = HEAD_DIM // 2
        _m = np.ones(_half, dtype=bool)
        _m[:TOP_K_ROPE] = False
        _m = np.concatenate([_m, _m])
        NOPE_MASK = np.tile(_m, KV_HEADS)
        ROPE_IDX = jnp.asarray(np.where(~NOPE_MASK)[0])
        NOPE_IDX = jnp.asarray(np.where(NOPE_MASK)[0])
        R_DIM = int((~NOPE_MASK).sum())
        C_DIM = LOW_RANK * KV_HEADS

        def _rope_tables(seq_len, dtype):
            inv_freq = 1.0 / ROPE_THETA ** (np.arange(0, HEAD_DIM, 2, dtype=np.float32) / HEAD_DIM)
            pos = np.arange(seq_len, dtype=np.float32)
            freqs = np.outer(pos, inv_freq)
            emb = np.concatenate([freqs, freqs], axis=-1)
            return (jnp.asarray(np.cos(emb), dtype), jnp.asarray(np.sin(emb), dtype))

        def _rotate_half(x):
            x1, x2 = (x[..., :HEAD_DIM // 2], x[..., HEAD_DIM // 2:])
            return jnp.concatenate([-x2, x1], axis=-1)
        key = jax.random.key(seed)
        ks = jax.random.split(key, 7)
        s = 0.02
        return {'hidden_states': jax.random.normal(ks[0], (B, S, HIDDEN), jnp.float32), 'Wq': jax.random.normal(ks[1], (N_HEADS * HEAD_DIM, HIDDEN), jnp.float32) * s, 'Wkr': jax.random.normal(ks[2], (R_DIM, HIDDEN), jnp.float32) * s, 'Wdk': jax.random.normal(ks[3], (C_DIM, HIDDEN), jnp.float32) * s, 'Wupk': jax.random.normal(ks[4], (KV_HEADS * HEAD_DIM - R_DIM, C_DIM), jnp.float32) * s, 'Wupv': jax.random.normal(ks[5], (KV_HEADS * HEAD_DIM, C_DIM), jnp.float32) * s, 'Wo': jax.random.normal(ks[6], (HIDDEN, N_HEADS * HEAD_DIM), jnp.float32) * s}
    _L0_attn_all = _L0_attn_setup()
    _L0_attn_in = {k: v for k, v in _L0_attn_all.items() if k in ('Wq', 'Wkr', 'Wdk', 'Wupk', 'Wupv', 'Wo')}
    del _L0_attn_all

    def _L0_cond2_setup():
        import math
        import jax, jax.numpy as jnp
        import numpy as np
        B, H, N, L = (16, 32, 64, 512)
        DT_MIN, DT_MAX = (0.001, 0.1)

        def _get_kernel(log_dt, C, log_A_real, A_imag, length):
            dt = jnp.exp(log_dt)
            Cc = C[..., 0] + 1j * C[..., 1]
            A = -jnp.exp(log_A_real) + 1j * A_imag
            dtA = A * dt[:, None]
            Ct = Cc * (jnp.exp(dtA) - 1.0) / A
            P = dtA[:, :, None] * jnp.arange(length, dtype=jnp.float32)
            K = 2.0 * jnp.einsum('hn,hnl->hl', Ct, jnp.exp(P)).real
            return K
        key = jax.random.key(seed)
        ks = jax.random.split(key, 5)
        u = jax.random.normal(ks[0], (B, H, L), dtype=jnp.float32)
        log_dt = jax.random.uniform(ks[1], (H,), dtype=jnp.float32) * (math.log(DT_MAX) - math.log(DT_MIN)) + math.log(DT_MIN)
        C = jax.random.normal(ks[2], (H, N, 2), dtype=jnp.float32)
        log_A_real = jnp.log(0.5 * jnp.ones((H, N), dtype=jnp.float32))
        A_imag = math.pi * jnp.broadcast_to(jnp.arange(N, dtype=jnp.float32), (H, N))
        D = jax.random.normal(ks[3], (H,), dtype=jnp.float32)
        length = jax.random.randint(ks[4], (B,), 1, L + 1, dtype=jnp.int32)
        return {'u': u, 'log_dt': log_dt, 'C': C, 'log_A_real': log_A_real, 'A_imag': A_imag, 'D': D, 'length': length}
    _L0_cond2_all = _L0_cond2_setup()
    _L0_cond2_in = {k: v for k, v in _L0_cond2_all.items() if k in ('log_dt', 'C', 'log_A_real', 'A_imag', 'D')}
    del _L0_cond2_all

    def _L0_ffn_setup():
        import jax, jax.numpy as jnp
        import numpy as np
        NUM_EXPERTS = 8
        RANK = 32
        ALPHA = 16.0
        TOP_K = 2
        TEMPERATURE = 1.0
        GAMMA = 0.5
        SOFT_TOPK_TEMP = 0.5
        N_GRAM = 2
        EPS = 1e-06
        key = jax.random.key(seed)
        ks = jax.random.split(key, 6)
        d_in, d_out = (512, 512)
        Bsz, T = (4, 256)
        x = jax.random.normal(ks[0], (Bsz, T, d_in), dtype=jnp.float32)
        W = jax.random.normal(ks[1], (d_out, d_in), dtype=jnp.float32) / np.sqrt(d_in)
        b = jax.random.normal(ks[2], (d_out,), dtype=jnp.float32) * 0.01
        A = jax.random.normal(ks[3], (d_in, RANK), dtype=jnp.float32) / np.sqrt(d_in)
        Bmat = jax.random.normal(ks[4], (RANK, d_out), dtype=jnp.float32) * 0.01
        LiMEs = jax.random.normal(ks[5], (NUM_EXPERTS, RANK), dtype=jnp.float32) * 0.1
        return {'x': x, 'W': W, 'b': b, 'A': A, 'Bmat': Bmat, 'LiMEs': LiMEs}
    _L0_ffn_all = _L0_ffn_setup()
    _L0_ffn_in = {k: v for k, v in _L0_ffn_all.items() if k in ('W', 'b', 'A', 'Bmat', 'LiMEs')}
    del _L0_ffn_all
    return {'x': x, 'itok_B_0_15': itok_B_0_15, 'itok_B_78_3631': itok_B_78_3631, 'L0_cond_weights': _L0_cond_in['weights'], 'L0_attn_Wq': _L0_attn_in['Wq'], 'L0_attn_Wkr': _L0_attn_in['Wkr'], 'L0_attn_Wdk': _L0_attn_in['Wdk'], 'L0_attn_Wupk': _L0_attn_in['Wupk'], 'L0_attn_Wupv': _L0_attn_in['Wupv'], 'L0_attn_Wo': _L0_attn_in['Wo'], 'L0_cond2_log_dt': _L0_cond2_in['log_dt'], 'L0_cond2_C': _L0_cond2_in['C'], 'L0_cond2_log_A_real': _L0_cond2_in['log_A_real'], 'L0_cond2_A_imag': _L0_cond2_in['A_imag'], 'L0_cond2_D': _L0_cond2_in['D'], 'L0_ffn_W': _L0_ffn_in['W'], 'L0_ffn_b': _L0_ffn_in['b'], 'L0_ffn_A': _L0_ffn_in['A'], 'L0_ffn_Bmat': _L0_ffn_in['Bmat'], 'L0_ffn_LiMEs': _L0_ffn_in['LiMEs']}

def reference(x, itok_B_0_15, itok_B_78_3631, L0_cond_weights, L0_attn_Wq, L0_attn_Wkr, L0_attn_Wdk, L0_attn_Wupk, L0_attn_Wupv, L0_attn_Wo, L0_cond2_log_dt, L0_cond2_C, L0_cond2_log_A_real, L0_cond2_A_imag, L0_cond2_D, L0_ffn_W, L0_ffn_b, L0_ffn_A, L0_ffn_Bmat, L0_ffn_LiMEs):
    import jax
    import jax.numpy as jnp

    def _L0_cond_ref(x, condition, weights):
        import jax, jax.numpy as jnp
        import numpy as np
        B, C, T = (64, 32, 512)
        S, D = (16, 32)
        W = weights[condition]
        return jnp.einsum('bct,bcd->bdt', x, W)

    def _L0_attn_ref(hidden_states, Wq, Wkr, Wdk, Wupk, Wupv, Wo):
        import jax, jax.numpy as jnp
        import numpy as np
        HIDDEN = 512
        N_HEADS = 32
        KV_HEADS = 8
        HEAD_DIM = 128
        LOW_RANK = 64
        TOP_K_ROPE = 32
        ROPE_THETA = 10000.0
        B, S = (2, 256)
        GROUPS = N_HEADS // KV_HEADS
        _half = HEAD_DIM // 2
        _m = np.ones(_half, dtype=bool)
        _m[:TOP_K_ROPE] = False
        _m = np.concatenate([_m, _m])
        NOPE_MASK = np.tile(_m, KV_HEADS)
        ROPE_IDX = jnp.asarray(np.where(~NOPE_MASK)[0])
        NOPE_IDX = jnp.asarray(np.where(NOPE_MASK)[0])
        R_DIM = int((~NOPE_MASK).sum())
        C_DIM = LOW_RANK * KV_HEADS

        def _rope_tables(seq_len, dtype):
            inv_freq = 1.0 / ROPE_THETA ** (np.arange(0, HEAD_DIM, 2, dtype=np.float32) / HEAD_DIM)
            pos = np.arange(seq_len, dtype=np.float32)
            freqs = np.outer(pos, inv_freq)
            emb = np.concatenate([freqs, freqs], axis=-1)
            return (jnp.asarray(np.cos(emb), dtype), jnp.asarray(np.sin(emb), dtype))

        def _rotate_half(x):
            x1, x2 = (x[..., :HEAD_DIM // 2], x[..., HEAD_DIM // 2:])
            return jnp.concatenate([-x2, x1], axis=-1)
        bsz, q_len, _ = hidden_states.shape
        dt = hidden_states.dtype
        q = (hidden_states @ Wq.T).reshape(bsz, q_len, N_HEADS, HEAD_DIM).transpose(0, 2, 1, 3)
        k_r0 = hidden_states @ Wkr.T
        key_flat = jnp.zeros((bsz, q_len, KV_HEADS * HEAD_DIM), dt).at[..., ROPE_IDX].set(k_r0)
        k = key_flat.reshape(bsz, q_len, KV_HEADS, HEAD_DIM).transpose(0, 2, 1, 3)
        cos, sin = _rope_tables(q_len, dt)
        cos, sin = (cos[None, None], sin[None, None])
        q = q * cos + _rotate_half(q) * sin
        k = k * cos + _rotate_half(k) * sin
        k_r = k.transpose(0, 2, 1, 3).reshape(bsz, q_len, KV_HEADS * HEAD_DIM)[..., ROPE_IDX]
        c_kv = hidden_states @ Wdk.T
        k_c = c_kv @ Wupk.T
        v = (c_kv @ Wupv.T).reshape(bsz, q_len, KV_HEADS, HEAD_DIM).transpose(0, 2, 1, 3)
        key_full = jnp.zeros((bsz, q_len, KV_HEADS * HEAD_DIM), dt).at[..., NOPE_IDX].set(k_c).at[..., ROPE_IDX].set(k_r)
        k = key_full.reshape(bsz, q_len, KV_HEADS, HEAD_DIM).transpose(0, 2, 1, 3)
        k = jnp.repeat(k, GROUPS, axis=1)
        v = jnp.repeat(v, GROUPS, axis=1)
        scale = 1.0 / jnp.sqrt(jnp.asarray(HEAD_DIM, dt))
        scores = jnp.einsum('bhqd,bhkd->bhqk', q, k) * scale
        causal = jnp.tril(jnp.ones((q_len, q_len), bool))
        scores = jnp.where(causal[None, None], scores, jnp.asarray(-1000000000.0, dt))
        attn = jax.nn.softmax(scores, axis=-1)
        out = jnp.einsum('bhqk,bhkd->bhqd', attn, v)
        out = out.transpose(0, 2, 1, 3).reshape(bsz, q_len, N_HEADS * HEAD_DIM)
        return out @ Wo.T

    def _L0_cond2_ref(u, log_dt, C, log_A_real, A_imag, D, length):
        import math
        import jax, jax.numpy as jnp
        import numpy as np
        B, H, N, L = (16, 32, 64, 512)
        DT_MIN, DT_MAX = (0.001, 0.1)

        def _get_kernel(log_dt, C, log_A_real, A_imag, length):
            dt = jnp.exp(log_dt)
            Cc = C[..., 0] + 1j * C[..., 1]
            A = -jnp.exp(log_A_real) + 1j * A_imag
            dtA = A * dt[:, None]
            Ct = Cc * (jnp.exp(dtA) - 1.0) / A
            P = dtA[:, :, None] * jnp.arange(length, dtype=jnp.float32)
            K = 2.0 * jnp.einsum('hn,hnl->hl', Ct, jnp.exp(P)).real
            return K
        Bq, Hq, Lq = u.shape
        K = _get_kernel(log_dt, C, log_A_real, A_imag, Lq)
        n = 2 * Lq
        kf = jnp.fft.rfft(K, n=n)
        uf = jnp.fft.rfft(u, n=n)
        y = jnp.fft.irfft(uf * kf[None], n=n)[..., :Lq]
        y = y + u * D[:, None]
        mask = (jnp.arange(Lq)[None, :] < length[:, None]).astype(u.dtype)
        return y * mask[:, None, :]

    def _L0_ffn_ref(x, W, b, A, Bmat, LiMEs):
        import jax, jax.numpy as jnp
        import numpy as np
        NUM_EXPERTS = 8
        RANK = 32
        ALPHA = 16.0
        TOP_K = 2
        TEMPERATURE = 1.0
        GAMMA = 0.5
        SOFT_TOPK_TEMP = 0.5
        N_GRAM = 2
        EPS = 1e-06
        Bsz, T, d_in = x.shape
        E = LiMEs.shape[0]
        scaling = ALPHA / RANK
        H = jnp.einsum('btd,od->bto', x, W) + b
        z = jnp.einsum('btd,dr->btr', x, A)
        anchors = jnp.arange(N_GRAM - 1, T, N_GRAM)
        H_slice = H[:, anchors, :E]
        delta_slice = jnp.einsum('bar,er->bae', z[:, anchors], LiMEs)
        H_scale = jnp.maximum(jnp.max(jnp.abs(H_slice)), EPS)
        d_scale = jnp.maximum(jnp.max(jnp.abs(delta_slice)), EPS)
        logits = ((1.0 - GAMMA) * (H_slice / H_scale) + GAMMA * (delta_slice / d_scale)) / TEMPERATURE
        probs = jax.nn.softmax(logits, axis=-1)
        topk_vals, _ = jax.lax.top_k(probs, TOP_K)
        thresh = topk_vals[..., -1:]
        mask = jax.nn.sigmoid((probs - thresh) / SOFT_TOPK_TEMP)
        weights = probs * mask
        weights = weights / (jnp.sum(weights, axis=-1, keepdims=True) + 1e-09)
        weights_full = jnp.repeat(weights, N_GRAM, axis=1)
        p_mix = jnp.einsum('bte,er->btr', weights_full, LiMEs)
        delta = jnp.einsum('btr,ro->bto', z * p_mix, Bmat) * scaling
        return H + delta
    x = x + _L0_attn_ref(_L0_cond_ref(x, itok_B_0_15, L0_cond_weights), L0_attn_Wq, L0_attn_Wkr, L0_attn_Wdk, L0_attn_Wupk, L0_attn_Wupv, L0_attn_Wo)
    x = x + _L0_ffn_ref(_L0_cond2_ref(x, L0_cond2_log_dt, L0_cond2_C, L0_cond2_log_A_real, L0_cond2_A_imag, L0_cond2_D, itok_B_78_3631), L0_ffn_W, L0_ffn_b, L0_ffn_A, L0_ffn_Bmat, L0_ffn_LiMEs)
    return x

_drawn_inputs = setup_inputs


def setup_inputs(seed=0):
    import zlib

    import numpy as np

    out = dict(_drawn_inputs(seed))
    spreads = {'L0_cond2_log_A_real': (-0.6931471824645996, 0.2)}
    factors = {'L0_attn_Wupk': 3.451,
     'L0_ffn_b': 8.0,
     'L0_ffn_A': 8.0,
     'L0_ffn_Bmat': 8.0,
     'L0_ffn_LiMEs': 8.0}
    for name, (base, spread) in spreads.items():
        noise = np.random.default_rng([zlib.crc32(name.encode()), seed]).standard_normal(out[name].shape)
        drawn = base * np.exp(spread * noise) if base else spread * noise
        out[name] = jnp.asarray(drawn.astype(out[name].dtype))
    for name, factor in factors.items():
        out[name] = (out[name] * factor).astype(out[name].dtype)
    return out
```

```python
from contextlib import ExitStack
import math

import numpy as np

import concourse.bass as bass
from concourse import mybir

F32 = mybir.dt.float32
F32R = mybir.dt.float32r
I32 = mybir.dt.int32
ALU = mybir.AluOpType
ACT = mybir.ActivationFunctionType
AX = mybir.AxisListType

P = 128
BATCH, SEQ, DM = 128, 32, 512
TOK = BATCH * SEQ
KB = DM // P
KVH, GRP, HD = 8, 4, 128
CH = 512
BCH = CH // SEQ
QTOK = 1024
NQ = TOK // QTOK
UPQ = KVH * (QTOK // CH)
TPC = CH // P
NST, NSTATE = 16, 64
NE, RANK = 8, 32
NC_, NF_ = 16, 32
NSEC = 5
SECW = [NC_, NC_, NF_, 1, 1]
SECO = [0, NC_, 2 * NC_, 2 * NC_ + NF_, 2 * NC_ + NF_ + 1]
NANG = 2 * NC_ + NF_ + 2
KPAD = P - 1 + DM + 1
SCALE = 1.0 / math.sqrt(HD)
TWO_PI = 2.0 * math.pi
PI_HEAD = 6.28125
PI_MID = float(np.float32(np.round((TWO_PI - PI_HEAD) * 2 ** 22) / 2 ** 22))
PI_TAIL = TWO_PI - PI_HEAD - PI_MID
LN2_HEAD = float(np.float32(np.round(math.log(2.0) * 2 ** 12) / 2 ** 12))
LN2_TAIL = math.log(2.0) - LN2_HEAD
MAGIC = float(1.5 * 2 ** 23)

C_ROPE = 0
C_MASK = C_ROPE + 4 * SEQ
C_ID = C_MASK + SEQ
C_PIDX = C_ID + P
C_LAG = C_PIDX + KB
C_PHASE = C_LAG + NANG
C_W = C_PHASE + 2 * NSEC


def constants():
    c = np.zeros((P, C_W), np.float32)
    inv = 1.0 / 10000.0 ** (np.arange(0, HD, 2, dtype=np.float32) / HD)
    freqs = np.outer(np.arange(SEQ, dtype=np.float32), inv)
    emb = np.concatenate([freqs, freqs], -1)
    cos, sin = np.cos(emb).T, np.sin(emb).T
    sin = np.concatenate([-sin[:64], sin[64:]], 0)
    roped = (np.arange(HD) % 64 < 32)[:, None]
    c[:, 0:SEQ], c[:, SEQ:2 * SEQ] = cos, sin
    c[:, 2 * SEQ:3 * SEQ], c[:, 3 * SEQ:4 * SEQ] = np.where(roped, cos, 1.0), np.where(roped, sin, 0.0)
    pos = np.arange(P) % SEQ
    c[:, C_MASK:C_MASK + SEQ] = np.where(np.arange(SEQ)[None] <= pos[:, None], 0.0, -1e9)
    c[:, C_ID:C_ID + P] = np.eye(P)
    c[:, C_PIDX:C_PIDX + KB] = np.arange(P)[:, None] + P * np.arange(KB)[None]
    coarse, fine = NF_ * np.arange(NC_), np.arange(NF_)
    c[:, C_LAG:C_LAG + NANG] = np.concatenate([coarse, coarse, fine, [0.5, 0.5]])[None]
    im = np.arange(P)[:, None] >= NSTATE
    quarter = np.where(im, 1, 0)
    turns = np.concatenate([quarter + 1, quarter, 1 - quarter, 0 * quarter, 0 * quarter + 1], 1) * 0.25
    c[:, C_PHASE:C_PHASE + NSEC] = turns
    c[:, C_PHASE + NSEC:C_PHASE + 2 * NSEC] = turns * TWO_PI
    return c


def weights_and_ssm(nc, io, scratch):
    with ExitStack() as ctx:
        def sb(name, shape, dt=F32):
            return ctx.enter_context(nc.sbuf_tensor(name, shape, dt))

        def sem(name):
            return ctx.enter_context(nc.semaphore(name))

        cst = sb("a_cst", [P, C_W])
        wdk = sb("a_wdk", [P, KB, DM])
        wupk = sb("a_wupk", [P, KB, DM])
        wupv = sb("a_wupv", [P, KB, KVH * HD])
        wkr = sb("a_wkr", [P, KB, DM])
        wkv = sb("a_wkv", [P, 2, KVH, 2 * HD])
        condi = sb("a_condi", [NST, BATCH], I32)
        condf = sb("a_condf", [NST, BATCH])
        onehot = sb("a_onehot", [NST, BATCH])
        wcond = sb("a_wcond", [NST, SEQ * SEQ])
        wg = sb("a_wg", [P, SEQ * SEQ])
        par = sb("a_par", [P, 5, SEQ])
        dskip = sb("a_dskip", [1, SEQ])
        eab = sb("a_eab", [P, 2, SEQ])
        ek = sb("a_ek", [P, 2, SEQ])
        er_ = sb("a_er", [P, 2, SEQ])
        ei_ = sb("a_ei", [P, 2, SEQ], I32)
        xy = sb("a_xy", [P, 2, SEQ])
        tnh = sb("a_tnh", [P, SEQ])
        mag = sb("a_mag", [P, SEQ, NC_ + NF_])
        ang = sb("a_ang", [P, SEQ, NANG])
        turn = sb("a_turn", [P, SEQ, NANG])
        sn = sb("a_sn", [P, SEQ, NANG])
        tmp = sb("a_tmp", [P, 16, SEQ])
        lft = sb("a_lft", [P, SEQ, NC_])
        lf2 = sb("a_lf2", [P, SEQ, NC_])
        rgt = sb("a_rgt", [P, SEQ, NF_])
        kern = sb("a_kern", [NC_, SEQ, NF_])
        zrow = sb("a_zrow", [SEQ, P])
        pe = [ctx.enter_context(nc.psum_tensor(f"a_pe{i}", [P, 512], F32)) for i in range(3)]
        pg = ctx.enter_context(nc.psum_tensor("a_pg", [P, 2, 512], F32))
        pk = ctx.enter_context(nc.psum_tensor("a_pk", [P, 2, 512], F32))

        cst_in, ssm_in, w_in, cond_in = sem("a_cst_in"), sem("a_ssm_in"), sem("a_w_in"), sem("a_cond_in")
        hot = sem("a_hot")
        gathered = sem("a_gathered")
        wg_ready = sem("a_wg_ready")
        folded = sem("a_folded")
        unfolded = sem("a_unfolded")
        roped = sem("a_roped")
        xy_ready, mag_ready = sem("a_xy_ready"), sem("a_mag_ready")
        mags, ang_ready, sines = sem("a_mags"), sem("a_ang_ready"), sem("a_sines")
        factors = sem("a_factors")
        kernel_mm = sem("a_kernel_mm")
        kern_ready = sem("a_kern_ready")
        zeroed = sem("a_zeroed")
        chain = sem("a_chain")
        stored = sem("a_stored")
        wkv_out = [sem("a_wkv_out0"), sem("a_wkv_out1")]
        block = ctx.enter_context(nc.Block())

        @block.sync
        def _(sp):
            sp.dma_start(cst[:], io["consts"]).then_inc(cst_in, 16)
            for n, name in ((0, "log_A_real"), (2, "A_imag"), (3, "C_re"), (4, "C_im")):
                for half in range(2):
                    sp.dma_start(par[half * NSTATE:(half + 1) * NSTATE, n, :], io[name]).then_inc(ssm_in, 16)
            sp.dma_start(par[:, 1, :], io["log_dt"].partition_broadcast(P)).then_inc(ssm_in, 16)
            sp.dma_start(dskip[:], io["D"].rearrange("(a h) -> a h", a=1)).then_inc(ssm_in, 16)
            sp.dma_start(condi[:], io["cond"].partition_broadcast(NST)).then_inc(cond_in, 16)
            sp.dma_start(wcond[:], io["w_cond"]).then_inc(cond_in, 16)
            sp.dma_start(wdk[:], io["wdk"].rearrange("(c p) n -> p c n", p=P)).then_inc(w_in, 16)
            sp.dma_start(wupk[:], io["wupkT"].rearrange("(c p) n -> p c n", p=P)).then_inc(w_in, 16)
            sp.dma_start(wupv[:], io["wupvT"].rearrange("(c p) n -> p c n", p=P)).then_inc(w_in, 16)
            sp.dma_start(wkr[:], io["wkrT"].rearrange("(c p) n -> p c n", p=P)).then_inc(w_in, 16)
            sp.wait_ge(wg_ready, 2)
            sp.dma_start(scratch["wg"], wg[:]).then_inc(stored, 16)
            for m in range(KB):
                sp.wait_ge(unfolded, 3 * (m + 1))
                sp.wait_ge(roped, m + 1)
                sp.dma_start(scratch["wkv"][m], wkv[:, m % 2, :, :]).then_inc(wkv_out[m % 2], 16)
            sp.wait_ge(zeroed, 1)
            sp.dma_start(scratch["kpad"][:, 0:P - 1], zrow[:, 0:P - 1]).then_inc(stored, 16)
            sp.wait_ge(kern_ready, 3)
            sp.dma_start(scratch["kpad"][:, P - 1:P - 1 + DM].rearrange("h (a c) -> a h c", c=NF_),
                         kern[:]).then_inc(stored, 16)
            sp.wait_ge(stored, 48)
            sp.wait_ge(wkv_out[0], 32)
            sp.wait_ge(wkv_out[1], 32)

        @block.gpsimd
        def _(pool):
            pool.memset(zrow[:], 0.0).then_inc(zeroed, 1)

        @block.scalar
        def _(act):
            act.wait_ge(xy_ready, 1)
            act.activation(tnh[:], xy[:, 0, :], ACT.Tanh, scale=0.5).then_inc(mags, 1)
            act.wait_ge(mag_ready, 1)
            act.activation(mag[:], mag[:], ACT.Exp).then_inc(mags, 1)
            for j in range(2):
                act.wait_ge(gathered, j + 1)
                act.activation(wg[:, j * 512:(j + 1) * 512], pg[:, j, :], ACT.Copy).then_inc(wg_ready, 1)
            for m in range(KB):
                if m >= 2:
                    act.wait_ge(wkv_out[m % 2], 16)
                act.wait_ge(folded, 3 * m + 1)
                act.activation(wkv[:, m % 2, :, 0:HD].rearrange("p h (a r) -> p h a r", a=2)[:, :, :, 32:64],
                               pe[0][:].rearrange("p (h a r) -> p h a r", h=KVH, a=2), ACT.Copy).then_inc(unfolded, 1)
                for j in range(2):
                    act.wait_ge(folded, 3 * m + 2 + j)
                    act.activation(wkv[:, m % 2, 4 * j:4 * j + 4, HD:2 * HD],
                                   pe[1 + j][:].rearrange("p (h d) -> p h d", h=4), ACT.Copy).then_inc(unfolded, 1)
            act.wait_ge(ang_ready, 1)
            act.activation(sn[:], ang[:], ACT.Sin).then_inc(sines, 1)

        @block.tensor
        def _(t):
            t.wait_ge(hot, 1)
            for j in range(2):
                t.matmul(pg[:, j, :], onehot[:], wcond[:, j * 512:(j + 1) * 512],
                         start=True, stop=True).then_inc(gathered, 1)
            t.wait_ge(w_in, 64)
            for m in range(KB):
                for j in range(3):
                    if m:
                        t.wait_ge(unfolded, 3 * (m - 1) + j + 1)
                    for c in range(KB):
                        w = wupk[:, c, :] if j == 0 else wupv[:, c, (j - 1) * 512:j * 512]
                        mm = t.matmul(pe[j][:], wdk[:, c, m * P:(m + 1) * P], w, start=c == 0, stop=c == KB - 1)
                    mm.then_inc(folded, 1)
            t.wait_ge(factors, 2)
            for h in range(SEQ):
                mm = t.matmul(pk[0:NC_, h // 16, (h % 16) * NF_:(h % 16 + 1) * NF_], lft[:, h, :], rgt[:, h, :],
                              start=True, stop=True)
            mm.then_inc(kernel_mm, 1)

        @block.vector
        def _(v):
            done = [0]

            def then(ins):
                done[0] += 1
                ins.then_inc(chain, 1)
                v.wait_ge(chain, done[0])

            def mul(out, a, b):
                then(v.tensor_tensor(out, a, b, ALU.mult))

            def add(out, a, b, op=ALU.add):
                then(v.tensor_tensor(out, a, b, op))

            v.wait_ge(cond_in, 32)
            v.wait_ge(cst_in, 16)
            then(v.tensor_copy(condf[:], condi[:]))
            v.tensor_scalar(onehot[:], condf[:], cst[0:NST, C_PIDX:C_PIDX + 1], None, ALU.is_equal).then_inc(hot, 1)
            ea, dt = eab[:, 0, :], eab[:, 1, :]
            x, y = xy[:, 0, :], xy[:, 1, :]
            v.wait_ge(ssm_in, 160)
            logs = par[:, 0:2, :]
            then(v.tensor_scalar(ek[:], logs, 1.0 / math.log(2.0), MAGIC, ALU.mult, ALU.add))
            then(v.tensor_scalar(ek[:], ek[:], -MAGIC, -126.0, ALU.add, ALU.max))
            then(v.tensor_scalar(ek[:], ek[:], 127.0, None, ALU.min))
            then(v.scalar_tensor_tensor(er_[:], ek[:], -LN2_HEAD, logs, ALU.mult, ALU.add))
            then(v.scalar_tensor_tensor(er_[:], ek[:], -LN2_TAIL, er_[:], ALU.mult, ALU.add))
            then(v.tensor_scalar(ek[:], ek[:], 127.0, None, ALU.add))
            then(v.tensor_copy(ei_[:], ek[:]))
            then(v.tensor_scalar(ei_[:], ei_[:], 23, None, ALU.logical_shift_left))
            then(v.tensor_scalar(eab[:], er_[:], 1.0 / math.factorial(8), None, ALU.mult))
            for order in range(7, 0, -1):
                then(v.scalar_tensor_tensor(eab[:], eab[:], 1.0 / math.factorial(order), er_[:], ALU.add, ALU.mult))
            then(v.scalar_tensor_tensor(eab[:], eab[:], 1.0, ei_[:].bitcast(F32), ALU.add, ALU.mult))
            mul(x, ea, dt)
            then(v.tensor_scalar(x, x, -1.0, None, ALU.mult))
            v.tensor_tensor(y, par[:, 2, :], dt, ALU.mult).then_inc(xy_ready, 1)
            v.wait_ge(xy_ready, 1)
            v.tensor_tensor(mag[:], x.unsqueeze(2).to_broadcast([P, SEQ, NC_ + NF_]),
                            cst[:, C_LAG + NC_:C_LAG + NC_ + NC_ + NF_].unsqueeze(1).to_broadcast([P, SEQ, NC_ + NF_]),
                            ALU.mult).then_inc(mag_ready, 1)
            mul(ang[:], y.unsqueeze(2).to_broadcast([P, SEQ, NANG]),
                cst[:, C_LAG:C_LAG + NANG].unsqueeze(1).to_broadcast([P, SEQ, NANG]))
            for s in range(NSEC):
                a, b = SECO[s], SECO[s] + SECW[s]
                then(v.tensor_scalar(turn[:, :, a:b], ang[:, :, a:b], 1.0 / TWO_PI,
                                     cst[:, C_PHASE + s:C_PHASE + s + 1], ALU.mult, ALU.add))
            then(v.tensor_scalar(turn[:], turn[:], MAGIC, None, ALU.add))
            then(v.tensor_scalar(turn[:], turn[:], -MAGIC, None, ALU.add))
            for part in (PI_HEAD, PI_MID, PI_TAIL):
                then(v.scalar_tensor_tensor(ang[:], turn[:], -part, ang[:], ALU.mult, ALU.add))
            for s in range(NSEC):
                a, b = SECO[s], SECO[s] + SECW[s]
                then(v.tensor_scalar(ang[:, :, a:b], ang[:, :, a:b],
                                     cst[:, C_PHASE + NSEC + s:C_PHASE + NSEC + s + 1], None, ALU.add))
            then(v.tensor_scalar(turn[:], ang[:], 1.0 / TWO_PI, MAGIC, ALU.mult, ALU.add))
            then(v.tensor_scalar(turn[:], turn[:], -MAGIC, None, ALU.add))
            then(v.scalar_tensor_tensor(ang[:], turn[:], -TWO_PI, ang[:], ALU.mult, ALU.add))
            then(v.tensor_scalar(ang[:], ang[:], 3.1415925, None, ALU.min))
            v.tensor_scalar(ang[:], ang[:], -3.1415925, None, ALU.max).then_inc(ang_ready, 1)
            v.wait_ge(w_in, 64)
            for m in range(KB):
                if m >= 2:
                    v.wait_ge(wkv_out[m % 2], 16)
                v.tensor_copy(wkv[:, m % 2, :, 0:HD].rearrange("p h (a r) -> p h a r", a=2)[:, :, :, 0:32],
                              wkr[:, m, :].rearrange("p (h a r) -> p h a r", h=KVH, a=2)).then_inc(roped, 1)
            em, e0, s2, er, ei, ar2, inv, mr, mi, cr, ci, t0, t1 = [tmp[:, i, :] for i in range(13)]
            v.wait_ge(mags, 2)
            then(v.tensor_scalar(e0, tnh[:], -1.0, 1.0, ALU.mult, ALU.add))
            then(v.reciprocal(em, e0))
            then(v.scalar_tensor_tensor(em, em, 2.0, tnh[:], ALU.mult, ALU.mult))
            v.wait_ge(sines, 1)
            sh, chf = sn[:, :, SECO[3]], sn[:, :, SECO[4]]
            mul(s2, sh, sh)
            then(v.tensor_scalar(s2, s2, 2.0, None, ALU.mult))
            then(v.tensor_scalar(t0, s2, -1.0, 1.0, ALU.mult, ALU.add))
            mul(er, em, t0)
            add(er, er, s2, ALU.subtract)
            mul(t1, sh, chf)
            then(v.tensor_scalar(e0, em, 1.0, 2.0, ALU.add, ALU.mult))
            mul(ei, e0, t1)
            ai = par[:, 2, :]
            mul(ar2, ea, ea)
            mul(t0, ai, ai)
            add(ar2, ar2, t0)
            then(v.reciprocal(inv, ar2))
            mul(t0, er, ea)
            mul(t1, ei, ai)
            add(mr, t1, t0, ALU.subtract)
            mul(mr, mr, inv)
            mul(t0, ei, ea)
            mul(t1, er, ai)
            add(mi, t0, t1)
            then(v.scalar_tensor_tensor(mi, mi, -1.0, inv, ALU.mult, ALU.mult))
            mul(t0, par[:, 3, :], mr)
            mul(t1, par[:, 4, :], mi)
            add(cr, t0, t1, ALU.subtract)
            then(v.tensor_scalar(cr, cr, 2.0, None, ALU.mult))
            mul(t0, par[:, 3, :], mi)
            mul(t1, par[:, 4, :], mr)
            add(ci, t0, t1)
            then(v.tensor_scalar(ci, ci, 2.0, None, ALU.mult))
            mul(lft[:], sn[:, :, 0:NC_], cr.unsqueeze(2).to_broadcast([P, SEQ, NC_]))
            mul(lf2[:], sn[:, :, NC_:2 * NC_], ci.unsqueeze(2).to_broadcast([P, SEQ, NC_]))
            add(lft[:], lft[:], lf2[:], ALU.subtract)
            v.tensor_tensor(lft[:], lft[:], mag[:, :, 0:NC_], ALU.mult).then_inc(factors, 1)
            v.tensor_tensor(rgt[:], sn[:, :, 2 * NC_:2 * NC_ + NF_], mag[:, :, NC_:NC_ + NF_],
                            ALU.mult).then_inc(factors, 1)
            v.wait_ge(kernel_mm, 1)
            for j in range(2):
                v.tensor_copy(kern[:, 16 * j:16 * j + 16, :], pk[0:NC_, j, :].rearrange("p (h c) -> p h c", h=16))\
                 .then_inc(kern_ready, 1)
            v.wait_ge(kern_ready, 2)
            v.tensor_tensor(kern[0:1, :, 0], kern[0:1, :, 0], dskip[:], ALU.add).then_inc(kern_ready, 1)


def attention(nc, io, scratch):
    with ExitStack() as ctx:
        def sb(name, shape, dt=F32):
            return ctx.enter_context(nc.sbuf_tensor(name, shape, dt))

        def sem(name):
            return ctx.enter_context(nc.semaphore(name))

        cst = sb("b_cst", [P, C_W])
        h_hi, h_lo = sb("h_hi", [P, KB, QTOK], F32R), sb("h_lo", [P, KB, QTOK], F32R)
        acc = sb("b_acc", [P, KB, QTOK])
        wq_hi, wq_lo = (sb(f"wq_{x}", [P, 2, KB, GRP * HD], F32R) for x in ("hi", "lo"))
        wkv_hi, wkv_lo = (sb(f"wkv_{x}", [P, 2, KB, 2 * HD], F32R) for x in ("hi", "lo"))
        wo_hi, wo_lo = (sb(f"wo_{x}", [P, 2, GRP, DM], F32R) for x in ("hi", "lo"))
        stage = sb("b_stage", [P, 2, 2, 512])
        work = sb("b_work", [P, GRP * CH + 5 * CH])
        qT = work[:, 0:GRP * CH].rearrange("p (g t) -> p g t", g=GRP)
        swapped = work[:, GRP * CH:GRP * CH + 5 * CH].rearrange("p (i t) -> p i t", i=5)
        xt = work[:, 0:8 * DM].rearrange("p (t f) -> p t f", t=8)
        kT = sb("b_kT", [P, CH])
        v_sb = sb("b_v", [P, TPC, HD])
        sc = sb("b_sc", [P, GRP * TPC, SEQ])
        pr = sb("b_pr", [P, GRP * TPC, SEQ])
        red = sb("b_red", [P, 2, GRP * TPC])
        rcp = sb("b_rcp", [P, GRP * TPC])
        diag = sb("b_diag", [P, TPC, 4, GRP * SEQ])
        o_hi, o_lo = sb("o_hi", [P, GRP, CH], F32R), sb("o_lo", [P, GRP, CH], F32R)
        bdc = sb("b_bdc", [P, QTOK // P, P])

        proj = [ctx.enter_context(nc.psum_tensor(f"proj{i}", [P, 512], F32)) for i in range(3)]
        ps = ctx.enter_context(nc.psum_tensor("scores", [P, 512], F32))
        pv = [ctx.enter_context(nc.psum_tensor(f"pv{i}", [P, 512], F32)) for i in range(2)]
        po = [ctx.enter_context(nc.psum_tensor(f"po{i}", [P, 512], F32)) for i in range(2)]

        cst_in = sem("b_cst_in")
        x_in, bdc_in = sem("x_in"), sem("bdc_in")
        acc_in, acc_out = sem("acc_in"), sem("acc_out")
        stage_in = [sem("stage_in0"), sem("stage_in1")]
        w_hi_done, w_lo_done = sem("w_hi_done"), sem("w_lo_done")
        cleared = sem("b_cleared")
        h_mm, h_hi_done, h_lo_done = sem("h_mm"), sem("h_hi_done"), sem("h_lo_done")
        proj_done = sem("proj_done")
        swap_done = sem("swap_done")
        cos_done = sem("cos_done")
        sin_done = sem("sin_done")
        rope_done = sem("rope_done")
        v_done = sem("v_done")
        scores_done = sem("scores_done")
        turned = sem("turned")
        smax = sem("smax")
        exp_done = sem("exp_done")
        diag_done = sem("diag_done")
        pv_done, o_hi_done, o_lo_done = sem("pv_done"), sem("o_hi_done"), sem("o_lo_done")
        wo_done, acc_done = sem("wo_done"), sem("acc_done")
        block = ctx.enter_context(nc.Block())

        SLOT = {i: i % 3 for i in range(6)}
        ropes = {"q": (cst[:, C_ROPE:C_ROPE + SEQ], cst[:, C_ROPE + SEQ:C_ROPE + 2 * SEQ]),
                 "k": (cst[:, C_ROPE + 2 * SEQ:C_ROPE + 3 * SEQ], cst[:, C_ROPE + 3 * SEQ:C_ROPE + 4 * SEQ])}

        def target(i):
            return kT[:] if i == 3 else qT[:, min(i, 3), :]

        def by_position(ap):
            return ap.rearrange("p (b s) -> p b s", s=SEQ)

        def table(i, which):
            return ropes["k" if i == 3 else "q"][which].unsqueeze(1).to_broadcast([P, BCH, SEQ])

        PIECES = [(wq_hi, wq_lo, 0), (wq_hi, wq_lo, 2), (wkv_hi, wkv_lo, 0), (wo_hi, wo_lo, 0), (wo_hi, wo_lo, 2)]

        def half(tensor, w, k0, j):
            if tensor in (wkv_hi, wkv_lo):
                return tensor[:, w, 2 * j:2 * j + 2, :].rearrange("p k n -> p (k n)")
            return tensor[:, w, k0 + j, :]

        def quarter(eng, q, prologue, step, finish):
            prologue(q)
            step(0, q * UPQ, (4 * q, 1, (0, 1)))
            with eng.Fori(0, 3) as j:
                n0 = q * UPQ + j * 4
                pair = q * 4 + j
                step(1, n0 + 1, (pair, 1, (2, 3, 4)))
                step(2, n0 + 2, (pair + 1, 0, (0, 1)))
                step(3, n0 + 3, (pair + 1, 0, (2, 3, 4)))
                step(4, n0 + 4, (pair + 1, 1, (0, 1)))
            n0 = q * UPQ
            step(13, n0 + 13, (q * 4 + 3, 1, (2, 3, 4)))
            step(14, n0 + 14, None)
            step(15, n0 + 15, None)
            finish(n0 + 16)

        @block.sync
        def _(sp):
            sp.dma_start(cst[:], io["consts"]).then_inc(cst_in, 16)
            sp.wait_ge(w_lo_done, 3)

            def load_tokens(q):
                for half_ in range(2):
                    sp.dma_start(xt[:, 4 * half_:4 * half_ + 4, :],
                                 io["x_tok"][bass.ds(q * QTOK + half_ * 512, 512), :]
                                 .rearrange("(t p) f -> p t f", p=P)).then_inc(x_in, 16)
                for b in range(4):
                    sp.dma_start(bdc[32 * b:32 * b + 32, :, 32 * b:32 * b + 32],
                                 scratch["wg"].rearrange("(t b) (c d) -> b c t d", b=4, c=SEQ)
                                 [b, :, bass.ds(q * (QTOK // P), QTOK // P), :]).then_inc(bdc_in, 16)

            def load_sums(start):
                sp.dma_start(acc[:], io["xT"].rearrange("(o p) t -> p o t", p=P)[:, :, bass.ds(start, QTOK)])\
                  .then_inc(acc_in, 16)

            def load_weights(q):
                with sp.Fori(0, KVH // 2) as pair:
                    for w in range(2):
                        for piece in range(5):
                            sp.wait_ge(w_lo_done, (q * 4 + pair) * 20 + (10 * w + 2 * piece + 1))
                            sp.wait_ge(cst_in, 16)
                            dst = stage[:, (w + piece) % 2, :, :]
                            if piece < 2:
                                src = io["wqT"].rearrange("(k p) (m n) -> p k m n", p=P, n=GRP * HD)[
                                    :, 2 * piece:2 * piece + 2, bass.ds(pair * 2 + w, 1), :]
                                dst = dst.unsqueeze(2)
                            elif piece == 2:
                                src = scratch["wkv"].rearrange("k p h n -> p k h n")[:, :, bass.ds(pair * 2 + w, 1), :]
                                dst = dst.rearrange("p a (k n) -> p (a k) n", k=2).unsqueeze(2)
                            else:
                                src = io["woT"].rearrange("(h g p) o -> p h g o", p=P, g=GRP)[
                                    :, bass.ds(pair * 2 + w, 1), 2 * (piece - 3):2 * (piece - 3) + 2, :]
                                dst = dst.unsqueeze(1)
                            sp.dma_start(dst, src).then_inc(stage_in[(w + piece) % 2], 16)

            def store_sums(q):
                sp.wait_ge(acc_done, (q + 1) * (4 * UPQ))
                sp.wait_ge(cst_in, 16)
                sp.dma_start(scratch["x2T"].rearrange("(o p) t -> p o t", p=P)[:, :, bass.ds(q * QTOK, QTOK)], acc[:])\
                  .then_inc(acc_out, 16)

            load_tokens(0)
            load_sums(0)
            with sp.Fori(0, NQ - 1) as q:
                load_weights(q)
                sp.wait_ge(scores_done, (q + 1) * UPQ)
                sp.wait_ge(cst_in, 16)
                load_tokens(q + 1)
                store_sums(q)
                sp.wait_ge(acc_out, (q + 1) * 16)
                sp.wait_ge(cst_in, 16)
                load_sums(q * QTOK + QTOK)
            load_weights(NQ - 1)
            store_sums(NQ - 1)
            sp.wait_ge(acc_out, NQ * 16)

        @block.gpsimd
        def _(pool):
            pool.memset(diag[:], 0.0).then_inc(w_lo_done, 1)
            pool.memset(bdc[:], 0.0).then_inc(w_lo_done, 1)
            pool.memset(stage[:], 0.0).then_inc(w_lo_done, 1)
            pool.wait_ge(cst_in, 16)

            def split(load):
                pair, w, pieces = load
                for piece in pieces:
                    hi, lo, k0 = PIECES[piece]
                    for j in range(2):
                        pool.wait_ge(w_hi_done, pair * 20 + (10 * w + 2 * piece + j + 1))
                        pool.tensor_tensor(half(lo, w, k0, j), stage[:, (w + piece) % 2, j, :],
                                           half(hi, w, k0, j).bitcast(F32), ALU.subtract).then_inc(w_lo_done, 1)

            def step(u, n, load):
                for i in range(5):
                    pool.wait_ge(swap_done, n * 5 + (i + 1))
                    s = by_position(swapped[:, i, :])
                    pool.tensor_tensor(s, s, table(i, 1), ALU.mult).then_inc(sin_done, 1)
                    pool.wait_ge(sin_done, n * 5 + (i + 1))
                    pool.wait_ge(cos_done, n * 5 + (i + 1))
                    pool.tensor_tensor(target(i), target(i), swapped[:, i, :], ALU.add).then_inc(rope_done, 1)
                if load:
                    split(load)

            def prologue(q):
                split((q * 4, 0, range(5)))

            with pool.Fori(0, NQ) as q:
                quarter(pool, q, prologue, step, lambda n: None)

        @block.scalar
        def _(act):
            act.wait_ge(cst_in, 16)

            def split(load):
                pair, w, pieces = load
                for piece in pieces:
                    hi, lo, k0 = PIECES[piece]
                    act.wait_ge(stage_in[(w + piece) % 2], pair * 80 + 16 * ((5 * w + piece) // 2 + 1))
                    for j in range(2):
                        act.activation(half(hi, w, k0, j), stage[:, (w + piece) % 2, j, :], ACT.Copy)\
                           .then_inc(w_hi_done, 1)

            def swap(i, n):
                act.wait_ge(proj_done, n * 6 + (i + 1))
                act.activation(swapped[0:64, i, :], proj[SLOT[i]][64:128, :], ACT.Copy)
                act.activation(swapped[64:128, i, :], proj[SLOT[i]][0:64, :], ACT.Copy).then_inc(swap_done, 1)

            def exps(n):
                act.wait_ge(smax, n * 6 - 3)
                act.activation(pr[:], sc[:], ACT.Exp, scale=SCALE).then_inc(exp_done, 1)

            def out_hi(n):
                for t in range(TPC):
                    act.wait_ge(pv_done, n * 4 + (t - 3))
                    act.activation(o_hi[:, :, t * P:(t + 1) * P].rearrange("p g (b s) -> p b g s", b=4),
                                   pv[t % 2][:].rearrange("p (b g s) -> p b g s", b=4, g=GRP), ACT.Copy)\
                       .then_inc(o_hi_done, 1)

            def step(u, n, load):
                swap(0, n)
                if u:
                    exps(n)
                for i in (1, 2, 3):
                    swap(i, n)
                if u:
                    out_hi(n)
                swap(4, n)
                act.wait_ge(proj_done, n * 6 + 6)
                act.activation(v_sb[:], proj[2][:].rearrange("p (t d) -> p t d", t=TPC), ACT.Copy).then_inc(v_done, 1)
                if load:
                    split(load)

            def prologue(q):
                for t in range(QTOK // P):
                    act.wait_ge(h_mm, q * (QTOK // P) + (t + 1))
                    act.activation(h_hi[:, :, t * P:(t + 1) * P], pv[t % 2][:].rearrange("p (k t) -> p k t", k=KB),
                                   ACT.Copy).then_inc(h_hi_done, 1)
                split((q * 4, 0, range(5)))

            def finish(n):
                exps(n)
                out_hi(n)

            with act.Fori(0, NQ) as q:
                quarter(act, q, prologue, step, finish)

        @block.vector
        def _(v):
            v.wait_ge(cst_in, 16)
            mask = cst[:, C_MASK:C_MASK + SEQ].unsqueeze(1).to_broadcast([P, GRP * TPC, SEQ])

            def per_row(ap):
                return ap.unsqueeze(2).to_broadcast([P, GRP * TPC, SEQ])

            def softmax_front(n):
                v.wait_ge(scores_done, n)
                v.transpose(sc[:].rearrange("p a k -> p (a k)"), ps[:]).then_inc(turned, 1)
                v.wait_ge(turned, n)
                v.tensor_tensor(sc[:], sc[:], mask, ALU.add).then_inc(smax, 1)
                v.wait_ge(smax, n * 6 - 5)
                v.tensor_reduce(red[:, 0, :], sc[:], AX.X, ALU.max).then_inc(smax, 1)
                v.wait_ge(smax, n * 6 - 4)
                v.tensor_tensor(sc[:], sc[:], per_row(red[:, 0, :]), ALU.subtract).then_inc(smax, 1)

            def softmax_back(n):
                v.wait_ge(exp_done, n)
                v.tensor_reduce(red[:, 1, :], pr[:], AX.X, ALU.add).then_inc(smax, 1)
                v.wait_ge(smax, n * 6 - 2)
                v.reciprocal(rcp[:], red[:, 1, :]).then_inc(smax, 1)
                v.wait_ge(smax, n * 6 - 1)
                v.tensor_tensor(pr[:], pr[:], per_row(rcp[:]), ALU.mult).then_inc(smax, 1)
                v.wait_ge(smax, n * 6)
                for b in range(4):
                    ins = v.transpose(diag[32 * b:32 * b + 32, :, b, :],
                                      pr[32 * b:32 * b + 32, :, :].rearrange("p (t g) k -> p t (g k)", t=TPC))
                ins.then_inc(diag_done, 1)

            def cosine(i, n):
                v.wait_ge(swap_done, n * 5 + (i + 1))
                v.tensor_tensor(by_position(target(i)), by_position(proj[SLOT[i]][:]), table(i, 0), ALU.mult)\
                 .then_inc(cos_done, 1)

            def out_lo(n):
                for t in range(TPC):
                    v.wait_ge(o_hi_done, n * 4 + (t - 3))
                    def view(o):
                        return o[:, :, t * P:(t + 1) * P].rearrange("p g (b s) -> p b g s", b=4)
                    v.tensor_tensor(view(o_lo), pv[t % 2][:].rearrange("p (b g s) -> p b g s", b=4, g=GRP),
                                    view(o_hi).bitcast(F32), ALU.subtract).then_inc(o_lo_done, 1)

            def accumulate(n, c):
                for o in range(KB):
                    v.wait_ge(wo_done, n * 4 + (o - 3))
                    a = acc[:, o, c * CH:(c + 1) * CH]
                    v.tensor_tensor(a, a, po[o % 2][:], ALU.add).then_inc(acc_done, 1)

            def step(u, n, load):
                if u:
                    softmax_front(n)
                cosine(0, n)
                if u:
                    softmax_back(n)
                for i in (1, 2, 3):
                    cosine(i, n)
                if u:
                    out_lo(n)
                cosine(4, n)
                if u:
                    accumulate(n, (u - 1) % 2)

            def prologue(q):
                for t in range(QTOK // P):
                    v.wait_ge(h_hi_done, q * (QTOK // P) + (t + 1))
                    h = slice(t * P, (t + 1) * P)
                    v.tensor_tensor(h_lo[:, :, h], pv[t % 2][:].rearrange("p (k t) -> p k t", k=KB),
                                    h_hi[:, :, h].bitcast(F32), ALU.subtract).then_inc(h_lo_done, 1)
                v.wait_ge(acc_in, q * 16 + 16)

            def finish(n):
                softmax_front(n)
                softmax_back(n)
                out_lo(n)
                accumulate(n, 1)

            with v.Fori(0, NQ) as q:
                quarter(v, q, prologue, step, finish)

        @block.tensor
        def _(t_):
            def product(out, left, right, blocks):
                for k in range(blocks):
                    (l_hi, l_lo), (r_hi, r_lo) = left(k), right(k)
                    t_.matmul(out, l_hi, r_hi, start=k == 0, stop=False)
                    t_.matmul(out, l_hi, r_lo, start=False, stop=False)
                    mm = t_.matmul(out, l_lo, r_hi, start=False, stop=k == blocks - 1)
                return mm

            def item(i, u, n):
                w, c = (u // 2) % 2, u % 2
                if i >= 3:
                    t_.wait_ge(cos_done, n * 5 + (i - 2))
                elif u and i < 2:
                    t_.wait_ge(cos_done, n * 5 + (i - 1))
                elif u:
                    t_.wait_ge(v_done, n)
                tok = slice(c * CH, (c + 1) * CH)
                if i == 5:
                    for t in range(TPC):
                        tt = slice(c * CH + t * P, c * CH + (t + 1) * P)
                        mm = product(proj[2][:, t * HD:(t + 1) * HD],
                                     lambda k: (h_hi[:, k, tt], h_lo[:, k, tt]),
                                     lambda k: (wkv_hi[:, w, k, HD:], wkv_lo[:, w, k, HD:]), KB)
                else:
                    wh, wl = (wkv_hi, wkv_lo) if i == 3 else (wq_hi, wq_lo)
                    cols = slice(0, HD) if i == 3 else slice(min(i, 3) * HD, min(i, 3) * HD + HD)
                    mm = product(proj[SLOT[i]][:],
                                 lambda k: (wh[:, w, k, cols], wl[:, w, k, cols]),
                                 lambda k: (h_hi[:, k, tok], h_lo[:, k, tok]), KB)
                mm.then_inc(proj_done, 1)

            def values(n):
                t_.wait_ge(diag_done, n)
                t_.wait_ge(v_done, n)
                for t in range(TPC):
                    if t >= 2:
                        t_.wait_ge(o_lo_done, n * 4 + (t - 5))
                    t_.matmul(pv[t % 2][:], v_sb[:, t, :], diag[:, t, :, :].rearrange("p b s -> p (b s)"),
                              start=True, stop=True).then_inc(pv_done, 1)

            def output(u, n, w, first):
                t_.wait_ge(o_lo_done, n * 4)
                if first:
                    t_.wait_ge(w_lo_done, n * 5 + 8)
                for o in range(KB):
                    if u > 1 or o > 1:
                        t_.wait_ge(acc_done, n * 4 + (max(o - 1, 0) - 4))
                    cols = slice(o * P, (o + 1) * P)
                    product(po[o % 2][:],
                            lambda g: (wo_hi[:, w, g, cols], wo_lo[:, w, g, cols]),
                            lambda g: (o_hi[:, g, :], o_lo[:, g, :]), GRP).then_inc(wo_done, 1)

            def scores(u, n):
                t_.wait_ge(rope_done, n * 5 + 5)
                if u:
                    t_.wait_ge(turned, n)
                for b in range(BCH):
                    s = slice(b * SEQ, (b + 1) * SEQ)
                    r = 32 * (b % 4)
                    mm = t_.matmul(ps[r:r + 32, (b // 4) * P:(b // 4 + 1) * P].rearrange("p (g s) -> p g s", g=GRP),
                                   kT[:, s], qT[:, :, s], start=True, stop=True)
                mm.then_inc(scores_done, 1)

            def step(u, n, load):
                if u % 2 == 0:
                    t_.wait_ge(w_lo_done, n * 5 + 9)
                for i in range(4):
                    item(i, u, n)
                if u:
                    values(n)
                item(4, u, n)
                item(5, u, n)
                if u:
                    output(u, n, ((u - 1) // 2) % 2, u % 2 == 1)
                scores(u, n)

            def prologue(q):
                t_.wait_ge(bdc_in, q * 64 + 64)
                t_.wait_ge(x_in, q * 32 + 32)
                for t in range(QTOK // P):
                    if t >= 2:
                        t_.wait_ge(h_lo_done, q * (QTOK // P) + (t - 1))
                    for k in range(KB):
                        mm = t_.matmul(pv[t % 2][:, k * P:(k + 1) * P], xt[:, t, k * P:(k + 1) * P], bdc[:, t, :],
                                       start=True, stop=True)
                    mm.then_inc(h_mm, 1)
                t_.wait_ge(h_lo_done, q * (QTOK // P) + QTOK // P)

            def finish(n):
                values(n)
                output(UPQ, n, 1, False)

            with t_.Fori(0, NQ) as q:
                quarter(t_, q, prologue, step, finish)


def ssm_and_ffn(nc, io, scratch, out):
    NCH = TOK // CH
    ANCH = TOK // 2
    NT = ANCH // P
    HU = 4
    with ExitStack() as ctx:
        def sb(name, shape, dt=F32):
            return ctx.enter_context(nc.sbuf_tensor(name, shape, dt))

        def sem(name):
            return ctx.enter_context(nc.semaphore(name))

        cst = sb("c_cst", [P, C_W])
        x2 = sb("c_x2", [P, KB, TOK])
        yT = sb("c_y", [P, KB, TOK])
        toep = sb("c_toep", [P, HU, DM])
        lens_i = sb("c_lens_i", [P, BATCH], I32)
        lens = sb("c_lens", [P, BATCH])
        keep = sb("c_keep", [P, KB, BATCH])
        wT = sb("c_wT", [P, KB, DM])
        wza = sb("c_wza", [P, KB, RANK + NE])
        bmat = sb("c_bmat", [P, DM])
        limes = sb("c_limes", [NE, RANK])
        pick = sb("c_pick", [RANK + NE, 2 * NE])
        bias = sb("c_bias", [P, KB])
        bias8 = sb("c_bias8", [RANK + NE, 1])
        zh = sb("c_zh", [P, TOK])
        gate = sb("c_gate", [P, NT, 2 * NE])
        g0, g1, g2 = (sb(f"c_g{i}", [P, NT, NE]) for i in range(3))
        top = sb("c_top", [P, NT, 8])
        row = sb("c_row", [P, 2, NT])
        big = sb("c_big", [P, 4, 2])
        wgt = sb("c_wgt", [NE, ANCH])
        fin = sb("c_fin", [P, 4, CH])
        bank = [ctx.enter_context(nc.psum_tensor(f"c_ps{i}", [P, 512], F32)) for i in range(8)]

        cst_in, x2_in, par_in, len_in = sem("c_cst_in"), sem("c_x2_in"), sem("c_par_in"), sem("c_len_in")
        toep_in = [sem(f"toep_in{i}") for i in range(HU)]
        conv_done, y_done = sem("conv_done"), sem("y_done")
        keep_done = sem("keep_done")
        zh_mm, zh_done = sem("zh_mm"), sem("zh_done")
        padded = sem("padded")
        pick_clear, pick_in = sem("pick_clear"), sem("pick_in")
        gate_mm, gate_done = sem("gate_mm"), sem("gate_done")
        peak_local, peak_all = sem("peak_local"), sem("peak_all")
        g_exp_in, g_exp = sem("g_exp_in"), sem("g_exp")
        chain = sem("c_chain")
        w_ready, w_turned, w_copied = sem("w_ready"), sem("w_turned"), sem("w_copied")
        mix_mm, mix_done = sem("mix_mm"), sem("mix_done")
        base_mm, base_done = sem("base_mm"), sem("base_done")
        delta_mm, fin_done = sem("delta_mm"), sem("fin_done")
        out_done = [sem(f"out_done{i}") for i in range(4)]
        block = ctx.enter_context(nc.Block())

        kp = scratch["kpad"]

        def at_position(ap, s):
            return ap.rearrange("p o (b s) -> p o b s", s=SEQ)[:, :, :, bass.ds(s, 1)]

        @block.sync
        def _(sp):
            sp.dma_start(cst[:], io["consts"]).then_inc(cst_in, 16)
            sp.dma_start(lens_i[:], io["length"].partition_broadcast(P)).then_inc(len_in, 16)
            for o in range(KB):
                sp.dma_start(x2[:, o, :], scratch["x2T"][o * P:(o + 1) * P, :]).then_inc(x2_in, 16)

            def load_toeplitz(s, i):
                base = kp[bass.ds(s, 1), 0:DM]
                src = bass.AP(tensor=base.tensor, offset=base.offset, ap=[[1, P], [1, DM]])
                sp.dma_start(toep[:, i, :], src).then_inc(toep_in[i], 16)

            for i in range(HU):
                load_toeplitz(i, i)
            with sp.Fori(0, SEQ // HU - 1) as g:
                for i in range(HU):
                    sp.wait_ge(conv_done, g * HU + (i + 1))
                    sp.wait_ge(cst_in, 16)
                    load_toeplitz(g * HU + (HU + i), i)
            sp.dma_start(wT[:], io["wT"].rearrange("(k p) n -> p k n", p=P)).then_inc(par_in, 16)
            sp.dma_start(wza[:], io["wza"].rearrange("(k p) n -> p k n", p=P)).then_inc(par_in, 16)
            sp.wait_ge(padded, 2)
            sp.dma_start(bmat[0:RANK, :], io["bmat"]).then_inc(par_in, 16)
            sp.dma_start(limes[:], io["limes"]).then_inc(par_in, 16)
            sp.dma_start(bias[:], io["bias"]).then_inc(par_in, 16)
            sp.dma_start(bias8[RANK:, :], io["bias8"].rearrange("(p a) -> p a", a=1)).then_inc(par_in, 16)
            sp.wait_ge(pick_clear, 1)
            sp.dma_start(pick[0:RANK, 0:NE], io["limesT"]).then_inc(pick_in, 16)
            sp.dma_start(pick[RANK:, NE:], io["consts"][0:NE, C_ID:C_ID + NE]).then_inc(pick_in, 16)
            with sp.Fori(0, NCH) as c:
                for o in range(KB):
                    sp.wait_ge(fin_done, c * KB + (KB + o + 1))
                    sp.wait_ge(cst_in, 16)
                    sp.dma_start(out[o * P:(o + 1) * P, bass.ds(c * CH, CH)], fin[:, o, :])\
                      .then_inc(out_done[o], 16)
            for o in range(KB):
                sp.wait_ge(out_done[o], NCH * 16)

        @block.gpsimd
        def _(pool):
            pool.memset(pick[:], 0.0).then_inc(pick_clear, 1)
            pool.memset(zh[:], 0.0).then_inc(padded, 1)
            pool.memset(bmat[:], 0.0).then_inc(padded, 1)
            pool.wait_ge(peak_local, 1)
            pool.partition_all_reduce(big[:, 1, :], big[:, 0, :], P, bass.bass_isa.ReduceOp.max)\
                .then_inc(peak_all, 1)

        @block.tensor
        def _(t_):
            t_.wait_ge(x2_in, KB * 16)
            with t_.Fori(0, SEQ // HU) as g:
                for i in range(HU):
                    t_.wait_ge(toep_in[i], g * 16 + 16)
                    t_.wait_ge(y_done, g * HU + (i + 1))
                    for d in range(KB):
                        mm = t_.matmul(bank[i][:, d * P:].rearrange("p (o b) -> p o b", b=P),
                                       toep[:, i, d * P:(d + 1) * P],
                                       at_position(x2[:, 0:KB - d, :], g * HU + i),
                                       start=d == 0, stop=d == KB - 1)
                    mm.then_inc(conv_done, 1)
            t_.wait_ge(y_done, HU + SEQ)
            t_.wait_ge(par_in, 6 * 16)
            def low_rank(c, first):
                for i in range(2):
                    if not first:
                        t_.wait_ge(zh_done, c * 4 + (2 * i - 2))
                    for k in range(KB):
                        mm = t_.matmul(bank[4 + i][0:RANK + NE, :], wza[:, k, :], yT[:, k, bass.ds(c * (2 * CH) + i * CH, CH)],
                                       start=k == 0, stop=k == KB - 1)
                    mm.then_inc(zh_mm, 1)

            low_rank(0, True)
            with t_.Fori(1, NCH // 2) as c:
                low_rank(c, False)
            t_.wait_ge(zh_done, 2 * NCH)
            t_.wait_ge(pick_in, 32)
            for i in range(NT):
                mm = t_.matmul(bank[6][:, i * 2 * NE:(i + 1) * 2 * NE],
                               zh[0:RANK + NE, 2 * P * i:2 * P * (i + 1)].rearrange("p (a s) -> p a s", s=2)[:, :, 1],
                               pick[:], start=True, stop=True)
            mm.then_inc(gate_mm, 1)

            def base(c):
                for o in range(KB):
                    t_.wait_ge(base_done, c * KB + (o + 1))
                    for k in range(KB):
                        mm = t_.matmul(bank[o][:], wT[:, k, o * P:(o + 1) * P], yT[:, k, bass.ds(c * CH, CH)],
                                       start=k == 0, stop=k == KB - 1)
                    mm.then_inc(base_mm, 1)

            with t_.Fori(0, NCH // 2) as c:
                base(c)
            t_.wait_ge(w_ready, 1)
            for i in range(4):
                if i >= 2:
                    t_.wait_ge(w_copied, i - 1)
                for j in range(4):
                    mm = t_.transpose(bank[6 + i % 2][0:NE, j * P:(j + 1) * P], g0[:, 4 * i + j, :], cst[:, C_ID:C_ID + P])
                mm.then_inc(w_turned, 1)
            for i in range(4):
                t_.wait_ge(w_copied, i + 1)
                if i >= 2:
                    t_.wait_ge(mix_done, i - 1)
                t_.matmul(bank[4 + i % 2][0:RANK, :], limes[:], wgt[:, i * 512:(i + 1) * 512],
                          start=True, stop=True).then_inc(mix_mm, 1)
            with t_.Fori(NCH // 2, NCH) as c:
                base(c)
            t_.wait_ge(mix_done, 4)
            t_.wait_ge(base_done, KB + NCH * KB)
            with t_.Fori(0, NCH) as c:
                for o in range(KB):
                    t_.wait_ge(fin_done, c * KB + (o + 1))
                    t_.matmul(bank[o][:], bmat[:, o * P:(o + 1) * P], zh[:, bass.ds(c * CH, CH)],
                              start=True, stop=True).then_inc(delta_mm, 1)

        @block.scalar
        def _(act):
            act.wait_ge(par_in, 6 * 16)
            act.wait_ge(padded, 2)
            with act.Fori(0, NCH // 2) as c:
                for i in range(2):
                    act.wait_ge(zh_mm, c * 2 + (i + 1))
                    cols = bass.ds(c * (2 * CH) + i * CH, CH)
                    act.activation(zh[0:RANK, cols], bank[4 + i][0:RANK, :], ACT.Copy).then_inc(zh_done, 1)
                    act.activation(zh[RANK:RANK + NE, cols], bank[4 + i][RANK:RANK + NE, :], ACT.Identity, bias=bias8[RANK:, :])\
                       .then_inc(zh_done, 1)
            act.wait_ge(g_exp_in, 1)
            act.activation(g1[:], g0[:], ACT.Exp).then_inc(g_exp, 1)
            act.wait_ge(g_exp_in, 2)
            act.activation(g2[:], g1[:], ACT.Exp, scale=-2.0).then_inc(g_exp, 1)

        @block.vector
        def _(v):
            done = [0]

            def then(ins):
                done[0] += 1
                ins.then_inc(chain, 1)
                v.wait_ge(chain, done[0])

            def per_token(ap):
                return ap.unsqueeze(2).to_broadcast([P, NT, NE])

            for o in range(KB):
                v.memset(fin[:, o, 0:1], 0.0).then_inc(base_done, 1)
                v.memset(fin[:, o, 1:2], 0.0).then_inc(fin_done, 1)
            v.wait_ge(len_in, 16)
            v.wait_ge(cst_in, 16)
            then(v.tensor_copy(lens[:], lens_i[:]))
            for o in range(KB):
                v.tensor_scalar(keep[:, o, :], lens[:], cst[:, C_PIDX + o:C_PIDX + o + 1], None, ALU.is_gt)\
                 .then_inc(y_done, 1)
            v.wait_ge(y_done, HU)
            with v.Fori(0, SEQ // HU) as g:
                for i in range(HU):
                    v.wait_ge(conv_done, g * HU + (i + 1))
                    v.tensor_tensor(at_position(yT[:], g * HU + i), bank[i][:].rearrange("p (o b) -> p o b", b=P).unsqueeze(3),
                                    keep[:].unsqueeze(3), ALU.mult).then_inc(y_done, 1)
            v.wait_ge(gate_mm, 1)
            then(v.tensor_copy(gate[:].rearrange("p t e -> p (t e)"), bank[6][:, 0:NT * 2 * NE]))
            v.tensor_reduce(big[:, 0, :], gate[:].rearrange("p t (s e) -> p s t e", s=2), AX.XY, ALU.max,
                            apply_absolute_value=True).then_inc(peak_local, 1)

            def base(c):
                for o in range(KB):
                    v.wait_ge(base_mm, c * KB + (o + 1))
                    xs = x2[:, o, bass.ds(c * CH, CH)]
                    v.scalar_tensor_tensor(xs, bank[o][:], bias[:, o:o + 1], xs, ALU.add, ALU.add)\
                     .then_inc(base_done, 1)

            with v.Fori(0, NCH // 2) as c:
                base(c)
            v.wait_ge(peak_all, 1)
            then(v.tensor_scalar(big[:, 2, :], big[:, 1, :], 1e-6, None, ALU.max))
            then(v.reciprocal(big[:, 3, :], big[:, 2, :]))
            then(v.tensor_scalar(big[:, 3, :], big[:, 3, :], 0.5, None, ALU.mult))
            then(v.tensor_scalar(g0[:], gate[:, :, 0:NE], big[:, 3, 0:1], None, ALU.mult))
            then(v.tensor_scalar(g1[:], gate[:, :, NE:], big[:, 3, 1:2], None, ALU.mult))
            then(v.tensor_tensor(g0[:], g0[:], g1[:], ALU.add))
            then(v.tensor_reduce(row[:, 0, :], g0[:], AX.X, ALU.max))
            v.tensor_tensor(g0[:], g0[:], per_token(row[:, 0, :]), ALU.subtract).then_inc(g_exp_in, 1)
            v.wait_ge(g_exp, 1)
            then(v.tensor_reduce(row[:, 0, :], g1[:], AX.X, ALU.add))
            then(v.reciprocal(row[:, 1, :], row[:, 0, :]))
            then(v.tensor_tensor(g0[:], g1[:], per_token(row[:, 1, :]), ALU.mult))
            for i in range(NT):
                ins = v.max(top[:, i, :], g0[:, i, :])
            then(ins)
            v.tensor_tensor(g1[:], g0[:], top[:, :, 1:2].to_broadcast([P, NT, NE]), ALU.subtract).then_inc(g_exp_in, 1)
            v.wait_ge(g_exp, 2)
            then(v.tensor_scalar(g2[:], g2[:], 1.0, None, ALU.add))
            then(v.reciprocal(g2[:], g2[:]))
            then(v.tensor_tensor(g0[:], g0[:], g2[:], ALU.mult))
            then(v.tensor_reduce(row[:, 0, :], g0[:], AX.X, ALU.add))
            then(v.tensor_scalar(row[:, 0, :], row[:, 0, :], 1e-9, None, ALU.add))
            then(v.reciprocal(row[:, 1, :], row[:, 0, :]))
            v.tensor_tensor(g0[:], g0[:], per_token(row[:, 1, :]), ALU.mult).then_inc(w_ready, 1)
            for i in range(4):
                v.wait_ge(w_turned, i + 1)
                v.tensor_copy(wgt[:, i * 512:(i + 1) * 512], bank[6 + i % 2][0:NE, :]).then_inc(w_copied, 1)
            for i in range(4):
                v.wait_ge(mix_mm, i + 1)
                z = zh[0:RANK, i * 1024:(i + 1) * 1024].rearrange("p (a s) -> p a s", s=2)
                v.scalar_tensor_tensor(z, z, 0.5, bank[4 + i % 2][0:RANK, :].unsqueeze(2).to_broadcast([RANK, 512, 2]),
                                       ALU.mult, ALU.mult).then_inc(mix_done, 1)
            with v.Fori(NCH // 2, NCH) as c:
                base(c)

            def last_sum(c, first):
                for o in range(KB):
                    v.wait_ge(delta_mm, c * KB + (o + 1))
                    if not first:
                        v.wait_ge(out_done[o], c * 16)
                    v.tensor_tensor(fin[:, o, :], bank[o][:], x2[:, o, bass.ds(c * CH, CH)], ALU.add)\
                     .then_inc(fin_done, 1)

            last_sum(0, True)
            with v.Fori(1, NCH) as c:
                last_sum(c, False)


def program(nc, io, out):
    scratch = {
        "wg": nc.dram_tensor("wg_scratch", [BATCH, SEQ * SEQ], F32, kind="Internal").ap(),
        "wkv": nc.dram_tensor("wkv_scratch", [KB, P, KVH, 2 * HD], F32, kind="Internal").ap(),
        "kpad": nc.dram_tensor("kpad_scratch", [SEQ, KPAD], F32, kind="Internal").ap(),
        "x2T": nc.dram_tensor("x2T_scratch", [DM, TOK], F32, kind="Internal").ap(),
    }
    weights_and_ssm(nc, io, scratch)
    attention(nc, io, scratch)
    ssm_and_ffn(nc, io, scratch, out)


def layouts(x, itok_B_0_15, itok_B_78_3631, L0_cond_weights, L0_attn_Wq, L0_attn_Wkr, L0_attn_Wdk, L0_attn_Wupk,
            L0_attn_Wupv, L0_attn_Wo, L0_cond2_log_dt, L0_cond2_C, L0_cond2_log_A_real, L0_cond2_A_imag, L0_cond2_D,
            L0_ffn_W, L0_ffn_b, L0_ffn_A, L0_ffn_Bmat, L0_ffn_LiMEs):
    def rev(a, axis):
        a = np.moveaxis(a, axis, 0)
        a = a.reshape(KB, P, *a.shape[1:])[:, ::-1].reshape(a.shape)
        return np.moveaxis(a, 0, axis)

    tok = x.reshape(TOK, DM)
    return {
        "consts": constants(),
        "x_tok": tok, "xT": rev(tok.T, 0), "cond": itok_B_0_15, "length": itok_B_78_3631,
        "w_cond": L0_cond_weights.reshape(NST, SEQ * SEQ),
        "wqT": L0_attn_Wq.T, "wkrT": L0_attn_Wkr.T, "wdk": L0_attn_Wdk, "wupkT": L0_attn_Wupk.T,
        "wupvT": L0_attn_Wupv.T, "woT": rev(L0_attn_Wo.T, 1),
        "log_dt": L0_cond2_log_dt, "C_re": L0_cond2_C[..., 0].T, "C_im": L0_cond2_C[..., 1].T,
        "log_A_real": L0_cond2_log_A_real.T, "A_imag": L0_cond2_A_imag.T, "D": L0_cond2_D,
        "wT": rev(L0_ffn_W.T, 1), "wza": np.concatenate([L0_ffn_A, L0_ffn_W[:NE].T], 1),
        "bias": rev(L0_ffn_b, 0).reshape(KB, P).T, "bias8": L0_ffn_b[:NE], "bmat": rev(L0_ffn_Bmat, 1),
        "limes": L0_ffn_LiMEs, "limesT": L0_ffn_LiMEs.T,
    }


def kernel(**inputs):
    import concourse.bacc as _bacc
    from concourse.bass_utils import run_bass_kernel_spmd as _run

    nc = _bacc.Bacc("TRN2", target_bir_lowering=False, num_devices=1)
    arrays, io = {}, {}
    for name, a in layouts(**{k: np.asarray(v) for k, v in inputs.items()}).items():
        a = np.ascontiguousarray(a)
        arrays[f"in_{name}"] = a
        io[name] = nc.dram_tensor(f"in_{name}", a.shape, mybir.dt.from_np(a.dtype), kind="ExternalInput").ap()
    out = nc.dram_tensor("out", [DM, TOK], F32, kind="ExternalOutput").ap()
    program(nc, io, out)
    r = _run(nc, [arrays], core_ids=[0])
    o = np.asarray(r.results[0]["out"]).reshape(KB, P, TOK)[:, ::-1].reshape(DM, TOK)
    return np.ascontiguousarray(o.T).reshape(BATCH, SEQ, DM)
```

```python
from contextlib import ExitStack
import math

import numpy as np

import concourse.bass as bass
from concourse import mybir

F32 = mybir.dt.float32
F32R = mybir.dt.float32r
I32 = mybir.dt.int32
ALU = mybir.AluOpType
ACT = mybir.ActivationFunctionType
AX = mybir.AxisListType

P = 128
BATCH, SEQ, DM = 128, 32, 512
TOK = BATCH * SEQ
KB = DM // P
KVH, GRP, HD = 8, 4, 128
CH = 512
BCH = CH // SEQ
QTOK = 1024
NQ = TOK // QTOK
UPQ = KVH * (QTOK // CH)
TPC = CH // P
NST, NSTATE = 16, 64
NE, RANK = 8, 32
NC_, NF_ = 16, 32
NSEC = 5
SECW = [NC_, NC_, NF_, 1, 1]
SECO = [0, NC_, 2 * NC_, 2 * NC_ + NF_, 2 * NC_ + NF_ + 1]
NANG = 2 * NC_ + NF_ + 2
KPAD = P - 1 + DM + 1
SCALE = 1.0 / math.sqrt(HD)
TWO_PI = 2.0 * math.pi
PI_HEAD = 6.28125
PI_MID = float(np.float32(np.round((TWO_PI - PI_HEAD) * 2 ** 22) / 2 ** 22))
PI_TAIL = TWO_PI - PI_HEAD - PI_MID
LN2_HEAD = float(np.float32(np.round(math.log(2.0) * 2 ** 12) / 2 ** 12))
LN2_TAIL = math.log(2.0) - LN2_HEAD
MAGIC = float(1.5 * 2 ** 23)

C_ROPE = 0
C_MASK = C_ROPE + 4 * SEQ
C_ID = C_MASK + SEQ
C_PIDX = C_ID + P
C_LAG = C_PIDX + KB
C_PHASE = C_LAG + NANG
C_W = C_PHASE + 2 * NSEC


def constants():
    c = np.zeros((P, C_W), np.float32)
    inv = 1.0 / 10000.0 ** (np.arange(0, HD, 2, dtype=np.float32) / HD)
    freqs = np.outer(np.arange(SEQ, dtype=np.float32), inv)
    emb = np.concatenate([freqs, freqs], -1)
    cos, sin = np.cos(emb).T, np.sin(emb).T
    sin = np.concatenate([-sin[:64], sin[64:]], 0)
    roped = (np.arange(HD) % 64 < 32)[:, None]
    c[:, 0:SEQ], c[:, SEQ:2 * SEQ] = cos, sin
    c[:, 2 * SEQ:3 * SEQ], c[:, 3 * SEQ:4 * SEQ] = np.where(roped, cos, 1.0), np.where(roped, sin, 0.0)
    pos = np.arange(P) % SEQ
    c[:, C_MASK:C_MASK + SEQ] = np.where(np.arange(SEQ)[None] <= pos[:, None], 0.0, -1e9)
    c[:, C_ID:C_ID + P] = np.eye(P)
    c[:, C_PIDX:C_PIDX + KB] = np.arange(P)[:, None] + P * np.arange(KB)[None]
    coarse, fine = NF_ * np.arange(NC_), np.arange(NF_)
    c[:, C_LAG:C_LAG + NANG] = np.concatenate([coarse, coarse, fine, [0.5, 0.5]])[None]
    im = np.arange(P)[:, None] >= NSTATE
    quarter = np.where(im, 1, 0)
    turns = np.concatenate([quarter + 1, quarter, 1 - quarter, 0 * quarter, 0 * quarter + 1], 1) * 0.25
    c[:, C_PHASE:C_PHASE + NSEC] = turns
    c[:, C_PHASE + NSEC:C_PHASE + 2 * NSEC] = turns * TWO_PI
    return c


def weights_and_ssm(nc, io, scratch):
    with ExitStack() as ctx:
        def sb(name, shape, dt=F32):
            return ctx.enter_context(nc.sbuf_tensor(name, shape, dt))

        def sem(name):
            return ctx.enter_context(nc.semaphore(name))

        cst = sb("a_cst", [P, C_W])
        wdk = sb("a_wdk", [P, KB, DM])
        wupk = sb("a_wupk", [P, KB, DM])
        wupv = sb("a_wupv", [P, KB, KVH * HD])
        wkr = sb("a_wkr", [P, KB, DM])
        wkv = sb("a_wkv", [P, 2, KVH, 2 * HD])
        condi = sb("a_condi", [NST, BATCH], I32)
        condf = sb("a_condf", [NST, BATCH])
        onehot = sb("a_onehot", [NST, BATCH])
        wcond = sb("a_wcond", [NST, SEQ * SEQ])
        wg = sb("a_wg", [P, SEQ * SEQ])
        par = sb("a_par", [P, 5, SEQ])
        dskip = sb("a_dskip", [1, SEQ])
        eab = sb("a_eab", [P, 2, SEQ])
        ek = sb("a_ek", [P, 2, SEQ])
        er_ = sb("a_er", [P, 2, SEQ])
        ei_ = sb("a_ei", [P, 2, SEQ], I32)
        xy = sb("a_xy", [P, 2, SEQ])
        tnh = sb("a_tnh", [P, SEQ])
        mag = sb("a_mag", [P, SEQ, NC_ + NF_])
        ang = sb("a_ang", [P, SEQ, NANG])
        turn = sb("a_turn", [P, SEQ, NANG])
        sn = sb("a_sn", [P, SEQ, NANG])
        tmp = sb("a_tmp", [P, 16, SEQ])
        lft = sb("a_lft", [P, SEQ, NC_])
        lf2 = sb("a_lf2", [P, SEQ, NC_])
        rgt = sb("a_rgt", [P, SEQ, NF_])
        kern = sb("a_kern", [NC_, SEQ, NF_])
        zrow = sb("a_zrow", [SEQ, P])
        pe = [ctx.enter_context(nc.psum_tensor(f"a_pe{i}", [P, 512], F32)) for i in range(3)]
        pg = ctx.enter_context(nc.psum_tensor("a_pg", [P, 2, 512], F32))
        pk = ctx.enter_context(nc.psum_tensor("a_pk", [P, 2, 512], F32))

        cst_in, ssm_in, cond_in = sem("a_cst_in"), sem("a_ssm_in"), sem("a_cond_in")
        wdk_in, wupk_in, wupv_in, wkr_in = (sem(f"a_{x}_in") for x in ("wdk", "wupk", "wupv", "wkr"))
        hot = sem("a_hot")
        gathered = sem("a_gathered")
        wg_ready = sem("a_wg_ready")
        folded = sem("a_folded")
        unfolded = sem("a_unfolded")
        roped = sem("a_roped")
        xy_ready, mag_ready = sem("a_xy_ready"), sem("a_mag_ready")
        mags, ang_ready, sines = sem("a_mags"), sem("a_ang_ready"), sem("a_sines")
        factors = sem("a_factors")
        kernel_mm = sem("a_kernel_mm")
        kern_ready = sem("a_kern_ready")
        zeroed = sem("a_zeroed")
        chain = sem("a_chain")
        stored = sem("a_stored")
        wkv_out = [sem("a_wkv_out0"), sem("a_wkv_out1")]
        block = ctx.enter_context(nc.Block())

        @block.sync
        def _(sp):
            sp.dma_start(cst[:], io["consts"]).then_inc(cst_in, 16)
            sp.dma_start(condi[:], io["cond"].partition_broadcast(NST)).then_inc(cond_in, 16)
            sp.dma_start(wcond[:], io["w_cond"]).then_inc(cond_in, 16)
            sp.dma_start(wdk[:], io["wdk"].rearrange("(c p) n -> p c n", p=P)).then_inc(wdk_in, 16)
            sp.dma_start(wupk[:], io["wupkT"].rearrange("(c p) n -> p c n", p=P)).then_inc(wupk_in, 16)
            for n, name in ((0, "log_A_real"), (2, "A_imag"), (3, "C_re"), (4, "C_im")):
                for half in range(2):
                    sp.dma_start(par[half * NSTATE:(half + 1) * NSTATE, n, :], io[name]).then_inc(ssm_in, 16)
            sp.dma_start(par[:, 1, :], io["log_dt"].partition_broadcast(P)).then_inc(ssm_in, 16)
            sp.dma_start(dskip[:], io["D"].rearrange("(a h) -> a h", a=1)).then_inc(ssm_in, 16)
            sp.dma_start(wupv[:], io["wupvT"].rearrange("(c p) n -> p c n", p=P)).then_inc(wupv_in, 16)
            sp.dma_start(wkr[:], io["wkrT"].rearrange("(c p) n -> p c n", p=P)).then_inc(wkr_in, 16)
            sp.wait_ge(wg_ready, 2)
            sp.dma_start(scratch["wg"], wg[:]).then_inc(stored, 16)
            for m in range(KB):
                sp.wait_ge(unfolded, 3 * (m + 1))
                sp.wait_ge(roped, m + 1)
                sp.dma_start(scratch["wkv"][m], wkv[:, m % 2, :, :]).then_inc(wkv_out[m % 2], 16)
            sp.wait_ge(zeroed, 1)
            sp.dma_start(scratch["kpad"][:, 0:P - 1], zrow[:, 0:P - 1]).then_inc(stored, 16)
            sp.wait_ge(kern_ready, 3)
            sp.dma_start(scratch["kpad"][:, P - 1:P - 1 + DM].rearrange("h (a c) -> a h c", c=NF_),
                         kern[:]).then_inc(stored, 16)
            sp.wait_ge(stored, 48)
            sp.wait_ge(wkv_out[0], 32)
            sp.wait_ge(wkv_out[1], 32)

        @block.gpsimd
        def _(pool):
            pool.memset(zrow[:], 0.0).then_inc(zeroed, 1)

        @block.scalar
        def _(act):
            for j in range(2):
                act.wait_ge(gathered, j + 1)
                act.activation(wg[:, j * 512:(j + 1) * 512], pg[:, j, :], ACT.Copy).then_inc(wg_ready, 1)
            act.wait_ge(xy_ready, 1)
            act.activation(tnh[:], xy[:, 0, :], ACT.Tanh, scale=0.5).then_inc(mags, 1)
            act.wait_ge(mag_ready, 1)
            act.activation(mag[:], mag[:], ACT.Exp).then_inc(mags, 1)
            for m in range(KB):
                if m == 2:
                    act.wait_ge(ang_ready, 1)
                    act.activation(sn[:], ang[:], ACT.Sin).then_inc(sines, 1)
                if m >= 2:
                    act.wait_ge(wkv_out[m % 2], 16)
                act.wait_ge(folded, 3 * m + 1)
                act.activation(wkv[:, m % 2, :, 0:HD].rearrange("p h (a r) -> p h a r", a=2)[:, :, :, 32:64],
                               pe[0][:].rearrange("p (h a r) -> p h a r", h=KVH, a=2), ACT.Copy).then_inc(unfolded, 1)
                for j in range(2):
                    act.wait_ge(folded, 3 * m + 2 + j)
                    act.activation(wkv[:, m % 2, 4 * j:4 * j + 4, HD:2 * HD],
                                   pe[1 + j][:].rearrange("p (h d) -> p h d", h=4), ACT.Copy).then_inc(unfolded, 1)

        @block.tensor
        def _(t):
            t.wait_ge(hot, 1)
            for j in range(2):
                t.matmul(pg[:, j, :], onehot[:], wcond[:, j * 512:(j + 1) * 512],
                         start=True, stop=True).then_inc(gathered, 1)
            t.wait_ge(wdk_in, 16)
            t.wait_ge(wupk_in, 16)
            for m in range(KB):
                for j in range(3):
                    if m == 0 and j == 1:
                        t.wait_ge(wupv_in, 16)
                    if m:
                        t.wait_ge(unfolded, 3 * (m - 1) + j + 1)
                    for c in range(KB):
                        w = wupk[:, c, :] if j == 0 else wupv[:, c, (j - 1) * 512:j * 512]
                        mm = t.matmul(pe[j][:], wdk[:, c, m * P:(m + 1) * P], w, start=c == 0, stop=c == KB - 1)
                    mm.then_inc(folded, 1)
            t.wait_ge(factors, 2)
            for h in range(SEQ):
                mm = t.matmul(pk[0:NC_, h // 16, (h % 16) * NF_:(h % 16 + 1) * NF_], lft[:, h, :], rgt[:, h, :],
                              start=True, stop=True)
            mm.then_inc(kernel_mm, 1)

        @block.vector
        def _(v):
            done = [0]

            def then(ins):
                done[0] += 1
                ins.then_inc(chain, 1)
                v.wait_ge(chain, done[0])

            def mul(out, a, b):
                then(v.tensor_tensor(out, a, b, ALU.mult))

            def add(out, a, b, op=ALU.add):
                then(v.tensor_tensor(out, a, b, op))

            v.wait_ge(cond_in, 32)
            v.wait_ge(cst_in, 16)
            then(v.tensor_copy(condf[:], condi[:]))
            v.tensor_scalar(onehot[:], condf[:], cst[0:NST, C_PIDX:C_PIDX + 1], None, ALU.is_equal).then_inc(hot, 1)
            ea, dt = eab[:, 0, :], eab[:, 1, :]
            x, y = xy[:, 0, :], xy[:, 1, :]
            v.wait_ge(ssm_in, 160)
            logs = par[:, 0:2, :]
            then(v.tensor_scalar(ek[:], logs, 1.0 / math.log(2.0), MAGIC, ALU.mult, ALU.add))
            then(v.tensor_scalar(ek[:], ek[:], -MAGIC, -126.0, ALU.add, ALU.max))
            then(v.tensor_scalar(ek[:], ek[:], 127.0, None, ALU.min))
            then(v.scalar_tensor_tensor(er_[:], ek[:], -LN2_HEAD, logs, ALU.mult, ALU.add))
            then(v.scalar_tensor_tensor(er_[:], ek[:], -LN2_TAIL, er_[:], ALU.mult, ALU.add))
            then(v.tensor_scalar(ek[:], ek[:], 127.0, None, ALU.add))
            then(v.tensor_copy(ei_[:], ek[:]))
            then(v.tensor_scalar(ei_[:], ei_[:], 23, None, ALU.logical_shift_left))
            then(v.tensor_scalar(eab[:], er_[:], 1.0 / math.factorial(8), None, ALU.mult))
            for order in range(7, 0, -1):
                then(v.scalar_tensor_tensor(eab[:], eab[:], 1.0 / math.factorial(order), er_[:], ALU.add, ALU.mult))
            then(v.scalar_tensor_tensor(eab[:], eab[:], 1.0, ei_[:].bitcast(F32), ALU.add, ALU.mult))
            mul(x, ea, dt)
            then(v.tensor_scalar(x, x, -1.0, None, ALU.mult))
            v.tensor_tensor(y, par[:, 2, :], dt, ALU.mult).then_inc(xy_ready, 1)
            v.wait_ge(xy_ready, 1)
            v.tensor_tensor(mag[:], x.unsqueeze(2).to_broadcast([P, SEQ, NC_ + NF_]),
                            cst[:, C_LAG + NC_:C_LAG + NC_ + NC_ + NF_].unsqueeze(1).to_broadcast([P, SEQ, NC_ + NF_]),
                            ALU.mult).then_inc(mag_ready, 1)
            mul(ang[:], y.unsqueeze(2).to_broadcast([P, SEQ, NANG]),
                cst[:, C_LAG:C_LAG + NANG].unsqueeze(1).to_broadcast([P, SEQ, NANG]))
            for s in range(NSEC):
                a, b = SECO[s], SECO[s] + SECW[s]
                then(v.tensor_scalar(turn[:, :, a:b], ang[:, :, a:b], 1.0 / TWO_PI,
                                     cst[:, C_PHASE + s:C_PHASE + s + 1], ALU.mult, ALU.add))
            then(v.tensor_scalar(turn[:], turn[:], MAGIC, None, ALU.add))
            then(v.tensor_scalar(turn[:], turn[:], -MAGIC, None, ALU.add))
            for part in (PI_HEAD, PI_MID, PI_TAIL):
                then(v.scalar_tensor_tensor(ang[:], turn[:], -part, ang[:], ALU.mult, ALU.add))
            for s in range(NSEC):
                a, b = SECO[s], SECO[s] + SECW[s]
                then(v.tensor_scalar(ang[:, :, a:b], ang[:, :, a:b],
                                     cst[:, C_PHASE + NSEC + s:C_PHASE + NSEC + s + 1], None, ALU.add))
            then(v.tensor_scalar(turn[:], ang[:], 1.0 / TWO_PI, MAGIC, ALU.mult, ALU.add))
            then(v.tensor_scalar(turn[:], turn[:], -MAGIC, None, ALU.add))
            then(v.scalar_tensor_tensor(ang[:], turn[:], -TWO_PI, ang[:], ALU.mult, ALU.add))
            then(v.tensor_scalar(ang[:], ang[:], 3.1415925, None, ALU.min))
            v.tensor_scalar(ang[:], ang[:], -3.1415925, None, ALU.max).then_inc(ang_ready, 1)
            v.wait_ge(wkr_in, 16)
            for m in range(KB):
                if m >= 2:
                    v.wait_ge(wkv_out[m % 2], 16)
                v.tensor_copy(wkv[:, m % 2, :, 0:HD].rearrange("p h (a r) -> p h a r", a=2)[:, :, :, 0:32],
                              wkr[:, m, :].rearrange("p (h a r) -> p h a r", h=KVH, a=2)).then_inc(roped, 1)
            em, e0, s2, er, ei, ar2, inv, mr, mi, cr, ci, t0, t1 = [tmp[:, i, :] for i in range(13)]
            v.wait_ge(mags, 2)
            then(v.tensor_scalar(e0, tnh[:], -1.0, 1.0, ALU.mult, ALU.add))
            then(v.reciprocal(em, e0))
            then(v.scalar_tensor_tensor(em, em, 2.0, tnh[:], ALU.mult, ALU.mult))
            v.wait_ge(sines, 1)
            sh, chf = sn[:, :, SECO[3]], sn[:, :, SECO[4]]
            mul(s2, sh, sh)
            then(v.tensor_scalar(s2, s2, 2.0, None, ALU.mult))
            then(v.tensor_scalar(t0, s2, -1.0, 1.0, ALU.mult, ALU.add))
            mul(er, em, t0)
            add(er, er, s2, ALU.subtract)
            mul(t1, sh, chf)
            then(v.tensor_scalar(e0, em, 1.0, 2.0, ALU.add, ALU.mult))
            mul(ei, e0, t1)
            ai = par[:, 2, :]
            mul(ar2, ea, ea)
            mul(t0, ai, ai)
            add(ar2, ar2, t0)
            then(v.reciprocal(inv, ar2))
            mul(t0, er, ea)
            mul(t1, ei, ai)
            add(mr, t1, t0, ALU.subtract)
            mul(mr, mr, inv)
            mul(t0, ei, ea)
            mul(t1, er, ai)
            add(mi, t0, t1)
            then(v.scalar_tensor_tensor(mi, mi, -1.0, inv, ALU.mult, ALU.mult))
            mul(t0, par[:, 3, :], mr)
            mul(t1, par[:, 4, :], mi)
            add(cr, t0, t1, ALU.subtract)
            then(v.tensor_scalar(cr, cr, 2.0, None, ALU.mult))
            mul(t0, par[:, 3, :], mi)
            mul(t1, par[:, 4, :], mr)
            add(ci, t0, t1)
            then(v.tensor_scalar(ci, ci, 2.0, None, ALU.mult))
            mul(lft[:], sn[:, :, 0:NC_], cr.unsqueeze(2).to_broadcast([P, SEQ, NC_]))
            mul(lf2[:], sn[:, :, NC_:2 * NC_], ci.unsqueeze(2).to_broadcast([P, SEQ, NC_]))
            add(lft[:], lft[:], lf2[:], ALU.subtract)
            v.tensor_tensor(lft[:], lft[:], mag[:, :, 0:NC_], ALU.mult).then_inc(factors, 1)
            v.tensor_tensor(rgt[:], sn[:, :, 2 * NC_:2 * NC_ + NF_], mag[:, :, NC_:NC_ + NF_],
                            ALU.mult).then_inc(factors, 1)
            v.wait_ge(kernel_mm, 1)
            for j in range(2):
                v.tensor_copy(kern[:, 16 * j:16 * j + 16, :], pk[0:NC_, j, :].rearrange("p (h c) -> p h c", h=16))\
                 .then_inc(kern_ready, 1)
            v.wait_ge(kern_ready, 2)
            v.tensor_tensor(kern[0:1, :, 0], kern[0:1, :, 0], dskip[:], ALU.add).then_inc(kern_ready, 1)


def attention(nc, io, scratch):
    with ExitStack() as ctx:
        def sb(name, shape, dt=F32):
            return ctx.enter_context(nc.sbuf_tensor(name, shape, dt))

        def sem(name):
            return ctx.enter_context(nc.semaphore(name))

        cst = sb("b_cst", [P, C_W])
        h_hi, h_lo = sb("h_hi", [P, KB, QTOK], F32R), sb("h_lo", [P, KB, QTOK], F32R)
        acc = sb("b_acc", [P, KB, QTOK])
        wq_hi, wq_lo = (sb(f"wq_{x}", [P, 2, KB, GRP * HD], F32R) for x in ("hi", "lo"))
        wkv_hi, wkv_lo = (sb(f"wkv_{x}", [P, 2, KB, 2 * HD], F32R) for x in ("hi", "lo"))
        wo_hi, wo_lo = (sb(f"wo_{x}", [P, GRP, DM], F32R) for x in ("hi", "lo"))
        stage = sb("b_stage", [P, 2, 2, 512])
        work = sb("b_work", [P, GRP * CH + 5 * CH])
        qT = work[:, 0:GRP * CH].rearrange("p (g t) -> p g t", g=GRP)
        swapped = work[:, GRP * CH:GRP * CH + 5 * CH].rearrange("p (i t) -> p i t", i=5)
        xt = sb("b_xt", [P, QTOK // P, DM])
        kT = sb("b_kT", [P, CH])
        vT = sb("b_vT", [P, CH])
        v_sb = sb("b_v", [P, TPC, HD])
        sc = sb("b_sc", [P, GRP * TPC, SEQ])
        pr = sb("b_pr", [P, GRP * TPC, SEQ])
        red = sb("b_red", [P, 2, GRP * TPC])
        rcp = sb("b_rcp", [P, GRP * TPC])
        diag = sb("b_diag", [P, TPC, 4, GRP * SEQ])
        o_hi, o_lo = sb("o_hi", [P, GRP, CH], F32R), sb("o_lo", [P, GRP, CH], F32R)
        bdc = sb("b_bdc", [P, QTOK // P, P])

        proj = [ctx.enter_context(nc.psum_tensor(f"proj{i}", [P, 512], F32)) for i in range(3)]
        ps = ctx.enter_context(nc.psum_tensor("scores", [P, 512], F32))
        ob = [ctx.enter_context(nc.psum_tensor(f"outs{i}", [P, 512], F32)) for i in range(4)]

        cst_in = sem("b_cst_in")
        x_in, bdc_in = sem("x_in"), sem("bdc_in")
        acc_in = [sem("acc_in0"), sem("acc_in1")]
        acc_out = [sem("acc_out0"), sem("acc_out1")]
        stage_in = [sem("stage_in0"), sem("stage_in1")]
        w_hi_done, w_lo_done = sem("w_hi_done"), sem("w_lo_done")
        cleared = sem("b_cleared")
        h_mm, h_hi_done, h_lo_done = sem("h_mm"), sem("h_hi_done"), sem("h_lo_done")
        proj_done = sem("proj_done")
        swap_done = sem("swap_done")
        cos_done = sem("cos_done")
        sin_done = sem("sin_done")
        rope_done = sem("rope_done")
        vT_done = sem("vT_done")
        v_mm = sem("v_mm")
        v_done = sem("v_done")
        scores_done = sem("scores_done")
        turned = sem("turned")
        smax = sem("smax")
        exp_done = sem("exp_done")
        diag_done = sem("diag_done")
        pv_done, o_hi_done, o_lo_done = sem("pv_done"), sem("o_hi_done"), sem("o_lo_done")
        wo_done, acc_done = sem("wo_done"), sem("acc_done")
        block = ctx.enter_context(nc.Block())

        Q0, Q1, Q2, KEYS, VALUES, Q3 = range(6)
        ROPED = (Q0, Q1, Q2, KEYS, Q3)

        ropes = {"q": (cst[:, C_ROPE:C_ROPE + SEQ], cst[:, C_ROPE + SEQ:C_ROPE + 2 * SEQ]),
                 "k": (cst[:, C_ROPE + 2 * SEQ:C_ROPE + 3 * SEQ], cst[:, C_ROPE + 3 * SEQ:C_ROPE + 4 * SEQ])}

        def head(i):
            return 3 if i == Q3 else i

        def target(i):
            return kT[:] if i == KEYS else qT[:, head(i), :]

        def by_position(ap):
            return ap.rearrange("p (b s) -> p b s", s=SEQ)

        def table(i, which):
            return ropes["k" if i == KEYS else "q"][which].unsqueeze(1).to_broadcast([P, BCH, SEQ])

        QA, QB, OA, OB, KV = range(5)
        FIRST_PIECES = ((0, QA, 0), (1, QB, 0), (2, KV, 0))

        def pieces(w, kinds, last=False):
            if last:
                return [(5 * w + 3 + kind - OA, kind, w) for kind in kinds if kind in (OA, OB)]
            return [(5 * w + 3 + kind, kind, 1 - w) for kind in kinds]

        def half(kind, part, w, j):
            if kind == KV:
                return (wkv_hi, wkv_lo)[part][:, w, 2 * j:2 * j + 2, :].rearrange("p k n -> p (k n)")
            if kind in (OA, OB):
                return (wo_hi, wo_lo)[part][:, 2 * (kind - OA) + j, :]
            return (wq_hi, wq_lo)[part][:, w, 2 * kind + j, :]

        def prev(n):
            return not isinstance(n, int) or n > 0

        def early(u, last):
            return pieces(u // 2 % 2, (OA, OB), last) if u % 2 else []

        def late(u, last):
            return pieces(u // 2 % 2, (KV,) if u % 2 else (QA, QB), last)

        def schedule(eng, mix, step, finish):
            def middle(q, last):
                with eng.Fori(0, 3) as j:
                    for u in range(1, 5):
                        step(u, q * UPQ + j * 4 + u, q * 4 + j + u // 4, q, False)
                for u in range(13, 16):
                    step(u, q * UPQ + u, q * 4 + 3, q, last and u >= 14)

            mix(0)
            step(0, 0, 0, 0, False)
            with eng.Fori(0, NQ - 1) as q:
                middle(q, False)
                step(0, q * UPQ + UPQ, q * 4 + 4, q + 1, False)
            middle(NQ - 1, True)
            finish(NQ * UPQ)

        def mixes(u, last):
            return u == UPQ - 1 and not last

        MIX_TILES = ((0, 1, 2), (3, 4, 5), (6, 7), ())

        @block.sync
        def _(sp):
            sp.dma_start(cst[:], io["consts"]).then_inc(cst_in, 16)
            sp.wait_ge(w_lo_done, 3)

            def load_tokens(q):
                for half_ in range(2):
                    sp.dma_start(xt[:, 4 * half_:4 * half_ + 4, :],
                                 io["x_tok"][bass.ds(q * QTOK + half_ * 512, 512), :]
                                 .rearrange("(t p) f -> p t f", p=P)).then_inc(x_in, 16)
                for b in range(4):
                    sp.dma_start(bdc[32 * b:32 * b + 32, :, 32 * b:32 * b + 32],
                                 scratch["wg"].rearrange("(t b) (c d) -> b c t d", b=4, c=SEQ)
                                 [b, :, bass.ds(q * (QTOK // P), QTOK // P), :]).then_inc(bdc_in, 16)

            def load_sums(c, start):
                sp.dma_start(acc[:, :, c * CH:(c + 1) * CH],
                             io["xT"].rearrange("(o p) t -> p o t", p=P)[:, :, bass.ds(start, CH)])\
                  .then_inc(acc_in[c], 16)

            def store_sums(q, c):
                sp.wait_ge(acc_done, q * (4 * UPQ) + 4 * (UPQ + c))
                sp.wait_ge(cst_in, 16)
                sp.dma_start(scratch["x2T"].rearrange("(o p) t -> p o t", p=P)[:, :, bass.ds(q * QTOK + c * CH, CH)],
                             acc[:, :, c * CH:(c + 1) * CH]).then_inc(acc_out[c], 16)

            def load_piece(pair, place, kind, own, following):
                sp.wait_ge(w_lo_done, pair * 20 + (2 * place + 1))
                sp.wait_ge(cst_in, 16)
                dst = stage[:, place % 2, :, :]
                if kind in (QA, QB):
                    src = io["wqT"].rearrange("(k p) (m n) -> p k m n", p=P, n=GRP * HD)[
                        :, 2 * kind:2 * kind + 2, bass.ds(following, 1), :]
                    dst = dst.unsqueeze(2)
                elif kind == KV:
                    src = scratch["wkv"].rearrange("k p h n -> p k h n")[:, :, bass.ds(following, 1), :]
                    dst = dst.rearrange("p a (k n) -> p (a k) n", k=2).unsqueeze(2)
                else:
                    g = 2 * (kind - OA)
                    src = io["woT"].rearrange("(h g p) o -> p h g o", p=P, g=GRP)[:, bass.ds(own, 1), g:g + 2, :]
                    dst = dst.unsqueeze(1)
                sp.dma_start(dst, src).then_inc(stage_in[place % 2], 16)

            def load_pair(pair, in_quarter, after, last, q=None):
                for w in range(2):
                    own = in_quarter * 2 + w
                    following = after if w else in_quarter * 2 + 1
                    if q is not None and w == 0:
                        store_sums(q, 0)
                    final = last and w == 1
                    for place, kind, _ in pieces(w, (QA, QB), final):
                        load_piece(pair, place, kind, own, following)
                    if q is not None and w == 0:
                        next_sums(q, 0)
                        store_sums(q, 1)
                        next_sums(q, 1)
                    for place, kind, _ in pieces(w, (OA, OB, KV), final):
                        load_piece(pair, place, kind, own, following)

            def next_sums(q, c):
                sp.wait_ge(acc_out[c], q * 16 + 16)
                sp.wait_ge(cst_in, 16)
                load_sums(c, q * QTOK + (QTOK + c * CH))

            load_tokens(0)
            for place, kind, _ in FIRST_PIECES[:2]:
                load_piece(0, place, kind, 0, 0)
            for c in range(2):
                load_sums(c, c * CH)
            load_piece(0, *FIRST_PIECES[2][:2], 0, 0)
            load_pair(0, 0, 2, False)
            with sp.Fori(0, NQ - 1) as q:
                with sp.Fori(1, 3) as p:
                    load_pair(q * 4 + p, p, p * 2 + 2, False)
                sp.wait_ge(h_mm, q * (QTOK // P) + QTOK // P)
                sp.wait_ge(cst_in, 16)
                load_tokens(q + 1)
                load_pair(q * 4 + 3, 3, 0, False)
                load_pair(q * 4 + 4, 0, 2, False, q)
            with sp.Fori(1, 3) as p:
                load_pair((NQ - 1) * 4 + p, p, p * 2 + 2, False)
            load_pair(NQ * 4 - 1, 3, 0, True)
            for c in range(2):
                store_sums(NQ - 1, c)
            for c in range(2):
                sp.wait_ge(acc_out[c], NQ * 16)

        @block.gpsimd
        def _(pool):
            pool.memset(diag[:], 0.0).then_inc(w_lo_done, 1)
            pool.memset(bdc[:], 0.0).then_inc(w_lo_done, 1)
            pool.memset(stage[:], 0.0).then_inc(w_lo_done, 1)
            pool.wait_ge(cst_in, 16)

            def split(pair, listed):
                for place, kind, w in listed:
                    for j in range(2):
                        pool.wait_ge(w_hi_done, pair * 20 + (2 * place + j + 1))
                        pool.tensor_tensor(half(kind, 1, w, j), stage[:, place % 2, j, :],
                                           half(kind, 0, w, j).bitcast(F32), ALU.subtract).then_inc(w_lo_done, 1)

            def rotate(i, n):
                r = ROPED.index(i)
                pool.wait_ge(swap_done, n * 5 + (r + 1))
                s = by_position(swapped[:, r, :])
                pool.tensor_tensor(s, s, table(i, 1), ALU.mult).then_inc(sin_done, 1)
                pool.wait_ge(sin_done, n * 5 + (r + 1))
                pool.wait_ge(cos_done, n * 5 + (r + 1))
                pool.tensor_tensor(target(i), target(i), swapped[:, r, :], ALU.add).then_inc(rope_done, 1)

            def step(u, n, pair, q, last):
                for i in (Q0, Q1):
                    rotate(i, n)
                split(pair, early(u, last))
                for i in (Q2, KEYS, Q3):
                    rotate(i, n)
                split(pair, late(u, last))

            def mix(q):
                split(0, FIRST_PIECES)

            schedule(pool, mix, step, lambda n: None)

        @block.scalar
        def _(act):
            act.wait_ge(cst_in, 16)

            def split(pair, listed, n):
                for place, kind, w in listed:
                    act.wait_ge(stage_in[place % 2], pair * 80 + 16 * (place // 2 + 1))
                    if kind == OA:
                        act.wait_ge(acc_done, n * 4)
                    for j in range(2):
                        act.activation(half(kind, 0, w, j), stage[:, place % 2, j, :], ACT.Copy)\
                           .then_inc(w_hi_done, 1)

            def swap(i, n):
                act.wait_ge(proj_done, n * 6 + (i + 1))
                r = ROPED.index(i)
                act.activation(swapped[0:64, r, :], proj[i % 3][64:128, :], ACT.Copy)
                act.activation(swapped[64:128, r, :], proj[i % 3][0:64, :], ACT.Copy).then_inc(swap_done, 1)

            def exps(n):
                act.wait_ge(smax, n * 6 - 3)
                act.activation(pr[:], sc[:], ACT.Exp, scale=SCALE).then_inc(exp_done, 1)

            def out_hi(n):
                for t in range(TPC):
                    act.wait_ge(pv_done, n * 4 + (t - 3))
                    act.activation(o_hi[:, :, t * P:(t + 1) * P].rearrange("p g (b s) -> p b g s", b=4),
                                   ob[t][:].rearrange("p (b g s) -> p b g s", b=4, g=GRP), ACT.Copy)\
                       .then_inc(o_hi_done, 1)

            def h_hi_tile(t, q):
                act.wait_ge(h_mm, q * (QTOK // P) + (t + 1))
                act.activation(h_hi[:, :, t * P:(t + 1) * P], proj[t % 3][:].rearrange("p (k t) -> p k t", k=KB),
                               ACT.Copy).then_inc(h_hi_done, 1)

            def step(u, n, pair, q, last):
                swap(Q0, n)
                if prev(n):
                    exps(n)
                swap(Q1, n)
                split(pair, early(u, last), n)
                for i in (Q2, KEYS):
                    swap(i, n)
                act.wait_ge(proj_done, n * 6 + (VALUES + 1))
                act.activation(vT[:], proj[VALUES % 3][:], ACT.Copy).then_inc(vT_done, 1)
                if prev(n):
                    out_hi(n)
                swap(Q3, n)
                if mixes(u, last):
                    for t in range(QTOK // P):
                        h_hi_tile(t, q + 1)
                act.wait_ge(v_mm, n + 1)
                act.activation(v_sb[:], ps[:].rearrange("p (t d) -> p t d", t=TPC), ACT.Copy).then_inc(v_done, 1)
                split(pair, late(u, last), n)

            def mix(q):
                for t in range(QTOK // P):
                    h_hi_tile(t, q)
                split(0, FIRST_PIECES, 0)

            def finish(n):
                exps(n)
                out_hi(n)

            schedule(act, mix, step, finish)

        @block.vector
        def _(v):
            for i in range(KB):
                v.memset(red[:, 0, i:i + 1], 0.0).then_inc(acc_done, 1)
            v.wait_ge(cst_in, 16)
            mask = cst[:, C_MASK:C_MASK + SEQ].unsqueeze(1).to_broadcast([P, GRP * TPC, SEQ])

            def per_row(ap):
                return ap.unsqueeze(2).to_broadcast([P, GRP * TPC, SEQ])

            def softmax_front(n):
                v.wait_ge(scores_done, n)
                v.transpose(sc[:].rearrange("p a k -> p (a k)"), ps[:]).then_inc(turned, 1)
                v.wait_ge(turned, n)
                v.tensor_tensor(sc[:], sc[:], mask, ALU.add).then_inc(smax, 1)
                v.wait_ge(smax, n * 6 - 5)
                v.tensor_reduce(red[:, 0, :], sc[:], AX.X, ALU.max).then_inc(smax, 1)
                v.wait_ge(smax, n * 6 - 4)
                v.tensor_tensor(sc[:], sc[:], per_row(red[:, 0, :]), ALU.subtract).then_inc(smax, 1)

            def softmax_back(n):
                v.wait_ge(exp_done, n)
                v.tensor_reduce(red[:, 1, :], pr[:], AX.X, ALU.add).then_inc(smax, 1)
                v.wait_ge(smax, n * 6 - 2)
                v.reciprocal(rcp[:], red[:, 1, :]).then_inc(smax, 1)
                v.wait_ge(smax, n * 6 - 1)
                v.tensor_tensor(pr[:], pr[:], per_row(rcp[:]), ALU.mult).then_inc(smax, 1)
                v.wait_ge(smax, n * 6)
                for b in range(4):
                    ins = v.transpose(diag[32 * b:32 * b + 32, :, b, :],
                                      pr[32 * b:32 * b + 32, :, :].rearrange("p (t g) k -> p t (g k)", t=TPC))
                ins.then_inc(diag_done, 1)

            def cosine(i, n):
                v.wait_ge(swap_done, n * 5 + (ROPED.index(i) + 1))
                v.tensor_tensor(by_position(target(i)), by_position(proj[i % 3][:]), table(i, 0), ALU.mult)\
                 .then_inc(cos_done, 1)

            def out_lo(n):
                for t in range(TPC):
                    v.wait_ge(o_hi_done, n * 4 + (t - 3))
                    def view(o):
                        return o[:, :, t * P:(t + 1) * P].rearrange("p g (b s) -> p b g s", b=4)
                    v.tensor_tensor(view(o_lo), ob[t][:].rearrange("p (b g s) -> p b g s", b=4, g=GRP),
                                    view(o_hi).bitcast(F32), ALU.subtract).then_inc(o_lo_done, 1)

            def h_lo_tile(t, q):
                v.wait_ge(h_hi_done, q * (QTOK // P) + (t + 1))
                h = slice(t * P, (t + 1) * P)
                v.tensor_tensor(h_lo[:, :, h], proj[t % 3][:].rearrange("p (k t) -> p k t", k=KB),
                                h_hi[:, :, h].bitcast(F32), ALU.subtract).then_inc(h_lo_done, 1)

            def accumulate(n, c, tiles=((),) * KB, q=None):
                for o in range(KB):
                    v.wait_ge(wo_done, n * 4 + (o - 3))
                    a = acc[:, o, c * CH:(c + 1) * CH]
                    v.tensor_tensor(a, a, ob[o][:], ALU.add).then_inc(acc_done, 1)
                    for t in tiles[o]:
                        h_lo_tile(t, q)

            def step(u, n, pair, q, last):
                if prev(n):
                    softmax_front(n)
                cosine(Q0, n)
                if prev(n):
                    softmax_back(n)
                for i in (Q1, Q2, KEYS):
                    cosine(i, n)
                if prev(n):
                    out_lo(n)
                cosine(Q3, n)
                if mixes(u, last):
                    accumulate(n, (u - 1) % 2, MIX_TILES, q + 1)
                elif prev(n):
                    if u in (1, 2):
                        v.wait_ge(acc_in[(u - 1) % 2], q * 16 + 16)
                    accumulate(n, (u - 1) % 2)

            def mix(q):
                for t in range(QTOK // P):
                    h_lo_tile(t, q)

            def finish(n):
                softmax_front(n)
                softmax_back(n)
                out_lo(n)
                accumulate(n, 1)

            schedule(v, mix, step, finish)

        @block.tensor
        def _(t_):
            def product(out, left, right, blocks):
                for k in range(blocks):
                    (l_hi, l_lo), (r_hi, r_lo) = left(k), right(k)
                    t_.matmul(out, l_hi, r_hi, start=k == 0, stop=False)
                    t_.matmul(out, l_hi, r_lo, start=False, stop=False)
                    mm = t_.matmul(out, l_lo, r_hi, start=False, stop=k == blocks - 1)
                return mm

            def item(i, u, n):
                w, c = (u // 2) % 2, u % 2
                if i >= KEYS:
                    t_.wait_ge(cos_done, n * 5 + (i - KEYS + 1))
                elif prev(n) and i == Q0:
                    t_.wait_ge(cos_done, n * 5 - 1)
                elif prev(n) and i == Q1:
                    t_.wait_ge(vT_done, n)
                elif prev(n):
                    t_.wait_ge(cos_done, n * 5)
                tok = slice(c * CH, (c + 1) * CH)
                wh, wl = (wkv_hi, wkv_lo) if i in (KEYS, VALUES) else (wq_hi, wq_lo)
                m = {KEYS: 0, VALUES: 1}.get(i, head(i))
                cols = slice(m * HD, (m + 1) * HD)
                product(proj[i % 3][:], lambda k: (wh[:, w, k, cols], wl[:, w, k, cols]),
                        lambda k: (h_hi[:, k, tok], h_lo[:, k, tok]), KB).then_inc(proj_done, 1)

            def turn_values(n):
                t_.wait_ge(vT_done, n + 1)
                if prev(n):
                    t_.wait_ge(turned, n)
                for t in range(TPC):
                    mm = t_.transpose(ps[:, t * HD:(t + 1) * HD], vT[:, t * P:(t + 1) * P], cst[:, C_ID:C_ID + P])
                mm.then_inc(v_mm, 1)

            def values(n):
                t_.wait_ge(diag_done, n)
                t_.wait_ge(v_done, n)
                for t in range(TPC):
                    t_.wait_ge(acc_done, n * 4 + (t - 3))
                    t_.matmul(ob[t][:], v_sb[:, t, :], diag[:, t, :, :].rearrange("p b s -> p (b s)"),
                              start=True, stop=True).then_inc(pv_done, 1)

            def output(n, o):
                cols = slice(o * P, (o + 1) * P)
                product(ob[o][:],
                        lambda g: (wo_hi[:, g, cols], wo_lo[:, g, cols]),
                        lambda g: (o_hi[:, g, :], o_lo[:, g, :]), GRP).then_inc(wo_done, 1)

            def mix_tile(t, q):
                if t >= 3:
                    t_.wait_ge(h_lo_done, q * (QTOK // P) + (t - 2))
                for k in range(KB):
                    mm = t_.matmul(proj[t % 3][:, k * P:(k + 1) * P], xt[:, t, k * P:(k + 1) * P], bdc[:, t, :],
                                   start=True, stop=True)
                mm.then_inc(h_mm, 1)

            def mix_inputs(q):
                t_.wait_ge(bdc_in, q * 64 + 64)
                t_.wait_ge(x_in, q * 32 + 32)

            def scores(n):
                t_.wait_ge(rope_done, n * 5 + 5)
                t_.wait_ge(v_done, n + 1)
                for b in range(BCH):
                    s = slice(b * SEQ, (b + 1) * SEQ)
                    r = 32 * (b % 4)
                    mm = t_.matmul(ps[r:r + 32, (b // 4) * P:(b // 4 + 1) * P].rearrange("p (g s) -> p g s", g=GRP),
                                   kT[:, s], qT[:, :, s], start=True, stop=True)
                mm.then_inc(scores_done, 1)

            def step(u, n, pair, q, last):
                if u % 2 == 0:
                    t_.wait_ge(w_lo_done, n * 5 + 9)
                for i in (Q0, Q1, Q2, KEYS, VALUES):
                    item(i, u, n)
                if prev(n):
                    values(n)
                item(Q3, u, n)
                if prev(n):
                    t_.wait_ge(o_lo_done, n * 4)
                    if u % 2:
                        t_.wait_ge(w_lo_done, n * 5 + (8 if last else 12))
                if mixes(u, last):
                    mix_inputs(q + 1)
                    t_.wait_ge(cos_done, n * 5 + 5)
                    t_.wait_ge(vT_done, n + 1)
                for o in range(KB - 1):
                    if prev(n):
                        output(n, o)
                    if mixes(u, last):
                        for t in MIX_TILES[o]:
                            mix_tile(t, q + 1)
                turn_values(n)
                if prev(n):
                    output(n, KB - 1)
                scores(n)
                if mixes(u, last):
                    t_.wait_ge(h_lo_done, q * (QTOK // P) + 2 * (QTOK // P))

            def mix(q):
                mix_inputs(q)
                for t in range(QTOK // P):
                    mix_tile(t, q)
                t_.wait_ge(h_lo_done, QTOK // P)

            def finish(n):
                values(n)
                t_.wait_ge(o_lo_done, n * 4)
                for o in range(KB):
                    output(n, o)

            schedule(t_, mix, step, finish)


def ssm_and_ffn(nc, io, scratch, out):
    NCH = TOK // CH
    ANCH = TOK // 2
    NT = ANCH // P
    EARLY = 2
    HU = 4
    with ExitStack() as ctx:
        def sb(name, shape, dt=F32):
            return ctx.enter_context(nc.sbuf_tensor(name, shape, dt))

        def sem(name):
            return ctx.enter_context(nc.semaphore(name))

        cst = sb("c_cst", [P, C_W])
        x2 = sb("c_x2", [P, KB, TOK])
        yT = sb("c_y", [P, KB, TOK])
        toep = sb("c_toep", [P, HU, DM])
        lens_i = sb("c_lens_i", [P, BATCH], I32)
        lens = sb("c_lens", [P, BATCH])
        keep = sb("c_keep", [P, KB, BATCH])
        wT = sb("c_wT", [P, KB, DM])
        wza = sb("c_wza", [P, KB, RANK + NE])
        bmat = sb("c_bmat", [3 * RANK, DM])
        b_split = sb("c_b_split", [3 * RANK, DM], F32R)
        b_hi = sb("c_b_hi", [2 * RANK, DM], F32R)
        z_split = sb("c_z_split", [3 * RANK, TOK], F32R)
        limes = sb("c_limes", [NE, RANK])
        pick = sb("c_pick", [RANK + NE, 2 * NE])
        bias = sb("c_bias", [P, KB])
        bias8 = sb("c_bias8", [RANK + NE, 1])
        zh = sb("c_zh", [RANK + NE, TOK])
        gate = sb("c_gate", [P, NT, 2 * NE])
        g0, g1, g2 = (sb(f"c_g{i}", [P, NT, NE]) for i in range(3))
        top = sb("c_top", [P, NT, 8])
        row = sb("c_row", [P, 2, NT])
        big = sb("c_big", [P, 4, 2])
        wgt = sb("c_wgt", [NE, ANCH])
        fin = sb("c_fin", [P, 4, CH])
        bank = [ctx.enter_context(nc.psum_tensor(f"c_ps{i}", [P, 512], F32)) for i in range(8)]

        cst_in, x2_in, par_in, len_in = sem("c_cst_in"), sem("c_x2_in"), sem("c_par_in"), sem("c_len_in")
        toep_in = [sem(f"toep_in{i}") for i in range(HU)]
        conv_done, y_done = sem("conv_done"), sem("y_done")
        keep_done = sem("keep_done")
        zh_mm, zh_done = sem("zh_mm"), sem("zh_done")
        pick_clear, pick_in = sem("pick_clear"), sem("pick_in")
        gate_mm, gate_done = sem("gate_mm"), sem("gate_done")
        peak_local, peak_all = sem("peak_local"), sem("peak_all")
        g_exp_in, g_exp = sem("g_exp_in"), sem("g_exp")
        chain = sem("c_chain")
        w_ready, w_turned, w_copied = sem("w_ready"), sem("w_turned"), sem("w_copied")
        b_done, z_hi_done = sem("b_done"), sem("z_hi_done")
        z_dup_done, z_lo_done = sem("z_dup_done"), sem("z_lo_done")
        mix_mm, mix_done = sem("mix_mm"), sem("mix_done")
        base_mm, base_done = sem("base_mm"), sem("base_done")
        delta_mm, fin_done = sem("delta_mm"), sem("fin_done")
        out_done = [sem(f"out_done{i}") for i in range(4)]
        block = ctx.enter_context(nc.Block())

        kp = scratch["kpad"]

        def at_position(ap, s):
            return ap.rearrange("p o (b s) -> p o b s", s=SEQ)[:, :, :, bass.ds(s, 1)]

        @block.sync
        def _(sp):
            sp.dma_start(cst[:], io["consts"]).then_inc(cst_in, 16)
            sp.dma_start(lens_i[:], io["length"].partition_broadcast(P)).then_inc(len_in, 16)
            for o in range(KB):
                sp.dma_start(x2[:, o, :], scratch["x2T"][o * P:(o + 1) * P, :]).then_inc(x2_in, 16)

            def load_toeplitz(s, i):
                base = kp[bass.ds(s, 1), 0:DM]
                src = bass.AP(tensor=base.tensor, offset=base.offset, ap=[[1, P], [1, DM]])
                sp.dma_start(toep[:, i, :], src).then_inc(toep_in[i], 16)

            for i in range(HU):
                load_toeplitz(i, i)
            with sp.Fori(0, SEQ // HU - 1) as g:
                for i in range(HU):
                    sp.wait_ge(conv_done, g * HU + (i + 1))
                    sp.wait_ge(cst_in, 16)
                    load_toeplitz(g * HU + (HU + i), i)
            sp.dma_start(wT[:], io["wT"].rearrange("(k p) n -> p k n", p=P)).then_inc(par_in, 16)
            sp.dma_start(wza[:], io["wza"].rearrange("(k p) n -> p k n", p=P)).then_inc(par_in, 16)
            for i in range(3):
                sp.dma_start(bmat[i * RANK:(i + 1) * RANK, :], io["bmat"]).then_inc(par_in, 16)
            sp.dma_start(limes[:], io["limes"]).then_inc(par_in, 16)
            sp.dma_start(bias[:], io["bias"]).then_inc(par_in, 16)
            sp.dma_start(bias8[RANK:, :], io["bias8"].rearrange("(p a) -> p a", a=1)).then_inc(par_in, 16)
            sp.wait_ge(pick_clear, 1)
            sp.dma_start(pick[0:RANK, 0:NE], io["limesT"]).then_inc(pick_in, 16)
            sp.dma_start(pick[RANK:, NE:], io["consts"][0:NE, C_ID:C_ID + NE]).then_inc(pick_in, 16)
            with sp.Fori(0, NCH) as c:
                for o in range(KB):
                    sp.wait_ge(fin_done, c * KB + (KB + o + 1))
                    sp.wait_ge(cst_in, 16)
                    sp.dma_start(out[o * P:(o + 1) * P, bass.ds(c * CH, CH)], fin[:, o, :])\
                      .then_inc(out_done[o], 16)
            for o in range(KB):
                sp.wait_ge(out_done[o], NCH * 16)

        @block.gpsimd
        def _(pool):
            pool.memset(pick[:], 0.0).then_inc(pick_clear, 1)
            pool.wait_ge(peak_local, 1)
            pool.partition_all_reduce(big[:, 1, :], big[:, 0, :], P, bass.bass_isa.ReduceOp.max)\
                .then_inc(peak_all, 1)

        @block.tensor
        def _(t_):
            t_.wait_ge(x2_in, KB * 16)
            with t_.Fori(0, SEQ // HU) as g:
                for i in range(HU):
                    t_.wait_ge(toep_in[i], g * 16 + 16)
                    t_.wait_ge(y_done, g * HU + (i + 1))
                    for d in range(KB):
                        mm = t_.matmul(bank[i][:, d * P:].rearrange("p (o b) -> p o b", b=P),
                                       toep[:, i, d * P:(d + 1) * P],
                                       at_position(x2[:, 0:KB - d, :], g * HU + i),
                                       start=d == 0, stop=d == KB - 1)
                    mm.then_inc(conv_done, 1)
            t_.wait_ge(y_done, HU + SEQ)
            t_.wait_ge(par_in, 8 * 16)
            def low_rank(c, first):
                for i in range(2):
                    if not first:
                        t_.wait_ge(zh_done, c * 4 + (2 * i - 2))
                    for k in range(KB):
                        mm = t_.matmul(bank[4 + i][0:RANK + NE, :], wza[:, k, :], yT[:, k, bass.ds(c * (2 * CH) + i * CH, CH)],
                                       start=k == 0, stop=k == KB - 1)
                    mm.then_inc(zh_mm, 1)

            low_rank(0, True)
            with t_.Fori(1, NCH // 2) as c:
                low_rank(c, False)
            t_.wait_ge(zh_done, 2 * NCH)
            t_.wait_ge(pick_in, 32)
            for i in range(NT):
                mm = t_.matmul(bank[6][:, i * 2 * NE:(i + 1) * 2 * NE],
                               zh[0:RANK + NE, 2 * P * i:2 * P * (i + 1)].rearrange("p (a s) -> p a s", s=2)[:, :, 1],
                               pick[:], start=True, stop=True)
            mm.then_inc(gate_mm, 1)

            def base(c):
                for o in range(KB):
                    t_.wait_ge(base_done, c * KB + (o + 1))
                    for k in range(KB):
                        mm = t_.matmul(bank[o][:], wT[:, k, o * P:(o + 1) * P], yT[:, k, bass.ds(c * CH, CH)],
                                       start=k == 0, stop=k == KB - 1)
                    mm.then_inc(base_mm, 1)

            with t_.Fori(0, EARLY) as c:
                base(c)
            t_.wait_ge(w_ready, 1)
            for i in range(4):
                if i >= 2:
                    t_.wait_ge(w_copied, i - 1)
                for j in range(4):
                    mm = t_.transpose(bank[6 + i % 2][0:NE, j * P:(j + 1) * P], g0[:, 4 * i + j, :], cst[:, C_ID:C_ID + P])
                mm.then_inc(w_turned, 1)
            for i in range(4):
                t_.wait_ge(w_copied, i + 1)
                if i >= 2:
                    t_.wait_ge(mix_done, i - 1)
                t_.matmul(bank[4 + i % 2][0:RANK, :], limes[:], wgt[:, i * 512:(i + 1) * 512],
                          start=True, stop=True).then_inc(mix_mm, 1)
            with t_.Fori(EARLY, NCH) as c:
                base(c)
            t_.wait_ge(b_done, 1)
            t_.wait_ge(z_dup_done, 4)
            t_.wait_ge(z_lo_done, 4)
            t_.wait_ge(base_done, KB + NCH * KB)
            with t_.Fori(0, NCH) as c:
                for o in range(KB):
                    t_.wait_ge(fin_done, c * KB + (o + 1))
                    t_.matmul(bank[o][:], b_split[:, o * P:(o + 1) * P], z_split[:, bass.ds(c * CH, CH)],
                              start=True, stop=True).then_inc(delta_mm, 1)

        @block.scalar
        def _(act):
            act.wait_ge(par_in, 8 * 16)
            with act.Fori(0, NCH // 2) as c:
                for i in range(2):
                    act.wait_ge(zh_mm, c * 2 + (i + 1))
                    cols = bass.ds(c * (2 * CH) + i * CH, CH)
                    act.activation(zh[0:RANK, cols], bank[4 + i][0:RANK, :], ACT.Copy).then_inc(zh_done, 1)
                    act.activation(zh[RANK:RANK + NE, cols], bank[4 + i][RANK:RANK + NE, :], ACT.Identity, bias=bias8[RANK:, :])\
                       .then_inc(zh_done, 1)
            act.wait_ge(g_exp_in, 1)
            act.activation(g1[:], g0[:], ACT.Exp).then_inc(g_exp, 1)
            act.wait_ge(g_exp_in, 2)
            act.activation(g2[:], g1[:], ACT.Exp, scale=-2.0).then_inc(g_exp, 1)
            for i in range(4):
                cols = slice(i * 1024, (i + 1) * 1024)
                act.wait_ge(mix_done, i + 1)
                act.activation(z_split[0:RANK, cols], zh[0:RANK, cols], ACT.Copy).then_inc(z_hi_done, 1)
                act.activation(z_split[RANK:2 * RANK, cols], zh[0:RANK, cols], ACT.Copy).then_inc(z_dup_done, 1)

        @block.vector
        def _(v):
            done = [0]

            def then(ins):
                done[0] += 1
                ins.then_inc(chain, 1)
                v.wait_ge(chain, done[0])

            def per_token(ap):
                return ap.unsqueeze(2).to_broadcast([P, NT, NE])

            for o in range(KB):
                v.memset(fin[:, o, 0:1], 0.0).then_inc(base_done, 1)
                v.memset(fin[:, o, 1:2], 0.0).then_inc(fin_done, 1)
            v.wait_ge(len_in, 16)
            v.wait_ge(cst_in, 16)
            then(v.tensor_copy(lens[:], lens_i[:]))
            for o in range(KB):
                v.tensor_scalar(keep[:, o, :], lens[:], cst[:, C_PIDX + o:C_PIDX + o + 1], None, ALU.is_gt)\
                 .then_inc(y_done, 1)
            v.wait_ge(y_done, HU)
            with v.Fori(0, SEQ // HU) as g:
                for i in range(HU):
                    v.wait_ge(conv_done, g * HU + (i + 1))
                    v.tensor_tensor(at_position(yT[:], g * HU + i), bank[i][:].rearrange("p (o b) -> p o b", b=P).unsqueeze(3),
                                    keep[:].unsqueeze(3), ALU.mult).then_inc(y_done, 1)
            v.wait_ge(gate_mm, 1)
            then(v.tensor_copy(gate[:].rearrange("p t e -> p (t e)"), bank[6][:, 0:NT * 2 * NE]))
            v.tensor_reduce(big[:, 0, :], gate[:].rearrange("p t (s e) -> p s t e", s=2), AX.XY, ALU.max,
                            apply_absolute_value=True).then_inc(peak_local, 1)

            def base(c):
                for o in range(KB):
                    v.wait_ge(base_mm, c * KB + (o + 1))
                    xs = x2[:, o, bass.ds(c * CH, CH)]
                    v.scalar_tensor_tensor(xs, bank[o][:], bias[:, o:o + 1], xs, ALU.add, ALU.add)\
                     .then_inc(base_done, 1)

            for i in (0, 2):
                then(v.tensor_copy(b_split[i * RANK:(i + 1) * RANK, :], bmat[i * RANK:(i + 1) * RANK, :]))
            then(v.tensor_copy(b_hi[RANK:2 * RANK, :], bmat[RANK:2 * RANK, :]))
            v.tensor_tensor(b_split[RANK:2 * RANK, :], bmat[RANK:2 * RANK, :], b_hi[RANK:2 * RANK, :].bitcast(F32),
                            ALU.subtract).then_inc(b_done, 1)
            v.wait_ge(peak_all, 1)
            then(v.tensor_scalar(big[:, 2, :], big[:, 1, :], 1e-6, None, ALU.max))
            then(v.reciprocal(big[:, 3, :], big[:, 2, :]))
            then(v.tensor_scalar(big[:, 3, :], big[:, 3, :], 0.5, None, ALU.mult))
            then(v.tensor_scalar(g0[:], gate[:, :, 0:NE], big[:, 3, 0:1], None, ALU.mult))
            then(v.tensor_scalar(g1[:], gate[:, :, NE:], big[:, 3, 1:2], None, ALU.mult))
            then(v.tensor_tensor(g0[:], g0[:], g1[:], ALU.add))
            then(v.tensor_reduce(row[:, 0, :], g0[:], AX.X, ALU.max))
            v.tensor_tensor(g0[:], g0[:], per_token(row[:, 0, :]), ALU.subtract).then_inc(g_exp_in, 1)
            v.wait_ge(g_exp, 1)
            then(v.tensor_reduce(row[:, 0, :], g1[:], AX.X, ALU.add))
            then(v.reciprocal(row[:, 1, :], row[:, 0, :]))
            then(v.tensor_tensor(g0[:], g1[:], per_token(row[:, 1, :]), ALU.mult))
            for i in range(NT):
                ins = v.max(top[:, i, :], g0[:, i, :])
            then(ins)
            v.tensor_tensor(g1[:], g0[:], top[:, :, 1:2].to_broadcast([P, NT, NE]), ALU.subtract).then_inc(g_exp_in, 1)
            v.wait_ge(g_exp, 2)
            then(v.tensor_scalar(g2[:], g2[:], 1.0, None, ALU.add))
            then(v.reciprocal(g2[:], g2[:]))
            then(v.tensor_tensor(g0[:], g0[:], g2[:], ALU.mult))
            then(v.tensor_reduce(row[:, 0, :], g0[:], AX.X, ALU.add))
            then(v.tensor_scalar(row[:, 0, :], row[:, 0, :], 1e-9, None, ALU.add))
            then(v.reciprocal(row[:, 1, :], row[:, 0, :]))
            v.tensor_tensor(g0[:], g0[:], per_token(row[:, 1, :]), ALU.mult).then_inc(w_ready, 1)
            with v.Fori(0, EARLY) as c:
                base(c)
            for i in range(4):
                v.wait_ge(w_turned, i + 1)
                v.tensor_copy(wgt[:, i * 512:(i + 1) * 512], bank[6 + i % 2][0:NE, :]).then_inc(w_copied, 1)
            for i in range(4):
                v.wait_ge(mix_mm, i + 1)
                z = zh[0:RANK, i * 1024:(i + 1) * 1024].rearrange("p (a s) -> p a s", s=2)
                v.scalar_tensor_tensor(z, z, 0.5, bank[4 + i % 2][0:RANK, :].unsqueeze(2).to_broadcast([RANK, 512, 2]),
                                       ALU.mult, ALU.mult).then_inc(mix_done, 1)
            for i in range(4):
                cols = slice(i * 1024, (i + 1) * 1024)
                v.wait_ge(z_hi_done, i + 1)
                v.tensor_tensor(z_split[2 * RANK:, cols], zh[0:RANK, cols], z_split[0:RANK, cols].bitcast(F32),
                                ALU.subtract).then_inc(z_lo_done, 1)
            with v.Fori(EARLY, NCH) as c:
                base(c)

            def last_sum(c, first):
                for o in range(KB):
                    v.wait_ge(delta_mm, c * KB + (o + 1))
                    if not first:
                        v.wait_ge(out_done[o], c * 16)
                    v.tensor_tensor(fin[:, o, :], bank[o][:], x2[:, o, bass.ds(c * CH, CH)], ALU.add)\
                     .then_inc(fin_done, 1)

            last_sum(0, True)
            with v.Fori(1, NCH) as c:
                last_sum(c, False)


def program(nc, io, out):
    scratch = {
        "wg": nc.dram_tensor("wg_scratch", [BATCH, SEQ * SEQ], F32, kind="Internal").ap(),
        "wkv": nc.dram_tensor("wkv_scratch", [KB, P, KVH, 2 * HD], F32, kind="Internal").ap(),
        "kpad": nc.dram_tensor("kpad_scratch", [SEQ, KPAD], F32, kind="Internal").ap(),
        "x2T": nc.dram_tensor("x2T_scratch", [DM, TOK], F32, kind="Internal").ap(),
    }
    weights_and_ssm(nc, io, scratch)
    attention(nc, io, scratch)
    ssm_and_ffn(nc, io, scratch, out)


def layouts(x, itok_B_0_15, itok_B_78_3631, L0_cond_weights, L0_attn_Wq, L0_attn_Wkr, L0_attn_Wdk, L0_attn_Wupk,
            L0_attn_Wupv, L0_attn_Wo, L0_cond2_log_dt, L0_cond2_C, L0_cond2_log_A_real, L0_cond2_A_imag, L0_cond2_D,
            L0_ffn_W, L0_ffn_b, L0_ffn_A, L0_ffn_Bmat, L0_ffn_LiMEs):
    def rev(a, axis):
        a = np.moveaxis(a, axis, 0)
        a = a.reshape(KB, P, *a.shape[1:])[:, ::-1].reshape(a.shape)
        return np.moveaxis(a, 0, axis)

    tok = x.reshape(TOK, DM)
    return {
        "consts": constants(),
        "x_tok": tok, "xT": rev(tok.T, 0), "cond": itok_B_0_15, "length": itok_B_78_3631,
        "w_cond": L0_cond_weights.reshape(NST, SEQ * SEQ),
        "wqT": L0_attn_Wq.T, "wkrT": L0_attn_Wkr.T, "wdk": L0_attn_Wdk, "wupkT": L0_attn_Wupk.T,
        "wupvT": L0_attn_Wupv.T, "woT": rev(L0_attn_Wo.T, 1),
        "log_dt": L0_cond2_log_dt, "C_re": L0_cond2_C[..., 0].T, "C_im": L0_cond2_C[..., 1].T,
        "log_A_real": L0_cond2_log_A_real.T, "A_imag": L0_cond2_A_imag.T, "D": L0_cond2_D,
        "wT": rev(L0_ffn_W.T, 1), "wza": np.concatenate([L0_ffn_A, L0_ffn_W[:NE].T], 1),
        "bias": rev(L0_ffn_b, 0).reshape(KB, P).T, "bias8": L0_ffn_b[:NE], "bmat": rev(L0_ffn_Bmat, 1),
        "limes": L0_ffn_LiMEs, "limesT": L0_ffn_LiMEs.T,
    }


def kernel(**inputs):
    import concourse.bacc as _bacc
    from concourse.bass_utils import run_bass_kernel_spmd as _run

    nc = _bacc.Bacc("TRN2", target_bir_lowering=False, num_devices=1)
    arrays, io = {}, {}
    for name, a in layouts(**{k: np.asarray(v) for k, v in inputs.items()}).items():
        a = np.ascontiguousarray(a)
        arrays[f"in_{name}"] = a
        io[name] = nc.dram_tensor(f"in_{name}", a.shape, mybir.dt.from_np(a.dtype), kind="ExternalInput").ap()
    out = nc.dram_tensor("out", [DM, TOK], F32, kind="ExternalOutput").ap()
    program(nc, io, out)
    r = _run(nc, [arrays], core_ids=[0])
    o = np.asarray(r.results[0]["out"]).reshape(KB, P, TOK)[:, ::-1].reshape(DM, TOK)
    return np.ascontiguousarray(o.T).reshape(BATCH, SEQ, DM)
```

```python
from contextlib import ExitStack
import math

import numpy as np

import concourse.bass as bass
from concourse import mybir

F32 = mybir.dt.float32
F32R = mybir.dt.float32r
I32 = mybir.dt.int32
ALU = mybir.AluOpType
ACT = mybir.ActivationFunctionType
AX = mybir.AxisListType

P = 128
BATCH, SEQ, DM = 128, 32, 512
TOK = BATCH * SEQ
KB = DM // P
KVH, GRP, HD = 8, 4, 128
CH = 512
BCH = CH // SEQ
QTOK = 1024
NQ = TOK // QTOK
UPQ = KVH * (QTOK // CH)
TPC = CH // P
NST, NSTATE = 16, 64
NE, RANK = 8, 32
NC_, NF_ = 16, 32
NSEC = 5
SECW = [NC_, NC_, NF_, 1, 1]
SECO = [0, NC_, 2 * NC_, 2 * NC_ + NF_, 2 * NC_ + NF_ + 1]
NANG = 2 * NC_ + NF_ + 2
KPAD = P - 1 + DM + 1
SCALE = 1.0 / math.sqrt(HD)
TWO_PI = 2.0 * math.pi
PI_HEAD = 6.28125
PI_MID = float(np.float32(np.round((TWO_PI - PI_HEAD) * 2 ** 22) / 2 ** 22))
PI_TAIL = TWO_PI - PI_HEAD - PI_MID
LN2_HEAD = float(np.float32(np.round(math.log(2.0) * 2 ** 12) / 2 ** 12))
LN2_TAIL = math.log(2.0) - LN2_HEAD
MAGIC = float(1.5 * 2 ** 23)

C_ROPE = 0
C_MASK = C_ROPE + 4 * SEQ
C_ID = C_MASK + SEQ
C_PIDX = C_ID + P
C_W = C_PIDX + KB
L_LAG = 0
L_PHASE = L_LAG + NANG
L_W = L_PHASE + 2 * NSEC


def constants():
    c, lags = np.zeros((P, C_W), np.float32), np.zeros((P, L_W), np.float32)
    inv = 1.0 / 10000.0 ** (np.arange(0, HD, 2, dtype=np.float32) / HD)
    freqs = np.outer(np.arange(SEQ, dtype=np.float32), inv)
    emb = np.concatenate([freqs, freqs], -1)
    cos, sin = np.cos(emb).T, np.sin(emb).T
    sin = np.concatenate([-sin[:64], sin[64:]], 0)
    roped = (np.arange(HD) % 64 < 32)[:, None]
    c[:, 0:SEQ], c[:, SEQ:2 * SEQ] = cos, sin
    c[:, 2 * SEQ:3 * SEQ], c[:, 3 * SEQ:4 * SEQ] = np.where(roped, cos, 1.0), np.where(roped, sin, 0.0)
    pos = np.arange(P) % SEQ
    c[:, C_MASK:C_MASK + SEQ] = np.where(np.arange(SEQ)[None] <= pos[:, None], 0.0, -1e9)
    c[:, C_ID:C_ID + P] = np.eye(P)
    c[:, C_PIDX:C_PIDX + KB] = np.arange(P)[:, None] + P * np.arange(KB)[None]
    coarse, fine = NF_ * np.arange(NC_), np.arange(NF_)
    lags[:, L_LAG:L_LAG + NANG] = np.concatenate([coarse, coarse, fine, [0.5, 0.5]])[None]
    im = np.arange(P)[:, None] >= NSTATE
    quarter = np.where(im, 1, 0)
    turns = np.concatenate([quarter + 1, quarter, 1 - quarter, 0 * quarter, 0 * quarter + 1], 1) * 0.25
    lags[:, L_PHASE:L_PHASE + NSEC] = turns
    lags[:, L_PHASE + NSEC:L_PHASE + 2 * NSEC] = turns * TWO_PI
    return c, lags


NCH = TOK // CH
HQ = GRP * CH


class Shared:
    pass


def shared(nc, ctx):
    def sb(name, shape, dt=F32):
        return ctx.enter_context(nc.sbuf_tensor(name, shape, dt))

    def sem(name):
        return ctx.enter_context(nc.semaphore(name))

    sh = Shared()
    sh.x2_offset = (nc.sbuf_base + 31) // 32 * 32
    sh.x2 = sb("x2", [P, NCH, KB, CH])
    sh.cst = sb("cst", [P, C_W])
    sh.bdc = sb("bdc", [P, QTOK // P, P])
    sh.lens_i = sb("lens_i", [P, BATCH], I32)
    flat = sh.x2[:].rearrange("p c o t -> p (c o t)")
    sh.xt = flat[:, 0:2 * HQ].rearrange("p (t f) -> p t f", f=DM)
    sh.stage = flat[:, 2 * HQ:3 * HQ].rearrange("p (b j n) -> p b j n", b=2, j=2)
    sh.qT = flat[:, 3 * HQ:4 * HQ].rearrange("p (g t) -> p g t", g=GRP)
    sh.swapped = flat[:, 4 * HQ:4 * HQ + 5 * CH].rearrange("p (i t) -> p i t", i=5)
    sh.kT, sh.vT, sh.sc = (flat[:, 4 * HQ + i * CH:4 * HQ + (i + 1) * CH] for i in (5, 6, 7))
    sh.wkv_last = flat[:, 4 * HQ:5 * HQ].rearrange("p (h n) -> p h n", h=KVH)
    sh.zrow = flat[0:SEQ, 4 * HQ + 5 * CH:4 * HQ + 5 * CH + P]
    sh.kern = flat[0:NC_, 4 * HQ + 6 * CH:4 * HQ + 8 * CH].rearrange("p (h c) -> p h c", c=NF_)
    sh.acc = sh.x2[:, NCH - 2:, :, :]
    sh.cst_in, sh.len_in = sem("cst_in"), sem("len_in")
    sh.x_in, sh.bdc_in = sem("x_in"), sem("bdc_in")
    sh.stage_in = [sem("stage_in0"), sem("stage_in1")]
    sh.w_lo_done = sem("w_lo_done")
    sh.acc_done = sem("acc_done")
    sh.kpad_out, sh.wkv_last_out = sem("kpad_out"), sem("wkv_last_out")
    sh.x2_in = sem("x2_in")
    sh.x2_out = [sem("x2_out0"), sem("x2_out1")]
    sh.toep_in = [sem(f"toep_in{i}") for i in range(4)]
    return sh


def load_tokens(sp, io, sh, q):
    for i in range(2):
        sp.dma_start(sh.xt[:, 4 * i:4 * i + 4, :],
                     io["x_tok"][bass.ds(q * QTOK + i * 512, 512), :].rearrange("(t p) f -> p t f", p=P))\
          .then_inc(sh.x_in, 16)


def load_cond(sp, scratch, sh, q):
    for b in range(4):
        sp.dma_start(sh.bdc[32 * b:32 * b + 32, :, 32 * b:32 * b + 32],
                     scratch["wg"].rearrange("(t b) (c d) -> b c t d", b=4, c=SEQ)
                     [b, :, bass.ds(q * (QTOK // P), QTOK // P), :]).then_inc(sh.bdc_in, 16)


def load_queries(sp, io, sh, kind, place, head):
    src = io["wqT"].rearrange("(k p) (m n) -> p k m n", p=P, n=GRP * HD)[
        :, 2 * kind:2 * kind + 2, bass.ds(head, 1), :]
    sp.dma_start(sh.stage[:, place % 2, :, :].unsqueeze(2), src).then_inc(sh.stage_in[place % 2], 16)


def load_toeplitz(sp, scratch, sh, dst, s, i):
    base = scratch["kpad"][bass.ds(s, 1), 0:DM]
    src = bass.AP(tensor=base.tensor, offset=base.offset, ap=[[1, P], [1, DM]])
    sp.dma_start(dst, src).then_inc(sh.toep_in[i], 16)


def weights_and_ssm(nc, io, scratch, sh):
    with ExitStack() as ctx:
        def sb(name, shape, dt=F32):
            return ctx.enter_context(nc.sbuf_tensor(name, shape, dt))

        def sem(name):
            return ctx.enter_context(nc.semaphore(name))

        cst = sh.cst
        lags = sb("a_lags", [P, L_W])
        wdk = sb("a_wdk", [P, KB, DM])
        wupk = sb("a_wupk", [P, KB, DM])
        wupv = sb("a_wupv", [P, KB, KVH * HD])
        wkr = sb("a_wkr", [P, KB, DM])
        wkv_ = sb("a_wkv", [P, KB - 1, KVH, 2 * HD])
        wkv = [wkv_[:, m, :, :] for m in range(KB - 1)] + [sh.wkv_last]
        condi = sb("a_condi", [NST, BATCH], I32)
        condf = sb("a_condf", [NST, BATCH])
        onehot = sb("a_onehot", [NST, BATCH])
        wcond = sb("a_wcond", [NST, SEQ * SEQ])
        wg = sb("a_wg", [P, SEQ * SEQ])
        par = sb("a_par", [P, 5, SEQ])
        dskip = sb("a_dskip", [1, SEQ])
        eab = sb("a_eab", [P, 2, SEQ])
        ek = sb("a_ek", [P, 2, SEQ])
        er_ = sb("a_er", [P, 2, SEQ])
        ei_ = sb("a_ei", [P, 2, SEQ], I32)
        xy = sb("a_xy", [P, 2, SEQ])
        tnh = sb("a_tnh", [P, SEQ])
        mag = sb("a_mag", [P, SEQ, NC_ + NF_])
        ang = sb("a_ang", [P, SEQ, NANG])
        turn = sb("a_turn", [P, SEQ, NANG])
        sn = sb("a_sn", [P, SEQ, NANG])
        tmp = sb("a_tmp", [P, 16, SEQ])
        lft = sb("a_lft", [P, SEQ, NC_])
        lf2 = sb("a_lf2", [P, SEQ, NC_])
        rgt = sb("a_rgt", [P, SEQ, NF_])
        kern, zrow = sh.kern, sh.zrow
        pe = [ctx.enter_context(nc.psum_tensor(f"a_pe{i}", [P, 512], F32)) for i in range(6)]
        pg = ctx.enter_context(nc.psum_tensor("a_pg", [P, 2, 512], F32))

        cst_in, ssm_in, cond_in = sh.cst_in, sem("a_ssm_in"), sem("a_cond_in")
        wupv_in, wkr_in = sem("a_wupv_in"), sem("a_wkr_in")
        keys_in = [sem("a_keys_in0"), sem("a_keys_in1")]
        wcond_in = sem("a_wcond_in")
        hot = sem("a_hot")
        gathered = sem("a_gathered")
        wg_ready = sem("a_wg_ready")
        folded = sem("a_folded")
        unfolded = sem("a_unfolded")
        roped = sem("a_roped")
        xy_ready, mag_ready = sem("a_xy_ready"), sem("a_mag_ready")
        mags, ang_ready, sines = sem("a_mags"), sem("a_ang_ready"), sem("a_sines")
        factors, rgt_ready = sem("a_factors"), sem("a_rgt_ready")
        kernel_mm = sem("a_kernel_mm")
        kern_ready = sem("a_kern_ready")
        zeroed = sem("a_zeroed")
        chain = sem("a_chain")
        wg_out = sem("a_wg_out")
        wkv_out = sem("a_wkv_out")
        block = ctx.enter_context(nc.Block())

        @block.sync
        def _(sp):
            sp.dma_start(cst[:], io["consts"]).then_inc(cst_in, 16)
            sp.dma_start(condi[:], io["cond"].partition_broadcast(NST)).then_inc(cond_in, 16)
            def load_keys(i):
                for dst, name in ((wdk, "wdk"), (wupk, "wupkT")):
                    sp.dma_start(dst[:, 2 * i:2 * i + 2, :],
                                 io[name].rearrange("(c p) n -> p c n", p=P)[:, 2 * i:2 * i + 2, :])\
                      .then_inc(keys_in[i], 16)

            load_keys(0)
            sp.dma_start(lags[:], io["lags"]).then_inc(ssm_in, 16)
            for n, name in ((0, "log_A_real"), (2, "A_imag"), (3, "C_re"), (4, "C_im")):
                for half in range(2):
                    sp.dma_start(par[half * NSTATE:(half + 1) * NSTATE, n, :], io[name]).then_inc(ssm_in, 16)
            sp.dma_start(par[:, 1, :], io["log_dt"].partition_broadcast(P)).then_inc(ssm_in, 16)
            sp.dma_start(dskip[:], io["D"].rearrange("(a h) -> a h", a=1)).then_inc(ssm_in, 16)
            load_keys(1)
            sp.dma_start(wupv[:], io["wupvT"].rearrange("(c p) n -> p c n", p=P)).then_inc(wupv_in, 16)
            sp.dma_start(wcond[:], io["w_cond"]).then_inc(wcond_in, 16)
            sp.dma_start(wkr[:], io["wkrT"].rearrange("(c p) n -> p c n", p=P)).then_inc(wkr_in, 16)
            sp.wait_ge(wg_ready, 2)
            sp.dma_start(scratch["wg"], wg[:]).then_inc(wg_out, 16)
            load_tokens(sp, io, sh, 0)
            for kind in range(2):
                sp.wait_ge(sh.w_lo_done, 2 * kind + 1)
                load_queries(sp, io, sh, kind, kind, 0)
            sp.wait_ge(wg_out, 16)
            load_cond(sp, scratch, sh, 0)
            sp.dma_start(sh.lens_i[:], io["length"].partition_broadcast(P)).then_inc(sh.len_in, 16)
            for m in range(KB):
                sp.wait_ge(unfolded, KB + 2 * (m + 1))
                sp.wait_ge(roped, m + 1)
                sp.dma_start(scratch["wkv"][m], wkv[m])\
                  .then_inc(wkv_out if m < KB - 1 else sh.wkv_last_out, 16)
            sp.wait_ge(zeroed, 1)
            sp.dma_start(scratch["kpad"][:, 0:P - 1], zrow[:, 0:P - 1]).then_inc(sh.kpad_out, 16)
            sp.wait_ge(kern_ready, 3)
            sp.dma_start(scratch["kpad"][:, P - 1:P - 1 + DM].rearrange("h (a c) -> a h c", c=NF_),
                         kern).then_inc(sh.kpad_out, 16)
            sp.wait_ge(wkv_out, 16 * (KB - 1))

        @block.gpsimd
        def _(pool):
            pool.memset(sh.stage[:, 0, 0, 0:1], 0.0).then_inc(sh.w_lo_done, 1)
            pool.memset(sh.bdc[:], 0.0).then_inc(sh.w_lo_done, 1)
            pool.memset(sh.stage[:, 1, 0, 0:1], 0.0).then_inc(sh.w_lo_done, 1)
            pool.memset(zrow, 0.0).then_inc(zeroed, 1)
            pool.wait_ge(ssm_in, 176)
            pool.wait_ge(xy_ready, 1)
            factor_lags = lags[:, L_LAG + NC_:L_LAG + NC_ + NC_ + NF_]
            pool.tensor_tensor(mag[:], xy[:, 0, :].unsqueeze(2).to_broadcast([P, SEQ, NC_ + NF_]),
                               factor_lags.unsqueeze(1).to_broadcast([P, SEQ, NC_ + NF_]),
                               ALU.mult).then_inc(mag_ready, 1)
            pool.wait_ge(wkr_in, 16)
            for m in range(KB):
                pool.tensor_copy(wkv[m][:, :, 0:HD].rearrange("p h (a r) -> p h a r", a=2)[:, :, :, 0:32],
                                 wkr[:, m, :].rearrange("p (h a r) -> p h a r", h=KVH, a=2)).then_inc(roped, 1)
            pool.wait_ge(mags, 2)
            pool.wait_ge(sines, 1)
            pool.tensor_tensor(rgt[:], sn[:, :, 2 * NC_:2 * NC_ + NF_], mag[:, :, NC_:NC_ + NF_],
                               ALU.mult).then_inc(rgt_ready, 1)

        @block.scalar
        def _(act):
            act.wait_ge(xy_ready, 1)
            act.activation(tnh[:], xy[:, 0, :], ACT.Tanh, scale=0.5).then_inc(mags, 1)
            act.wait_ge(mag_ready, 1)
            act.activation(mag[:], mag[:], ACT.Exp).then_inc(mags, 1)
            for m in range(KB):
                act.wait_ge(folded, m + 1)
                act.activation(wkv[m][:, :, 0:HD].rearrange("p h (a r) -> p h a r", a=2)[:, :, :, 32:64],
                               pe[m][:].rearrange("p (h a r) -> p h a r", h=KVH, a=2), ACT.Copy).then_inc(unfolded, 1)
            for j in range(2):
                act.wait_ge(gathered, j + 1)
                act.activation(wg[:, j * 512:(j + 1) * 512], pg[:, j, :], ACT.Copy).then_inc(wg_ready, 1)
            for i in range(2 * KB):
                if i == 4:
                    act.wait_ge(ang_ready, 1)
                    act.activation(sn[:], ang[:], ACT.Sin).then_inc(sines, 1)
                act.wait_ge(folded, KB + i + 1)
                act.activation(wkv[i // 2][:, 4 * (i % 2):4 * (i % 2) + 4, HD:2 * HD],
                               pe[(KB + i) % 6][:].rearrange("p (h d) -> p h d", h=4), ACT.Copy).then_inc(unfolded, 1)

        @block.tensor
        def _(t):
            def gather():
                t.wait_ge(hot, 1)
                t.wait_ge(wcond_in, 16)
                for j in range(2):
                    t.matmul(pg[:, j, :], onehot[:], wcond[:, j * 512:(j + 1) * 512],
                             start=True, stop=True).then_inc(gathered, 1)

            def fold(bank, m, w, blocks):
                for c in blocks:
                    mm = t.matmul(bank, wdk[:, c, m * P:(m + 1) * P], w[:, c, :], start=c == 0, stop=c == KB - 1)
                return mm

            for half in range(2):
                t.wait_ge(keys_in[half], 32)
                for m in range(KB):
                    mm = fold(pe[m][:], m, wupk, range(2 * half, 2 * half + 2))
                    if half:
                        mm.then_inc(folded, 1)
            gather()
            t.wait_ge(wupv_in, 16)
            for i in range(2 * KB):
                if KB + i >= 6:
                    t.wait_ge(unfolded, KB + i - 5)
                fold(pe[(KB + i) % 6][:], i // 2, wupv[:, :, i % 2 * 512:(i % 2 + 1) * 512], range(KB))\
                    .then_inc(folded, 1)
            t.wait_ge(factors, 1)
            t.wait_ge(rgt_ready, 1)
            t.wait_ge(wg_ready, 2)
            for h in range(SEQ):
                mm = t.matmul(pg[0:NC_, h // 16, (h % 16) * NF_:(h % 16 + 1) * NF_], lft[:, h, :], rgt[:, h, :],
                              start=True, stop=True)
            mm.then_inc(kernel_mm, 1)

        @block.vector
        def _(v):
            done = [0]

            def then(ins):
                done[0] += 1
                ins.then_inc(chain, 1)
                v.wait_ge(chain, done[0])

            def mul(out, a, b):
                then(v.tensor_tensor(out, a, b, ALU.mult))

            def add(out, a, b, op=ALU.add):
                then(v.tensor_tensor(out, a, b, op))

            v.wait_ge(cond_in, 16)
            v.wait_ge(cst_in, 16)
            then(v.tensor_copy(condf[:], condi[:]))
            v.tensor_scalar(onehot[:], condf[:], cst[0:NST, C_PIDX:C_PIDX + 1], None, ALU.is_equal).then_inc(hot, 1)
            ea, dt = eab[:, 0, :], eab[:, 1, :]
            x, y = xy[:, 0, :], xy[:, 1, :]
            v.wait_ge(ssm_in, 176)
            logs = par[:, 0:2, :]
            then(v.tensor_scalar(ek[:], logs, 1.0 / math.log(2.0), MAGIC, ALU.mult, ALU.add))
            then(v.tensor_scalar(ek[:], ek[:], -MAGIC, -126.0, ALU.add, ALU.max))
            then(v.tensor_scalar(ek[:], ek[:], 127.0, None, ALU.min))
            then(v.scalar_tensor_tensor(er_[:], ek[:], -LN2_HEAD, logs, ALU.mult, ALU.add))
            then(v.scalar_tensor_tensor(er_[:], ek[:], -LN2_TAIL, er_[:], ALU.mult, ALU.add))
            then(v.tensor_scalar(ek[:], ek[:], 127.0, None, ALU.add))
            then(v.tensor_copy(ei_[:], ek[:]))
            then(v.tensor_scalar(ei_[:], ei_[:], 23, None, ALU.logical_shift_left))
            then(v.tensor_scalar(eab[:], er_[:], 1.0 / math.factorial(8), None, ALU.mult))
            for order in range(7, 0, -1):
                then(v.scalar_tensor_tensor(eab[:], eab[:], 1.0 / math.factorial(order), er_[:], ALU.add, ALU.mult))
            then(v.scalar_tensor_tensor(eab[:], eab[:], 1.0, ei_[:].bitcast(F32), ALU.add, ALU.mult))
            mul(x, ea, dt)
            then(v.tensor_scalar(x, x, -1.0, None, ALU.mult))
            v.tensor_tensor(y, par[:, 2, :], dt, ALU.mult).then_inc(xy_ready, 1)
            v.wait_ge(xy_ready, 1)
            mul(ang[:], y.unsqueeze(2).to_broadcast([P, SEQ, NANG]),
                lags[:, L_LAG:L_LAG + NANG].unsqueeze(1).to_broadcast([P, SEQ, NANG]))
            for s in range(NSEC):
                a, b = SECO[s], SECO[s] + SECW[s]
                then(v.tensor_scalar(turn[:, :, a:b], ang[:, :, a:b], 1.0 / TWO_PI,
                                     lags[:, L_PHASE + s:L_PHASE + s + 1], ALU.mult, ALU.add))
            then(v.tensor_scalar(turn[:], turn[:], MAGIC, None, ALU.add))
            then(v.tensor_scalar(turn[:], turn[:], -MAGIC, None, ALU.add))
            for part in (PI_HEAD, PI_MID, PI_TAIL):
                then(v.scalar_tensor_tensor(ang[:], turn[:], -part, ang[:], ALU.mult, ALU.add))
            for s in range(NSEC):
                a, b = SECO[s], SECO[s] + SECW[s]
                then(v.tensor_scalar(ang[:, :, a:b], ang[:, :, a:b],
                                     lags[:, L_PHASE + NSEC + s:L_PHASE + NSEC + s + 1], None, ALU.add))
            then(v.tensor_scalar(turn[:], ang[:], 1.0 / TWO_PI, MAGIC, ALU.mult, ALU.add))
            then(v.tensor_scalar(turn[:], turn[:], -MAGIC, None, ALU.add))
            then(v.scalar_tensor_tensor(ang[:], turn[:], -TWO_PI, ang[:], ALU.mult, ALU.add))
            then(v.tensor_scalar(ang[:], ang[:], 3.1415925, None, ALU.min))
            v.tensor_scalar(ang[:], ang[:], -3.1415925, None, ALU.max).then_inc(ang_ready, 1)
            em, e0, s2, er, ei, ar2, inv, mr, mi, cr, ci, t0, t1 = [tmp[:, i, :] for i in range(13)]
            v.wait_ge(mags, 2)
            then(v.tensor_scalar(e0, tnh[:], -1.0, 1.0, ALU.mult, ALU.add))
            then(v.reciprocal(em, e0))
            then(v.scalar_tensor_tensor(em, em, 2.0, tnh[:], ALU.mult, ALU.mult))
            v.wait_ge(sines, 1)
            sh, chf = sn[:, :, SECO[3]], sn[:, :, SECO[4]]
            mul(s2, sh, sh)
            then(v.tensor_scalar(s2, s2, 2.0, None, ALU.mult))
            then(v.tensor_scalar(t0, s2, -1.0, 1.0, ALU.mult, ALU.add))
            mul(er, em, t0)
            add(er, er, s2, ALU.subtract)
            mul(t1, sh, chf)
            then(v.tensor_scalar(e0, em, 1.0, 2.0, ALU.add, ALU.mult))
            mul(ei, e0, t1)
            ai = par[:, 2, :]
            mul(ar2, ea, ea)
            mul(t0, ai, ai)
            add(ar2, ar2, t0)
            then(v.reciprocal(inv, ar2))
            mul(t0, er, ea)
            mul(t1, ei, ai)
            add(mr, t1, t0, ALU.subtract)
            mul(mr, mr, inv)
            mul(t0, ei, ea)
            mul(t1, er, ai)
            add(mi, t0, t1)
            then(v.scalar_tensor_tensor(mi, mi, -1.0, inv, ALU.mult, ALU.mult))
            mul(t0, par[:, 3, :], mr)
            mul(t1, par[:, 4, :], mi)
            add(cr, t0, t1, ALU.subtract)
            then(v.tensor_scalar(cr, cr, 2.0, None, ALU.mult))
            mul(t0, par[:, 3, :], mi)
            mul(t1, par[:, 4, :], mr)
            add(ci, t0, t1)
            then(v.tensor_scalar(ci, ci, 2.0, None, ALU.mult))
            mul(lft[:], sn[:, :, 0:NC_], cr.unsqueeze(2).to_broadcast([P, SEQ, NC_]))
            mul(lf2[:], sn[:, :, NC_:2 * NC_], ci.unsqueeze(2).to_broadcast([P, SEQ, NC_]))
            add(lft[:], lft[:], lf2[:], ALU.subtract)
            v.tensor_tensor(lft[:], lft[:], mag[:, :, 0:NC_], ALU.mult).then_inc(factors, 1)
            v.wait_ge(kernel_mm, 1)
            for j in range(2):
                v.tensor_copy(kern[:, 16 * j:16 * j + 16, :], pg[0:NC_, j, :].rearrange("p (h c) -> p h c", h=16))\
                 .then_inc(kern_ready, 1)
            v.wait_ge(kern_ready, 2)
            v.tensor_tensor(kern[0:1, :, 0], kern[0:1, :, 0], dskip[:], ALU.add).then_inc(kern_ready, 1)


def attention(nc, io, scratch, sh):
    with ExitStack() as ctx:
        def sb(name, shape, dt=F32):
            return ctx.enter_context(nc.sbuf_tensor(name, shape, dt))

        def sem(name):
            return ctx.enter_context(nc.semaphore(name))

        cst, bdc, xt, stage, qT, swapped, kT, vT, acc = (
            sh.cst, sh.bdc, sh.xt, sh.stage, sh.qT, sh.swapped, sh.kT, sh.vT, sh.acc)
        sc = sh.sc.rearrange("p (a k) -> p a k", k=SEQ)
        h_hi, h_lo = sb("h_hi", [P, KB, QTOK], F32R), sb("h_lo", [P, KB, QTOK], F32R)
        wq_hi, wq_lo = (sb(f"wq_{x}", [P, 2, KB, GRP * HD], F32R) for x in ("hi", "lo"))
        wkv_hi, wkv_lo = (sb(f"wkv_{x}", [P, 2, KB, 2 * HD], F32R) for x in ("hi", "lo"))
        wo_hi, wo_lo = (sb(f"wo_{x}", [P, GRP, DM], F32R) for x in ("hi", "lo"))
        v_hi = sb("v_hi", [P, TPC, HD], F32R)
        v_pair = sb("v_pair", [P, 2, TPC, HD], F32R)
        pr = sb("b_pr", [P, GRP * TPC, SEQ])
        red = sb("b_red", [P, 2, GRP * TPC])
        rcp = sb("b_rcp", [P, GRP * TPC])
        p_hi = sb("p_hi", [P, GRP * TPC, SEQ], F32R)
        diag_lo = sb("diag_lo", [P, TPC, 4, GRP * SEQ], F32R)
        p_pair = sb("p_pair", [P, TPC, 2, 2 * GRP * SEQ], F32R)
        o_hi, o_lo = sb("o_hi", [P, GRP, CH], F32R), sb("o_lo", [P, GRP, CH], F32R)

        proj = [ctx.enter_context(nc.psum_tensor(f"proj{i}", [P, 512], F32)) for i in range(3)]
        ps = ctx.enter_context(nc.psum_tensor("scores", [P, 512], F32))
        ob = [ctx.enter_context(nc.psum_tensor(f"outs{i}", [P, 512], F32)) for i in range(4)]

        first_banks = proj + ob + [ps]
        cst_in, x_in, bdc_in, stage_in, w_lo_done, acc_done = (
            sh.cst_in, sh.x_in, sh.bdc_in, sh.stage_in, sh.w_lo_done, sh.acc_done)
        acc_in = [sem("acc_in0"), sem("acc_in1")]
        acc_out = sh.x2_out
        w_hi_done = sem("w_hi_done")
        wo_hi_done = sem("wo_hi_done")
        cleared = sem("b_cleared")
        h_mm, h_hi_done, h_lo_done = sem("h_mm"), sem("h_hi_done"), sem("h_lo_done")
        proj_done = sem("proj_done")
        swap_done = sem("swap_done")
        cos_done = sem("cos_done")
        sin_done = sem("sin_done")
        rope_done = sem("rope_done")
        vT_done = sem("vT_done")
        v_mm = sem("v_mm")
        v_copied = sem("v_copied")
        v_hi_done, v_pair_hi_done, v_pair_lo_done = sem("v_hi_done"), sem("v_pair_hi_done"), sem("v_pair_lo_done")
        scores_done = sem("scores_done")
        turned = sem("turned")
        smax = sem("smax")
        exp_done = sem("exp_done")
        keys_done = sem("keys_done")
        p_hi_done, diag_lo_done = sem("p_hi_done"), sem("diag_lo_done")
        pair_act_done, pair_dve_done = sem("pair_act_done"), sem("pair_dve_done")
        pv_done, o_hi_done, o_lo_done = sem("pv_done"), sem("o_hi_done"), sem("o_lo_done")
        wo_done = sem("wo_done")
        block = ctx.enter_context(nc.Block())

        values = vT.rearrange("p (t d) -> p t d", t=TPC)

        Q0, Q1, Q2, KEYS, VALUES, Q3 = range(6)
        ROPED = (Q0, Q1, Q2, KEYS, Q3)

        ropes = {"q": (cst[:, C_ROPE:C_ROPE + SEQ], cst[:, C_ROPE + SEQ:C_ROPE + 2 * SEQ]),
                 "k": (cst[:, C_ROPE + 2 * SEQ:C_ROPE + 3 * SEQ], cst[:, C_ROPE + 3 * SEQ:C_ROPE + 4 * SEQ])}

        def head(i):
            return 3 if i == Q3 else i

        def target(i):
            return kT[:] if i == KEYS else qT[:, head(i), :]

        def by_position(ap):
            return ap.rearrange("p (b s) -> p b s", s=SEQ)

        def table(i, which):
            return ropes["k" if i == KEYS else "q"][which].unsqueeze(1).to_broadcast([P, BCH, SEQ])

        QA, QB, OA, OB, KV = range(5)
        FIRST_PIECES = ((0, QA, 0), (1, QB, 0), (2, KV, 0))

        def pieces(w, kinds, last=False):
            if last:
                return [(5 * w + 3 + kind - OA, kind, w) for kind in kinds if kind in (OA, OB)]
            return [(5 * w + 3 + kind, kind, 1 - w) for kind in kinds]

        def half(kind, part, w, j):
            if kind == KV:
                return (wkv_hi, wkv_lo)[part][:, w, 2 * j:2 * j + 2, :].rearrange("p k n -> p (k n)")
            if kind in (OA, OB):
                return (wo_hi, wo_lo)[part][:, 2 * (kind - OA) + j, :]
            return (wq_hi, wq_lo)[part][:, w, 2 * kind + j, :]

        PAIR_ACT = ((0, 0), (0, 1), (0, 2), (0, 3), (1, 0), (1, 1))
        PAIR_DVE = ((1, 2), (1, 3))

        def pair_place(copy, b):
            start = 64 * copy + 32 * (b % 2)
            return p_pair[start:start + 32, :, b // 2, P * (b % 2):P * (b % 2 + 1)]

        def by_tile(ap, b):
            return ap[32 * b:32 * b + 32, :, :].rearrange("p (t g) k -> p t (g k)", t=TPC)

        def prev(n):
            return not isinstance(n, int) or n > 0

        def early(u, last):
            return pieces(u // 2 % 2, (OA, OB), last) if u % 2 else []

        def late(u, last):
            return pieces(u // 2 % 2, (KV,) if u % 2 else (QA, QB), last)

        def schedule(eng, mix, step, finish):
            def middle(q, last):
                with eng.Fori(0, 3) as j:
                    for u in range(1, 5):
                        step(u, q * UPQ + j * 4 + u, q * 4 + j + u // 4, q, False)
                for u in range(13, 16):
                    step(u, q * UPQ + u, q * 4 + 3, q, last and u >= 14)

            mix(0)
            step(0, 0, 0, 0, False)
            with eng.Fori(0, NQ - 1) as q:
                middle(q, False)
                step(0, q * UPQ + UPQ, q * 4 + 4, q + 1, False)
            middle(NQ - 1, True)
            finish(NQ * UPQ)

        def mixes(u, last):
            return u == UPQ - 1 and not last

        def ends(u, last):
            return u == UPQ - 1 and last

        EARLY_BLOCKS = 1

        MIX_TILES = ((0, 1, 2), (3, 4, 5), (6, 7), ())

        @block.sync
        def _(sp):
            def load_sums(c, start):
                sp.dma_start(acc[:, c, :, :],
                             io["xT"].rearrange("(o p) t -> p o t", p=P)[:, :, bass.ds(start, CH)])\
                  .then_inc(acc_in[c], 16)

            def store_sums(q, c):
                sp.wait_ge(acc_done, q * (4 * UPQ) + 4 * (UPQ + c))
                sp.wait_ge(cst_in, 16)
                sp.dma_start(scratch["x2T"][bass.ds(q * 2 + c, 1)].rearrange("a p o t -> (a p) o t"),
                             acc[:, c, :, :]).then_inc(acc_out[c], 16)

            def load_piece(pair, place, kind, own, following):
                sp.wait_ge(w_lo_done, pair * 20 + (2 * place + 1))
                sp.wait_ge(cst_in, 16)
                if kind in (QA, QB):
                    load_queries(sp, io, sh, kind, place, following)
                    return
                dst = stage[:, place % 2, :, :]
                if kind == KV:
                    src = scratch["wkv"].rearrange("k p h n -> p k h n")[:, :, bass.ds(following, 1), :]
                    dst = dst.rearrange("p a (k n) -> p (a k) n", k=2).unsqueeze(2)
                else:
                    g = 2 * (kind - OA)
                    src = io["woT"].rearrange("(h g p) o -> p h g o", p=P, g=GRP)[:, bass.ds(own, 1), g:g + 2, :]
                    dst = dst.unsqueeze(1)
                sp.dma_start(dst, src).then_inc(stage_in[place % 2], 16)

            def load_pair(pair, in_quarter, after, last, q=None):
                for w in range(2):
                    own = in_quarter * 2 + w
                    following = after if w else in_quarter * 2 + 1
                    if q is not None and w == 0:
                        store_sums(q, 0)
                    final = last and w == 1
                    for place, kind, _ in pieces(w, (QA, QB), final):
                        load_piece(pair, place, kind, own, following)
                    if q is not None and w == 0:
                        next_sums(q, 0)
                    for place, kind, _ in pieces(w, (OA, OB), final):
                        load_piece(pair, place, kind, own, following)
                    if q is not None and w == 0:
                        store_sums(q, 1)
                        next_sums(q, 1)
                    for place, kind, _ in pieces(w, (KV,), final):
                        load_piece(pair, place, kind, own, following)

            def next_sums(q, c):
                sp.wait_ge(acc_out[c], q * 16 + 16)
                sp.wait_ge(cst_in, 16)
                load_sums(c, q * QTOK + (QTOK + c * CH))

            sp.wait_ge(sh.wkv_last_out, 16)
            load_piece(0, *FIRST_PIECES[2][:2], 0, 0)
            for c in range(2):
                load_sums(c, c * CH)
            load_pair(0, 0, 2, False)
            with sp.Fori(0, NQ - 1) as q:
                with sp.Fori(1, 3) as p:
                    load_pair(q * 4 + p, p, p * 2 + 2, False)
                sp.wait_ge(h_mm, q * (QTOK // P) + QTOK // P)
                sp.wait_ge(cst_in, 16)
                load_tokens(sp, io, sh, q + 1)
                load_cond(sp, scratch, sh, q + 1)
                load_pair(q * 4 + 3, 3, 0, False)
                load_pair(q * 4 + 4, 0, 2, False, q)
            with sp.Fori(1, 3) as p:
                load_pair((NQ - 1) * 4 + p, p, p * 2 + 2, False)
            load_pair(NQ * 4 - 1, 3, 0, True)

            def load_x2(c):
                sp.dma_start(sh.x2[:, c, :, :], scratch["x2T"][c]).then_inc(sh.x2_in, 16)

            sp.wait_ge(h_mm, NQ * (QTOK // P))
            for c in range(2):
                sp.wait_ge(acc_out[c], (NQ - 1) * 16)
            for c in (0, 1):
                load_x2(c)
            for i in range(2):
                load_toeplitz(sp, scratch, sh, bdc[:, 4 * i:4 * i + 4, :].rearrange("p t c -> p (t c)"), i, i)
            sp.wait_ge(w_lo_done, 3 + 6 + 10 * NQ * KVH - 6)
            load_x2(2)
            sp.wait_ge(scores_done, NQ * UPQ)
            for c in (3, 4):
                load_x2(c)
            sp.wait_ge(diag_lo_done, NQ * UPQ * 4)
            sp.wait_ge(pair_act_done, NQ * UPQ * len(PAIR_ACT))
            sp.wait_ge(pair_dve_done, NQ * UPQ * len(PAIR_DVE))
            load_x2(5)
            for c in range(2):
                store_sums(NQ - 1, c)

        @block.gpsimd
        def _(pool):
            pool.memset(p_pair[:].bitcast(F32), 0.0).then_inc(cleared, 1)
            pool.memset(diag_lo[:].bitcast(F32), 0.0).then_inc(cleared, 1)
            pool.wait_ge(cst_in, 16)

            def split(pair, listed):
                for place, kind, w in listed:
                    for j in range(2):
                        if kind in (OA, OB):
                            before = 2 * (kind - OA) + (4 if place >= 8 else 0)
                            pool.wait_ge(wo_hi_done, pair * 8 + (before + j + 1))
                        else:
                            before = place if place < 5 else place - (2 if place < 10 else 4)
                            pool.wait_ge(w_hi_done, pair * 12 + (2 * before + j + 1))
                        pool.tensor_tensor(half(kind, 1, w, j), stage[:, place % 2, j, :],
                                           half(kind, 0, w, j).bitcast(F32), ALU.subtract).then_inc(w_lo_done, 1)

            def rotate(i, n):
                r = ROPED.index(i)
                pool.wait_ge(swap_done, n * 5 + (r + 1))
                s = by_position(swapped[:, r, :])
                pool.tensor_tensor(s, s, table(i, 1), ALU.mult).then_inc(sin_done, 1)
                pool.wait_ge(sin_done, n * 5 + (r + 1))
                pool.wait_ge(cos_done, n * 5 + (r + 1))
                pool.tensor_tensor(target(i), target(i), swapped[:, r, :], ALU.add).then_inc(rope_done, 1)

            def step(u, n, pair, q, last):
                for i in (Q0, Q1):
                    rotate(i, n)
                split(pair, early(u, last))
                for i in (Q2, KEYS, Q3):
                    rotate(i, n)
                split(pair, late(u, last))

            def mix(q):
                split(0, FIRST_PIECES)

            schedule(pool, mix, step, lambda n: None)

        @block.scalar
        def _(act):
            act.wait_ge(cst_in, 16)

            def split(pair, listed, n):
                for place, kind, w in listed:
                    act.wait_ge(stage_in[place % 2], pair * 80 + 16 * (place // 2 + 1))
                    for j in range(2):
                        act.activation(half(kind, 0, w, j), stage[:, place % 2, j, :], ACT.Copy)\
                           .then_inc(w_hi_done, 1)

            def swap(i, n):
                act.wait_ge(proj_done, n * 6 + (i + 1))
                r = ROPED.index(i)
                act.activation(swapped[0:64, r, :], proj[i % 3][64:128, :], ACT.Copy)
                act.activation(swapped[64:128, r, :], proj[i % 3][0:64, :], ACT.Copy).then_inc(swap_done, 1)

            def exps(n):
                act.wait_ge(smax, n * 6 - 3)
                act.activation(pr[:], sc[:], ACT.Exp, scale=SCALE).then_inc(exp_done, 1)

            def diag_parts(n):
                act.wait_ge(keys_done, n)
                act.activation(p_hi[:], sc[:], ACT.Copy).then_inc(p_hi_done, 1)
                for copy, b in PAIR_ACT:
                    act.activation(pair_place(copy, b), by_tile(sc, b), ACT.Copy).then_inc(pair_act_done, 1)

            def out_hi(n):
                for t in range(TPC):
                    act.wait_ge(pv_done, n * 4 + (t - 3))
                    act.activation(o_hi[:, :, t * P:(t + 1) * P].rearrange("p g (b s) -> p b g s", b=4),
                                   ob[t][:].rearrange("p (b g s) -> p b g s", b=4, g=GRP), ACT.Copy)\
                       .then_inc(o_hi_done, 1)

            def h_hi_tile(t, q, banks=proj):
                act.wait_ge(h_mm, q * (QTOK // P) + (t + 1))
                mixed = banks[t % len(banks)][:].rearrange("p (k t) -> p k t", k=KB)
                act.activation(h_hi[:, :, t * P:(t + 1) * P], mixed, ACT.Copy).then_inc(h_hi_done, 1)

            def step(u, n, pair, q, last):
                swap(Q0, n)
                if prev(n):
                    exps(n)
                swap(Q1, n)
                if prev(n):
                    diag_parts(n)
                swap(Q2, n)
                swap(KEYS, n)
                act.wait_ge(proj_done, n * 6 + (VALUES + 1))
                if prev(n):
                    act.wait_ge(v_pair_lo_done, n * 2)
                act.activation(vT[:], proj[VALUES % 3][:], ACT.Copy).then_inc(vT_done, 1)
                if prev(n):
                    out_hi(n)
                swap(Q3, n)
                if mixes(u, last):
                    for t in range(QTOK // P):
                        h_hi_tile(t, q + 1)
                act.wait_ge(v_mm, n + 1)
                act.activation(vT[:], ps[:], ACT.Copy).then_inc(v_copied, 1)
                split(pair, late(u, last), n)
                act.wait_ge(v_copied, n + 1)
                act.activation(v_hi[:], values, ACT.Copy).then_inc(v_hi_done, 1)
                for j in range(2):
                    act.activation(v_pair[0:64, j, :, :], values[64 * j:64 * j + 64], ACT.Copy)\
                       .then_inc(v_pair_hi_done, 1)

            def mix(q):
                split(0, FIRST_PIECES[:2], 0)
                for t in range(QTOK // P):
                    h_hi_tile(t, q, first_banks)
                act.wait_ge(cleared, 2)
                act.wait_ge(sh.kpad_out, 32)
                act.wait_ge(sh.wkv_last_out, 16)
                split(0, FIRST_PIECES[2:], 0)

            def finish(n):
                exps(n)
                diag_parts(n)
                out_hi(n)

            schedule(act, mix, step, finish)

        @block.vector
        def _(v):
            for i in range(KB):
                v.memset(red[:, 0, i:i + 1], 0.0).then_inc(acc_done, 1)
            v.wait_ge(cst_in, 16)
            mask = cst[:, C_MASK:C_MASK + SEQ].unsqueeze(1).to_broadcast([P, GRP * TPC, SEQ])

            def per_row(ap):
                return ap.unsqueeze(2).to_broadcast([P, GRP * TPC, SEQ])

            def softmax_front(n):
                v.wait_ge(scores_done, n)
                v.transpose(sc[:].rearrange("p a k -> p (a k)"), ps[:]).then_inc(turned, 1)
                v.wait_ge(turned, n)
                v.tensor_tensor(sc[:], sc[:], mask, ALU.add).then_inc(smax, 1)
                v.wait_ge(smax, n * 6 - 5)
                v.tensor_reduce(red[:, 0, :], sc[:], AX.X, ALU.max).then_inc(smax, 1)
                v.wait_ge(smax, n * 6 - 4)
                v.tensor_tensor(sc[:], sc[:], per_row(red[:, 0, :]), ALU.subtract).then_inc(smax, 1)

            def softmax_back(n):
                v.wait_ge(exp_done, n)
                v.tensor_reduce(red[:, 1, :], pr[:], AX.X, ALU.add).then_inc(smax, 1)
                v.wait_ge(smax, n * 6 - 2)
                v.reciprocal(rcp[:], red[:, 1, :]).then_inc(smax, 1)
                v.wait_ge(smax, n * 6 - 1)
                v.tensor_tensor(pr[:], pr[:], per_row(rcp[:]), ALU.mult).then_inc(smax, 1)
                v.wait_ge(smax, n * 6)
                v.transpose(sc[:].rearrange("p a k -> p (a k)"), pr[:].rearrange("p a k -> p (a k)"))\
                 .then_inc(keys_done, 1)

            def diag_parts(n):
                v.wait_ge(p_hi_done, n)
                for b in range(4):
                    v.tensor_tensor(diag_lo[32 * b:32 * b + 32, :, b, :], by_tile(sc, b), by_tile(p_hi, b).bitcast(F32),
                                    ALU.subtract).then_inc(diag_lo_done, 1)
                for copy, b in PAIR_DVE:
                    v.tensor_copy(pair_place(copy, b), by_tile(sc, b)).then_inc(pair_dve_done, 1)

            def v_low(n):
                v.wait_ge(v_hi_done, n)
                for j in range(2):
                    rows = slice(64 * j, 64 * j + 64)
                    v.tensor_tensor(v_pair[64:, j, :, :], values[rows], v_hi[rows, :, :].bitcast(F32), ALU.subtract)\
                     .then_inc(v_pair_lo_done, 1)

            def cosine(i, n):
                v.wait_ge(swap_done, n * 5 + (ROPED.index(i) + 1))
                v.tensor_tensor(by_position(target(i)), by_position(proj[i % 3][:]), table(i, 0), ALU.mult)\
                 .then_inc(cos_done, 1)

            def out_lo(n):
                for t in range(TPC):
                    v.wait_ge(o_hi_done, n * 4 + (t - 3))
                    def view(o):
                        return o[:, :, t * P:(t + 1) * P].rearrange("p g (b s) -> p b g s", b=4)
                    v.tensor_tensor(view(o_lo), ob[t][:].rearrange("p (b g s) -> p b g s", b=4, g=GRP),
                                    view(o_hi).bitcast(F32), ALU.subtract).then_inc(o_lo_done, 1)

            def h_lo_tile(t, q, banks=proj):
                v.wait_ge(h_hi_done, q * (QTOK // P) + (t + 1))
                h = slice(t * P, (t + 1) * P)
                v.tensor_tensor(h_lo[:, :, h], banks[t % len(banks)][:].rearrange("p (k t) -> p k t", k=KB),
                                h_hi[:, :, h].bitcast(F32), ALU.subtract).then_inc(h_lo_done, 1)

            def accumulate(n, c, blocks=range(KB), tiles=((),) * KB, q=None):
                for o in blocks:
                    v.wait_ge(wo_done, n * 4 + (o - 3))
                    a = acc[:, c, o, :]
                    v.tensor_tensor(a, a, ob[o][:], ALU.add).then_inc(acc_done, 1)
                    for t in tiles[o]:
                        h_lo_tile(t, q)

            def step(u, n, pair, q, last):
                if prev(n):
                    softmax_front(n)
                    v_low(n)
                cosine(Q0, n)
                if prev(n):
                    softmax_back(n)
                cosine(Q1, n)
                for place, kind, w in early(u, last):
                    v.wait_ge(stage_in[place % 2], pair * 80 + 16 * (place // 2 + 1))
                    for j in range(2):
                        v.tensor_copy(half(kind, 0, w, j), stage[:, place % 2, j, :]).then_inc(wo_hi_done, 1)
                if prev(n):
                    diag_parts(n)
                for i in (Q2, KEYS):
                    cosine(i, n)
                if prev(n):
                    out_lo(n)
                cosine(Q3, n)
                if mixes(u, last):
                    accumulate(n, (u - 1) % 2, tiles=MIX_TILES, q=q + 1)
                elif prev(n):
                    if u in (1, 2):
                        v.wait_ge(acc_in[(u - 1) % 2], q * 16 + 16)
                    accumulate(n, (u - 1) % 2, range(EARLY_BLOCKS) if ends(u, last) else range(KB))

            def mix(q):
                for t in range(QTOK // P):
                    h_lo_tile(t, q, first_banks)

            def finish(n):
                softmax_front(n)
                v_low(n)
                accumulate(n - 1, 0, range(EARLY_BLOCKS, KB - 1))
                softmax_back(n)
                accumulate(n - 1, 0, [KB - 1])
                diag_parts(n)
                out_lo(n)
                accumulate(n, 1)

            schedule(v, mix, step, finish)

        @block.tensor
        def _(t_):
            def product(out, left, right, blocks):
                for k in range(blocks):
                    (l_hi, l_lo), (r_hi, r_lo) = left(k), right(k)
                    t_.matmul(out, l_hi, r_hi, start=k == 0, stop=False)
                    t_.matmul(out, l_hi, r_lo, start=False, stop=False)
                    mm = t_.matmul(out, l_lo, r_hi, start=False, stop=k == blocks - 1)
                return mm

            def item(i, u, n):
                w, c = (u // 2) % 2, u % 2
                if i >= KEYS:
                    t_.wait_ge(cos_done, n * 5 + (i - KEYS + 1))
                elif prev(n) and i == Q0:
                    t_.wait_ge(cos_done, n * 5 - 1)
                elif prev(n) and i == Q1:
                    t_.wait_ge(vT_done, n)
                elif prev(n):
                    t_.wait_ge(cos_done, n * 5)
                tok = slice(c * CH, (c + 1) * CH)
                wh, wl = (wkv_hi, wkv_lo) if i in (KEYS, VALUES) else (wq_hi, wq_lo)
                m = {KEYS: 0, VALUES: 1}.get(i, head(i))
                cols = slice(m * HD, (m + 1) * HD)
                product(proj[i % 3][:], lambda k: (wh[:, w, k, cols], wl[:, w, k, cols]),
                        lambda k: (h_hi[:, k, tok], h_lo[:, k, tok]), KB).then_inc(proj_done, 1)

            def turn_values(n):
                t_.wait_ge(vT_done, n + 1)
                if prev(n):
                    t_.wait_ge(turned, n)
                for t in range(TPC):
                    mm = t_.transpose(ps[:, t * HD:(t + 1) * HD], vT[:, t * P:(t + 1) * P], cst[:, C_ID:C_ID + P])
                mm.then_inc(v_mm, 1)

            def attend(n):
                t_.wait_ge(v_pair_hi_done, n * 2)
                t_.wait_ge(v_pair_lo_done, n * 2)
                t_.wait_ge(diag_lo_done, n * 4)
                t_.wait_ge(pair_act_done, n * len(PAIR_ACT))
                t_.wait_ge(pair_dve_done, n * len(PAIR_DVE))
                for t in range(TPC):
                    t_.wait_ge(acc_done, n * 4 + (t - 3))
                    t_.matmul(ob[t][:], v_hi[:, t, :], diag_lo[:, t, :, :].rearrange("p b s -> p (b s)"),
                              start=True, stop=False)
                    for j in range(2):
                        mm = t_.matmul(ob[t][:, 2 * P * j:2 * P * (j + 1)], v_pair[:, j, t, :], p_pair[:, t, j, :],
                                       start=False, stop=j == 1)
                    mm.then_inc(pv_done, 1)

            def output(n, o):
                cols = slice(o * P, (o + 1) * P)
                product(ob[o][:],
                        lambda g: (wo_hi[:, g, cols], wo_lo[:, g, cols]),
                        lambda g: (o_hi[:, g, :], o_lo[:, g, :]), GRP).then_inc(wo_done, 1)

            def mix_tile(t, q, banks=proj):
                if t >= len(banks):
                    t_.wait_ge(h_lo_done, q * (QTOK // P) + (t - 2))
                for k in range(KB):
                    features = slice(k * P, (k + 1) * P)
                    mm = t_.matmul(banks[t % len(banks)][:, features], xt[:, t, features], bdc[:, t, :],
                                   start=True, stop=True)
                mm.then_inc(h_mm, 1)

            def mix_inputs(q):
                t_.wait_ge(bdc_in, q * 64 + 64)
                t_.wait_ge(x_in, q * 32 + 32)

            def scores(n):
                t_.wait_ge(rope_done, n * 5 + 5)
                t_.wait_ge(v_copied, n + 1)
                for b in range(BCH):
                    s = slice(b * SEQ, (b + 1) * SEQ)
                    r = 32 * (b % 4)
                    mm = t_.matmul(ps[r:r + 32, (b // 4) * P:(b // 4 + 1) * P].rearrange("p (g s) -> p g s", g=GRP),
                                   kT[:, s], qT[:, :, s], start=True, stop=True)
                mm.then_inc(scores_done, 1)

            def step(u, n, pair, q, last):
                if u % 2 == 0:
                    t_.wait_ge(w_lo_done, n * 5 + (3 if prev(n) else 7))
                for i in (Q0, Q1, Q2, KEYS, VALUES):
                    if i == KEYS and u % 2 == 0:
                        t_.wait_ge(w_lo_done, n * 5 + 9)
                    item(i, u, n)
                if prev(n):
                    attend(n)
                item(Q3, u, n)
                if prev(n):
                    t_.wait_ge(o_lo_done, n * 4)
                    if u % 2:
                        t_.wait_ge(w_lo_done, n * 5 + (8 if last else 12))
                before_scores = EARLY_BLOCKS if ends(u, last) else KB
                for o in range(KB):
                    if o == before_scores - 1:
                        turn_values(n)
                    if prev(n):
                        output(n, o)
                    if mixes(u, last):
                        if o == 0:
                            mix_inputs(q + 1)
                            t_.wait_ge(cos_done, n * 5 + 5)
                            t_.wait_ge(vT_done, n + 1)
                        for t in MIX_TILES[o]:
                            mix_tile(t, q + 1)
                    if o == before_scores - 1:
                        scores(n)
                if mixes(u, last):
                    t_.wait_ge(h_lo_done, q * (QTOK // P) + 2 * (QTOK // P))

            def mix(q):
                mix_inputs(q)
                for t in range(QTOK // P):
                    mix_tile(t, q, first_banks)
                t_.wait_ge(h_lo_done, QTOK // P)

            def finish(n):
                attend(n)
                t_.wait_ge(o_lo_done, n * 4)
                for o in range(KB):
                    output(n, o)

            schedule(t_, mix, step, finish)


def ssm_and_ffn(nc, io, scratch, sh, out):
    ANCH = TOK // 2
    NT = ANCH // P
    SPLIT = 3
    HU = 4
    with ExitStack() as ctx:
        def sb(name, shape, dt=F32):
            return ctx.enter_context(nc.sbuf_tensor(name, shape, dt))

        def sem(name):
            return ctx.enter_context(nc.semaphore(name))

        cst, x2, lens_i = sh.cst, sh.x2, sh.lens_i
        y_hi = sb("c_y_hi", [P, NCH, KB, CH], F32R)
        y_lo = nc.alloc_sbuf_tensor_at("c_y_lo", [P, NCH, KB, CH], F32R, offset=sh.x2_offset)
        xs = sb("c_xs", [P, 3, KB, CH])
        toep = [sh.bdc[:, 4 * i:4 * i + 4, :].rearrange("p t c -> p (t c)") for i in range(2)]
        toep += [xs[:, 0, i, :] for i in range(2)]
        y_tmp = [xs[:, 0, 2 + i, :].rearrange("p (o b) -> p o b", b=P) for i in range(2)]
        wT = xs[:, 1, :, :]
        w_hi, w_lo = (sb(f"c_w_{x}", [P, KB, DM], F32R) for x in ("hi", "lo"))
        wza_hi, wza_lo = (sb(f"c_wza_{x}", [P, KB, P], F32R) for x in ("hi", "lo"))
        lens = sb("c_lens", [P, BATCH])
        keep = sb("c_keep", [P, KB, BATCH])
        wza = sb("c_wza", [P, KB, RANK + NE])
        bmat = sb("c_bmat", [RANK, DM])
        b_split = sb("c_b_split", [3 * RANK, DM], F32R)
        z_split = y_hi[0:3 * RANK, 0:2, :, :].rearrange("p c o t -> p (c o t)")
        limes = sb("c_limes", [NE, RANK])
        pick = sb("c_pick", [RANK + NE, 2 * NE])
        bias = sb("c_bias", [P, KB])
        bias8 = sb("c_bias8", [RANK + NE, 1])
        zh = sb("c_zh", [RANK + NE, TOK])
        gate = sb("c_gate", [P, NT, 2 * NE])
        g0, g1, g2 = (sb(f"c_g{i}", [P, NT, NE]) for i in range(3))
        top = sb("c_top", [P, NT, 8])
        row = sb("c_row", [P, 2, NT])
        big = sb("c_big", [P, 4, 2])
        wgt = [sh.bdc[0:NE, 0:4, :].rearrange("p t c -> p (t c)"), sh.bdc[0:NE, 4:8, :].rearrange("p t c -> p (t c)"),
               keep[0:NE, :, :].rearrange("p o b -> p (o b)"), bmat[0:NE, :]]
        bank = [ctx.enter_context(nc.psum_tensor(f"c_ps{i}", [P, 512], F32)) for i in range(8)]

        cst_in, x2_in, par_in, len_in, toep_in = sh.cst_in, sh.x2_in, sem("c_par_in"), sh.len_in, sh.toep_in
        wT_in, wza_in = sem("wT_in"), sem("wza_in")
        wza_clear, wza_hi_done, wza_lo_done = sem("wza_clear"), sem("wza_hi_done"), sem("wza_lo_done")
        w_hi_done, w_lo_done = sem("c_w_hi_done"), sem("c_w_lo_done")
        y_hi_done, y_lo_done = sem("y_hi_done"), sem("y_lo_done")
        xs_in = [sem(f"xs_in{i}") for i in range(3)]
        conv_done, y_done = sem("conv_done"), sem("y_done")
        zh_mm, zh_done = sem("zh_mm"), sem("zh_done")
        pick_clear, pick_in = sem("pick_clear"), sem("pick_in")
        gate_mm = sem("gate_mm")
        peak_local, peak_all = sem("peak_local"), sem("peak_all")
        g_exp_in, g_exp = sem("g_exp_in"), sem("g_exp")
        chain = sem("c_chain")
        w_ready, w_turned, w_copied = sem("w_ready"), sem("w_turned"), sem("w_copied")
        b_done, z_hi_done = sem("b_done"), sem("z_hi_done")
        z_dup_done, z_lo_done = sem("z_dup_done"), sem("z_lo_done")
        mix_mm, mix_done = sem("mix_mm"), sem("mix_done")
        base_mm, base_done = sem("base_mm"), sem("base_done")
        delta_mm, fin_done = sem("delta_mm"), sem("fin_done")
        out_done = [sem(f"out_done{i}") for i in range(3)]
        block = ctx.enter_context(nc.Block())

        def at_position(ap, blocks, s):
            return ap[:, :, 0:blocks, :].rearrange("p c o (b s) -> p o c b s", s=SEQ)[:, :, :, :, bass.ds(s, 1)]\
                .rearrange("p o c b s -> p o c (b s)")

        def by_chunk(ap):
            return ap.rearrange("p o (c b) -> p o c b", c=NCH)

        def chunk(ap, c, o):
            return ap[:, bass.ds(c, 1), o, :].rearrange("p a t -> p (a t)")

        def place(c):
            return 0 if c == 0 else 1 + (c - 1) % 2

        def partial(c, o):
            return xs[:, 0, o, :] if c == 0 else x2[:, c - 1, o, :]

        @block.sync
        def _(sp):
            for i in range(2, HU):
                load_toeplitz(sp, scratch, sh, toep[i], i, i)
            sp.dma_start(wza[:], io["wza"].rearrange("(k p) n -> p k n", p=P)).then_inc(wza_in, 16)
            sp.dma_start(wT, io["wT"].rearrange("(k p) n -> p k n", p=P)).then_inc(wT_in, 16)
            sp.dma_start(bmat[:], io["bmat"]).then_inc(par_in, 16)
            sp.dma_start(limes[:], io["limes"]).then_inc(par_in, 16)
            sp.dma_start(bias[:], io["bias"]).then_inc(par_in, 16)
            sp.dma_start(bias8[RANK:, :], io["bias8"].rearrange("(p a) -> p a", a=1)).then_inc(par_in, 16)
            sp.wait_ge(pick_clear, 1)
            sp.dma_start(pick[0:RANK, 0:NE], io["limesT"]).then_inc(pick_in, 16)
            sp.dma_start(pick[RANK:, NE:], io["consts"][0:NE, C_ID:C_ID + NE]).then_inc(pick_in, 16)
            with sp.Fori(0, SEQ // HU - 1) as g:
                for i in range(HU):
                    sp.wait_ge(conv_done, g * HU + (i + 1))
                    sp.wait_ge(cst_in, 16)
                    load_toeplitz(sp, scratch, sh, toep[i], g * HU + (HU + i), i)

            def load_x2(c):
                sp.dma_start(xs[:, place(c), :, :], scratch["x2T"][c]).then_inc(xs_in[place(c)], 16)

            for i in range(2):
                sp.wait_ge(sh.x2_out[i], NQ * 16)
            load_x2(2)
            sp.wait_ge(y_lo_done, 2 + SEQ)
            load_x2(0)
            sp.wait_ge(w_lo_done, KB)
            load_x2(1)

            def store(c):
                early = c < SPLIT
                for o in range(KB):
                    sp.wait_ge(fin_done if early else base_done, c * KB + (KB + o + 1))
                    src = partial(c, o) if early else xs[:, place(c), o, :]
                    sp.dma_start(out[o * P:(o + 1) * P, c * CH:(c + 1) * CH], src)\
                      .then_inc(out_done[0 if early else place(c)], 16)

            for c in (SPLIT, SPLIT + 1):
                sp.wait_ge(base_done, KB + KB * (c - 1))
                load_x2(c)
            for c in range(SPLIT, NCH):
                store(c)
                if c - SPLIT < SPLIT:
                    store(c - SPLIT)
                if c + 2 < NCH:
                    sp.wait_ge(out_done[place(c)], 16 * KB * ((c - SPLIT) // 2 + 1))
                    load_x2(c + 2)
            sp.wait_ge(out_done[0], 16 * KB * SPLIT)
            sp.wait_ge(out_done[1], 16 * KB * 3)
            sp.wait_ge(out_done[2], 16 * KB * 2)

        @block.gpsimd
        def _(pool):
            pool.memset(wza_hi[:].bitcast(F32), 0.0).then_inc(wza_clear, 1)
            pool.memset(wza_lo[:].bitcast(F32), 0.0).then_inc(wza_clear, 1)
            pool.memset(pick[:], 0.0).then_inc(pick_clear, 1)
            for i in range(2):
                pool.memset(y_tmp[i][:, 0, 0:1], 0.0).then_inc(y_lo_done, 1)
            for i in range(2):
                pool.wait_ge(sh.x2_out[i], NQ * 16)
            with pool.Fori(0, SEQ // HU) as g:
                for i in range(HU):
                    pool.wait_ge(y_hi_done, g * HU + (i + 1))
                    pool.tensor_tensor(at_position(y_lo, KB, g * HU + i), by_chunk(y_tmp[i % 2]),
                                       at_position(y_hi, KB, g * HU + i).bitcast(F32), ALU.subtract)\
                        .then_inc(y_lo_done, 1)
            pool.wait_ge(peak_local, 1)
            pool.partition_all_reduce(big[:, 1, :], big[:, 0, :], P, bass.bass_isa.ReduceOp.max)\
                .then_inc(peak_all, 1)

        @block.tensor
        def _(t_):
            t_.wait_ge(x2_in, (NCH - 2) * 16)
            t_.wait_ge(sh.acc_done, KB + NQ * UPQ * KB)
            with t_.Fori(0, SEQ // HU) as g:
                for i in range(HU):
                    t_.wait_ge(toep_in[i], g * 16 + 16)
                    t_.wait_ge(y_done, g * HU + (i + 1))
                    for d in range(KB):
                        mm = t_.matmul(by_chunk(bank[i][:, d * P:].rearrange("p (o b) -> p o b", b=P)),
                                       toep[i][:, d * P:(d + 1) * P],
                                       at_position(x2, KB - d, g * HU + i),
                                       start=d == 0, stop=d == KB - 1)
                    mm.then_inc(conv_done, 1)

            def product(out_, left, c, last=True, y_lo_ready=None):
                for k in range(KB):
                    l_hi, l_lo = left(k)
                    t_.matmul(out_, l_hi, chunk(y_hi, c, k), start=k == 0, stop=False)
                    t_.matmul(out_, l_lo, chunk(y_hi, c, k), start=False, stop=False)
                if y_lo_ready:
                    t_.wait_ge(y_lo_done, y_lo_ready)
                for k in range(KB):
                    mm = t_.matmul(out_, left(k)[0], chunk(y_lo, c, k), start=False, stop=last and k == KB - 1)
                return mm

            t_.wait_ge(y_hi_done, SEQ)
            t_.wait_ge(wza_lo_done, 1)

            def low_rank(c, first):
                for i in range(2):
                    if not first:
                        t_.wait_ge(zh_done, c * 4 + (2 * i - 2))
                    product(bank[4 + i][:], lambda k: (wza_hi[:, k, :], wza_lo[:, k, :]), c * 2 + i,
                            y_lo_ready=2 + SEQ if first and i == 0 else None).then_inc(zh_mm, 1)

            low_rank(0, True)
            with t_.Fori(1, NCH // 2) as c:
                low_rank(c, False)

            def base_block(c, o, whole):
                cols = slice(o * P, (o + 1) * P)
                t_.wait_ge(base_done, c * KB + (o + 1))
                mm = product(bank[o][:], lambda k: (w_hi[:, k, cols], w_lo[:, k, cols]), c, not whole)
                if whole:
                    mm = t_.matmul(bank[o][:], b_split[:, cols], z_split[:, bass.ds(c * CH, CH)],
                                   start=False, stop=True)
                mm.then_inc(base_mm, 1)

            def base(c, whole):
                for o in range(KB):
                    base_block(c, o, whole)

            t_.wait_ge(pick_in, 32)
            for i in range(NT):
                if i % 2 == 0:
                    t_.wait_ge(zh_done, i + 2)
                mm = t_.matmul(bank[6][:, i * 2 * NE:(i + 1) * 2 * NE],
                               zh[0:RANK + NE, 2 * P * i:2 * P * (i + 1)].rearrange("p (a s) -> p a s", s=2)[:, :, 1],
                               pick[:], start=True, stop=True)
            mm.then_inc(gate_mm, 1)
            t_.wait_ge(w_lo_done, KB)
            base(0, False)

            def turn_gates(i):
                if i >= 2:
                    t_.wait_ge(w_copied, i - 1)
                for j in range(4):
                    mm = t_.transpose(bank[6 + i % 2][0:NE, j * P:(j + 1) * P], g0[:, 4 * i + j, :],
                                      cst[:, C_ID:C_ID + P])
                mm.then_inc(w_turned, 1)

            def mixture(i):
                t_.wait_ge(w_copied, i + 1)
                if i >= 2:
                    t_.wait_ge(mix_done, i - 1)
                t_.matmul(bank[4 + i % 2][0:RANK, :], limes[:], wgt[i], start=True, stop=True).then_inc(mix_mm, 1)

            base_block(1, 0, False)
            t_.wait_ge(w_ready, 1)
            turn_gates(0)
            turn_gates(1)
            base_block(1, 1, False)
            turn_gates(2)
            turn_gates(3)
            mixture(0)
            mixture(1)
            base_block(1, 2, False)
            mixture(2)
            mixture(3)
            base_block(1, 3, False)
            base(2, False)
            t_.wait_ge(b_done, 1)
            t_.wait_ge(z_dup_done, 4)
            t_.wait_ge(z_lo_done, 4)
            with t_.Fori(0, SPLIT) as c:
                base(c + SPLIT, True)
                for o in range(KB):
                    t_.wait_ge(fin_done, c * KB + (o + 1))
                    t_.matmul(bank[4 + o][:], b_split[:, o * P:(o + 1) * P], z_split[:, bass.ds(c * CH, CH)],
                              start=True, stop=True).then_inc(delta_mm, 1)
            with t_.Fori(2 * SPLIT, NCH) as c:
                base(c, True)

        @block.scalar
        def _(act):
            act.wait_ge(wza_in, 16)
            act.wait_ge(wza_clear, 2)
            act.activation(wza_hi[:, :, 0:RANK + NE], wza[:], ACT.Copy).then_inc(wza_hi_done, 1)
            with act.Fori(0, SEQ // HU) as g:
                for i in range(HU):
                    act.wait_ge(y_done, g * HU + (HU + i + 1))
                    act.activation(at_position(y_hi, KB, g * HU + i), by_chunk(y_tmp[i % 2]), ACT.Copy)\
                       .then_inc(y_hi_done, 1)
            act.wait_ge(wT_in, 16)
            act.wait_ge(par_in, 4 * 16)
            for k in range(KB):
                act.activation(w_hi[:, k, :], wT[:, k, :], ACT.Copy).then_inc(w_hi_done, 1)
            with act.Fori(0, NCH // 2) as c:
                for i in range(2):
                    act.wait_ge(zh_mm, c * 2 + (i + 1))
                    cols = bass.ds(c * (2 * CH) + i * CH, CH)
                    act.activation(zh[0:RANK, cols], bank[4 + i][0:RANK, :], ACT.Copy).then_inc(zh_done, 1)
                    act.activation(zh[RANK:RANK + NE, cols], bank[4 + i][RANK:RANK + NE, :], ACT.Identity,
                                   bias=bias8[RANK:, :]).then_inc(zh_done, 1)
            act.wait_ge(g_exp_in, 1)
            act.activation(g1[:], g0[:], ACT.Exp).then_inc(g_exp, 1)
            act.wait_ge(g_exp_in, 2)
            act.activation(g2[:], g1[:], ACT.Exp, scale=-2.0).then_inc(g_exp, 1)
            act.wait_ge(base_mm, 2 * KB)
            for i in range(4):
                cols = slice(i * 1024, (i + 1) * 1024)
                act.wait_ge(mix_done, i + 1)
                act.activation(z_split[0:RANK, cols], zh[0:RANK, cols], ACT.Copy).then_inc(z_hi_done, 1)
                act.activation(z_split[RANK:2 * RANK, cols], zh[0:RANK, cols], ACT.Copy).then_inc(z_dup_done, 1)

        @block.vector
        def _(v):
            done = [0]

            def then(ins):
                done[0] += 1
                ins.then_inc(chain, 1)
                v.wait_ge(chain, done[0])

            def per_token(ap):
                return ap.unsqueeze(2).to_broadcast([P, NT, NE])

            for o in range(KB):
                v.memset(big[:, o, 0:1], 0.0).then_inc(base_done, 1)
                v.memset(big[:, o, 1:2], 0.0).then_inc(fin_done, 1)
            v.wait_ge(len_in, 16)
            v.wait_ge(cst_in, 16)
            then(v.tensor_copy(lens[:], lens_i[:]))
            for o in range(KB):
                v.tensor_scalar(keep[:, o, :], lens[:], cst[:, C_PIDX + o:C_PIDX + o + 1], None, ALU.is_gt)\
                 .then_inc(y_done, 1)
            v.wait_ge(y_done, HU)
            v.wait_ge(wza_hi_done, 1)
            v.tensor_tensor(wza_lo[:, :, 0:RANK + NE], wza[:], wza_hi[:, :, 0:RANK + NE].bitcast(F32), ALU.subtract)\
             .then_inc(wza_lo_done, 1)
            with v.Fori(0, SEQ // HU) as g:
                for i in range(HU):
                    v.wait_ge(conv_done, g * HU + (i + 1))
                    v.wait_ge(y_lo_done, g * HU + (i + 1))
                    v.tensor_tensor(y_tmp[i % 2], bank[i][:].rearrange("p (o b) -> p o b", b=P), keep[:], ALU.mult)\
                     .then_inc(y_done, 1)
            for k in range(KB):
                v.wait_ge(w_hi_done, k + 1)
                v.tensor_tensor(w_lo[:, k, :], wT[:, k, :], w_hi[:, k, :].bitcast(F32), ALU.subtract)\
                 .then_inc(w_lo_done, 1)
            v.wait_ge(par_in, 4 * 16)
            for i in (0, 2):
                then(v.tensor_copy(b_split[i * RANK:(i + 1) * RANK, :], bmat[:]))
            v.tensor_tensor(b_split[RANK:2 * RANK, :], bmat[:], b_split[0:RANK, :].bitcast(F32), ALU.subtract)\
             .then_inc(b_done, 1)
            v.wait_ge(gate_mm, 1)
            then(v.tensor_copy(gate[:].rearrange("p t e -> p (t e)"), bank[6][:, 0:NT * 2 * NE]))
            v.tensor_reduce(big[:, 0, :], gate[:].rearrange("p t (s e) -> p s t e", s=2), AX.XY, ALU.max,
                            apply_absolute_value=True).then_inc(peak_local, 1)
            v.wait_ge(peak_all, 1)
            then(v.tensor_scalar(big[:, 2, :], big[:, 1, :], 1e-6, None, ALU.max))
            then(v.reciprocal(big[:, 3, :], big[:, 2, :]))
            then(v.tensor_scalar(big[:, 3, :], big[:, 3, :], 0.5, None, ALU.mult))
            then(v.tensor_scalar(g0[:], gate[:, :, 0:NE], big[:, 3, 0:1], None, ALU.mult))
            then(v.tensor_scalar(g1[:], gate[:, :, NE:], big[:, 3, 1:2], None, ALU.mult))
            then(v.tensor_tensor(g0[:], g0[:], g1[:], ALU.add))
            then(v.tensor_reduce(row[:, 0, :], g0[:], AX.X, ALU.max))
            v.tensor_tensor(g0[:], g0[:], per_token(row[:, 0, :]), ALU.subtract).then_inc(g_exp_in, 1)
            v.wait_ge(g_exp, 1)
            then(v.tensor_reduce(row[:, 0, :], g1[:], AX.X, ALU.add))
            then(v.reciprocal(row[:, 1, :], row[:, 0, :]))
            then(v.tensor_tensor(g0[:], g1[:], per_token(row[:, 1, :]), ALU.mult))
            for i in range(NT):
                ins = v.max(top[:, i, :], g0[:, i, :])
            then(ins)
            v.tensor_tensor(g1[:], g0[:], top[:, :, 1:2].to_broadcast([P, NT, NE]), ALU.subtract).then_inc(g_exp_in, 1)
            v.wait_ge(g_exp, 2)
            then(v.tensor_scalar(g2[:], g2[:], 1.0, None, ALU.add))
            then(v.reciprocal(g2[:], g2[:]))
            then(v.tensor_tensor(g0[:], g0[:], g2[:], ALU.mult))
            then(v.tensor_reduce(row[:, 0, :], g0[:], AX.X, ALU.add))
            then(v.tensor_scalar(row[:, 0, :], row[:, 0, :], 1e-9, None, ALU.add))
            then(v.reciprocal(row[:, 1, :], row[:, 0, :]))
            v.tensor_tensor(g0[:], g0[:], per_token(row[:, 1, :]), ALU.mult).then_inc(w_ready, 1)

            def base(c, blocks=range(KB)):
                v.wait_ge(xs_in[place(c)], 16)
                for o in blocks:
                    v.wait_ge(base_mm, c * KB + (o + 1))
                    v.scalar_tensor_tensor(partial(c, o), bank[o][:], bias[:, o:o + 1], xs[:, place(c), o, :],
                                           ALU.add, ALU.add).then_inc(base_done, 1)

            def whole(c):
                v.wait_ge(xs_in[place(c)], 16 * ((c - 1) // 2 + 1))
                for o in range(KB):
                    v.wait_ge(base_mm, c * KB + (o + 1))
                    x = xs[:, place(c), o, :]
                    v.scalar_tensor_tensor(x, bank[o][:], bias[:, o:o + 1], x, ALU.add, ALU.add).then_inc(base_done, 1)

            def last_sum(c):
                for o in range(KB):
                    v.wait_ge(delta_mm, c * KB + (o + 1))
                    x = partial(c, o)
                    v.tensor_tensor(x, bank[4 + o][:], x, ALU.add).then_inc(fin_done, 1)

            def gates_out(i):
                v.wait_ge(w_turned, i + 1)
                v.tensor_copy(wgt[i], bank[6 + i % 2][0:NE, :]).then_inc(w_copied, 1)

            def scale_z(i):
                v.wait_ge(mix_mm, i + 1)
                z = zh[0:RANK, i * 1024:(i + 1) * 1024].rearrange("p (a s) -> p a s", s=2)
                v.scalar_tensor_tensor(z, z, 0.5, bank[4 + i % 2][0:RANK, :].unsqueeze(2).to_broadcast([RANK, 512, 2]),
                                       ALU.mult, ALU.mult).then_inc(mix_done, 1)

            base(0)
            base(1, [0])
            gates_out(0)
            gates_out(1)
            base(1, [1])
            gates_out(2)
            gates_out(3)
            scale_z(0)
            scale_z(1)
            base(1, [2])
            scale_z(2)
            scale_z(3)
            base(1, [3])
            for i in range(4):
                cols = slice(i * 1024, (i + 1) * 1024)
                v.wait_ge(z_hi_done, i + 1)
                v.tensor_tensor(z_split[2 * RANK:, cols], zh[0:RANK, cols], z_split[0:RANK, cols].bitcast(F32),
                                ALU.subtract).then_inc(z_lo_done, 1)
            base(2)
            for c in range(SPLIT, NCH):
                whole(c)
                if c - SPLIT < SPLIT:
                    last_sum(c - SPLIT)


def program(nc, io, out):
    scratch = {
        "wg": nc.dram_tensor("wg_scratch", [BATCH, SEQ * SEQ], F32, kind="Internal").ap(),
        "wkv": nc.dram_tensor("wkv_scratch", [KB, P, KVH, 2 * HD], F32, kind="Internal").ap(),
        "kpad": nc.dram_tensor("kpad_scratch", [SEQ, KPAD], F32, kind="Internal").ap(),
        "x2T": nc.dram_tensor("x2T_scratch", [NCH, P, KB, CH], F32, kind="Internal").ap(),
    }
    with ExitStack() as ctx:
        sh = shared(nc, ctx)
        weights_and_ssm(nc, io, scratch, sh)
        attention(nc, io, scratch, sh)
        ssm_and_ffn(nc, io, scratch, sh, out)


def layouts(x, itok_B_0_15, itok_B_78_3631, L0_cond_weights, L0_attn_Wq, L0_attn_Wkr, L0_attn_Wdk, L0_attn_Wupk,
            L0_attn_Wupv, L0_attn_Wo, L0_cond2_log_dt, L0_cond2_C, L0_cond2_log_A_real, L0_cond2_A_imag, L0_cond2_D,
            L0_ffn_W, L0_ffn_b, L0_ffn_A, L0_ffn_Bmat, L0_ffn_LiMEs):
    def rev(a, axis):
        a = np.moveaxis(a, axis, 0)
        a = a.reshape(KB, P, *a.shape[1:])[:, ::-1].reshape(a.shape)
        return np.moveaxis(a, 0, axis)

    tok = x.reshape(TOK, DM)
    consts, lags = constants()
    return {
        "consts": consts, "lags": lags,
        "x_tok": tok, "xT": rev(tok.T, 0), "cond": itok_B_0_15, "length": itok_B_78_3631,
        "w_cond": L0_cond_weights.reshape(NST, SEQ * SEQ),
        "wqT": L0_attn_Wq.T, "wkrT": L0_attn_Wkr.T, "wdk": L0_attn_Wdk, "wupkT": L0_attn_Wupk.T,
        "wupvT": L0_attn_Wupv.T, "woT": rev(L0_attn_Wo.T, 1),
        "log_dt": L0_cond2_log_dt, "C_re": L0_cond2_C[..., 0].T, "C_im": L0_cond2_C[..., 1].T,
        "log_A_real": L0_cond2_log_A_real.T, "A_imag": L0_cond2_A_imag.T, "D": L0_cond2_D,
        "wT": rev(L0_ffn_W.T, 1), "wza": np.concatenate([L0_ffn_A, L0_ffn_W[:NE].T], 1),
        "bias": rev(L0_ffn_b, 0).reshape(KB, P).T, "bias8": L0_ffn_b[:NE], "bmat": rev(L0_ffn_Bmat, 1),
        "limes": L0_ffn_LiMEs, "limesT": L0_ffn_LiMEs.T,
    }


def kernel(**inputs):
    import concourse.bacc as _bacc
    from concourse.bass_utils import run_bass_kernel_spmd as _run

    nc = _bacc.Bacc("TRN2", target_bir_lowering=False, num_devices=1)
    arrays, io = {}, {}
    for name, a in layouts(**{k: np.asarray(v) for k, v in inputs.items()}).items():
        a = np.ascontiguousarray(a)
        arrays[f"in_{name}"] = a
        io[name] = nc.dram_tensor(f"in_{name}", a.shape, mybir.dt.from_np(a.dtype), kind="ExternalInput").ap()
    out = nc.dram_tensor("out", [DM, TOK], F32, kind="ExternalOutput").ap()
    program(nc, io, out)
    r = _run(nc, [arrays], core_ids=[0])
    o = np.asarray(r.results[0]["out"]).reshape(KB, P, TOK)[:, ::-1].reshape(DM, TOK)
    return np.ascontiguousarray(o.T).reshape(BATCH, SEQ, DM)
```
